# Optimizing a Trainium2 kernel written in Bass

```python
import numpy as np
import jax
import jax.numpy as jnp

def _softmax(x, axis=-1):
    return jax.nn.softmax(x, axis=axis)

def _gelu(x):
    return jax.nn.gelu(x, approximate=True)

def _silu(x):
    return jax.nn.silu(x)

def _sigmoid(x):
    return jax.nn.sigmoid(x)

def _layernorm(x, axis=-1, eps=1e-05):
    m = jnp.mean(x, axis=axis, keepdims=True)
    v = jnp.var(x, axis=axis, keepdims=True)
    return (x - m) / jnp.sqrt(v + eps)

def _scatter_add(tgt, idx, src, axis=0):
    return tgt.at[idx].add(src)

def _segment_sum(src, seg, n):
    return jax.ops.segment_sum(src, seg, n)
kernel_name = 'mk_perceiver_d2_seqx_r8_6a10d6'

def setup_inputs(seed: int=0):
    np.random.seed(seed)
    _w = jnp.asarray

    def _rec_inputs():
        import jax
        import jax.numpy as jnp
        _rk = jax.random.key(seed)
        x = -0.0003929 + 0.9999 * jax.random.normal(jax.random.fold_in(_rk, 1), (32, 64, 128), jnp.float32)
        _lenS = 64 - jax.random.randint(jax.random.fold_in(_rk, 7), (32,), 0, max(1, 64 // 4) + 1, jnp.int32)
        _lenS2 = 1601 - jax.random.randint(jax.random.fold_in(_rk, 8), (32,), 0, max(1, 1601 // 4) + 1, jnp.int32)
        _ctx_768P = jax.random.normal(jax.random.fold_in(_rk, 11), (32, 16, 96), jnp.float32)
        _ctx_768c = jax.random.dirichlet(jax.random.fold_in(_rk, 511), 0.3 * jnp.ones((16,), jnp.float32), (32, 1601))
        _ctx_768t = jnp.einsum('bsk,bkd->bsd', _ctx_768c, _ctx_768P)
        _ctx_768t = _ctx_768t * jax.lax.rsqrt(jnp.mean(jnp.square(_ctx_768t)) + 1e-12) * 0.953939
        ctx_768 = 0.00095986 + 0.999812 * (_ctx_768t + 0.3 * jax.random.normal(jax.random.fold_in(_rk, 611), (32, 1601, 96), jnp.float32))
        _validS = jnp.arange(64)[None, :] < _lenS[:, None]
        _validS2 = jnp.arange(1601)[None, :] < _lenS2[:, None]
        _causal = jnp.tril(jnp.ones((64, 64), dtype=bool))
        mask_BxS2_bf1 = jnp.ones((32, 1601), dtype=bool)
        return (x, ctx_768, mask_BxS2_bf1)
    x, ctx_768, mask_BxS2_bf1 = _rec_inputs()

    def _L0_xattn_setup():
        import jax, jax.numpy as jnp
        import numpy as np
        DIM = 128
        CTX_DIM = 96
        HEADS = 16
        key = jax.random.key(seed)
        ks = jax.random.split(key, 7)
        B, N, M = (4, 512, 32)
        x = jax.random.normal(ks[0], (B, N, DIM), dtype=jnp.float32)
        context = jax.random.normal(ks[1], (B, M, CTX_DIM), dtype=jnp.float32)
        context_mask = jnp.ones((B, M), dtype=bool)
        s_d = 1.0 / np.sqrt(DIM)
        s_c = 1.0 / np.sqrt(CTX_DIM)
        Wq = jax.random.normal(ks[2], (DIM, DIM), dtype=jnp.float32) * s_d
        Wk = jax.random.normal(ks[3], (CTX_DIM, DIM), dtype=jnp.float32) * s_c
        Wv = jax.random.normal(ks[4], (CTX_DIM, DIM), dtype=jnp.float32) * s_c
        Wo = jax.random.normal(ks[5], (DIM, DIM), dtype=jnp.float32) * s_d
        return {'x': x, 'context': context, 'context_mask': context_mask, 'Wq': Wq, 'Wk': Wk, 'Wv': Wv, 'Wo': Wo}
    _L0_xattn_all = _L0_xattn_setup()
    _L0_xattn_in = {k: v for k, v in _L0_xattn_all.items() if k in ('Wq', 'Wk', 'Wv', 'Wo')}
    del _L0_xattn_all

    def _L0_attn_setup():
        import jax, jax.numpy as jnp
        import numpy as np
        EMBED_DIM = 128
        NUM_HEADS = 16
        HEAD_DIM = EMBED_DIM // NUM_HEADS
        ROPE_BASE = 10000.0

        def _rotary_emb(seq_len, dtype=jnp.float32):
            half = HEAD_DIM // 2
            inv_freq = 1.0 / ROPE_BASE ** (jnp.arange(half, dtype=dtype) / half)
            pos = jnp.arange(seq_len, dtype=dtype)
            sinusoid = pos[:, None] * inv_freq[None, :]
            sin = jnp.sin(sinusoid)
            cos = jnp.cos(sinusoid)
            sin = jnp.stack((sin, sin), axis=-1).reshape(seq_len, HEAD_DIM)
            cos = jnp.stack((cos, cos), axis=-1).reshape(seq_len, HEAD_DIM)
            return (sin, cos)

        def _rotate_half(x):
            x1 = x[..., ::2]
            x2 = x[..., 1::2]
            return jnp.stack((-x2, x1), axis=-1).reshape(x.shape)

        def _apply_rope(x, sin, cos):
            return x * cos[None, None] + _rotate_half(x) * sin[None, None]
        key = jax.random.key(seed)
        ks = jax.random.split(key, 9)
        B, S, E = (2, 256, EMBED_DIM)
        scale = 1.0 / np.sqrt(E)
        x = jax.random.normal(ks[0], (B, S, E), dtype=jnp.float32)
        Wq = jax.random.normal(ks[1], (E, E), dtype=jnp.float32) * scale
        bq = jnp.zeros((E,), dtype=jnp.float32)
        Wk = jax.random.normal(ks[2], (E, E), dtype=jnp.float32) * scale
        bk = jnp.zeros((E,), dtype=jnp.float32)
        Wv = jax.random.normal(ks[3], (E, E), dtype=jnp.float32) * scale
        bv = jnp.zeros((E,), dtype=jnp.float32)
        Wo = jax.random.normal(ks[4], (E, E), dtype=jnp.float32) * scale
        bo = jnp.zeros((E,), dtype=jnp.float32)
        return {'x': x, 'Wq': Wq, 'bq': bq, 'Wk': Wk, 'bk': bk, 'Wv': Wv, 'bv': bv, 'Wo': Wo, 'bo': bo}
    _L0_attn_all = _L0_attn_setup()
    _L0_attn_in = {k: v for k, v in _L0_attn_all.items() if k in ('Wq', 'bq', 'Wk', 'bk', 'Wv', 'bv', 'Wo', 'bo')}
    del _L0_attn_all

    def _L0_ffn_setup():
        import jax, jax.numpy as jnp
        import numpy as np
        HIDDEN = 128
        INTER = 512
        N_EXPERTS = 8
        TOP_K = 2
        INIT_STD = 0.02
        key = jax.random.key(seed)
        ks = jax.random.split(key, 6)
        x = jax.random.normal(ks[0], (2, 128, HIDDEN), dtype=jnp.float32)
        Wg = jax.random.normal(ks[1], (N_EXPERTS, HIDDEN), dtype=jnp.float32) * INIT_STD
        W1 = jax.random.normal(ks[2], (N_EXPERTS, HIDDEN, INTER), dtype=jnp.float32) * INIT_STD
        b1 = jnp.zeros((N_EXPERTS, INTER), dtype=jnp.float32)
        W2 = jax.random.normal(ks[3], (N_EXPERTS, INTER, HIDDEN), dtype=jnp.float32) * INIT_STD
        b2 = jnp.zeros((N_EXPERTS, HIDDEN), dtype=jnp.float32)
        return {'x': x, 'Wg': Wg, 'W1': W1, 'b1': b1, 'W2': W2, 'b2': b2}
    _L0_ffn_all = _L0_ffn_setup()
    _L0_ffn_in = {k: v for k, v in _L0_ffn_all.items() if k in ('Wg', 'W1', 'b1', 'W2', 'b2')}
    del _L0_ffn_all

    def _L1_xattn_setup():
        import jax, jax.numpy as jnp
        import numpy as np
        EPS = 1e-05
        key = jax.random.key(seed)
        ks = jax.random.split(key, 6)
        B, Nq, Nk, Dq, Dk = (16, 256, 256, 128, 96)
        s = lambda d: 1.0 / np.sqrt(d)
        return {'q': jax.random.normal(ks[0], (B, Nq, Dq), dtype=jnp.float32), 'k': jax.random.normal(ks[1], (B, Nk, Dk), dtype=jnp.float32), 'Wq': jax.random.normal(ks[2], (Dq, Dq), dtype=jnp.float32) * s(Dq), 'Wk': jax.random.normal(ks[3], (Dq, Dk), dtype=jnp.float32) * s(Dk), 'Wv': jax.random.normal(ks[4], (Dq, Dk), dtype=jnp.float32) * s(Dk), 'Wo': jax.random.normal(ks[5], (Dq, Dq), dtype=jnp.float32) * s(Dq)}
    _L1_xattn_all = _L1_xattn_setup()
    _L1_xattn_in = {k: v for k, v in _L1_xattn_all.items() if k in ('Wq', 'Wk', 'Wv', 'Wo')}
    del _L1_xattn_all

    def _L1_attn_setup():
        import jax, jax.numpy as jnp
        import numpy as np
        D_MODEL = 128
        HIDDEN = 256
        D_STATE = 16
        KERN = 3
        BATCH = 2
        SEQ = 256

        def _layernorm(x, g, b, eps=1e-05):
            m = jnp.mean(x, axis=-1, keepdims=True)
            v = jnp.var(x, axis=-1, keepdims=True)
            return (x - m) * jax.lax.rsqrt(v + eps) * g + b
        key = jax.random.key(seed)
        ks = jax.random.split(key, 10)
        w_scale = 0.02
        return {'x': jax.random.normal(ks[0], (BATCH, SEQ, D_MODEL), jnp.float32), 'W_x': jax.random.normal(ks[1], (HIDDEN, D_MODEL), jnp.float32) * w_scale, 'b_x': jnp.zeros((HIDDEN,), jnp.float32), 'W_g': jax.random.normal(ks[2], (HIDDEN, D_MODEL), jnp.float32) * w_scale, 'b_g': jnp.zeros((HIDDEN,), jnp.float32), 'conv_w': jax.random.normal(ks[3], (HIDDEN, 1, KERN), jnp.float32) * 0.3, 'conv_b': jnp.zeros((HIDDEN,), jnp.float32), 'A_raw': jax.random.normal(ks[4], (HIDDEN, D_STATE), jnp.float32), 'B_ssm': jax.random.normal(ks[5], (HIDDEN, D_STATE), jnp.float32), 'C_ssm': jax.random.normal(ks[6], (HIDDEN, D_STATE), jnp.float32), 'W_dt': jax.random.normal(ks[7], (HIDDEN, D_MODEL), jnp.float32) * w_scale, 'b_dt': jnp.zeros((HIDDEN,), jnp.float32), 'W_out': jax.random.normal(ks[8], (D_MODEL, HIDDEN), jnp.float32) * w_scale, 'b_out': jnp.zeros((D_MODEL,), jnp.float32), 'ln_g': jnp.ones((D_MODEL,), jnp.float32), 'ln_b': jnp.zeros((D_MODEL,), jnp.float32)}
    _L1_attn_all = _L1_attn_setup()
    _L1_attn_in = {k: v for k, v in _L1_attn_all.items() if k in ('W_x', 'b_x', 'W_g', 'b_g', 'conv_w', 'conv_b', 'A_raw', 'B_ssm', 'C_ssm', 'W_dt', 'b_dt', 'W_out', 'b_out', 'ln_g', 'ln_b')}
    del _L1_attn_all

    def _L1_ffn_setup():
        import jax, jax.numpy as jnp
        import numpy as np
        E = 8
        K = 2
        key = jax.random.key(seed)
        ks = jax.random.split(key, 8)
        B, T, d = (4, 256, 128)
        h = 4 * d // E
        s = 0.02
        X = jax.random.normal(ks[0], (B, T, d), jnp.float32)
        routing_W = jax.random.normal(ks[1], (E, d), jnp.float32) * s
        expert_bias = jnp.zeros((E,), jnp.float32)
        sW1 = jax.random.normal(ks[2], (d, h), jnp.float32) * s
        sb1 = jnp.zeros((h,), jnp.float32)
        sW2 = jax.random.normal(ks[3], (h, d), jnp.float32) * s
        sb2 = jnp.zeros((d,), jnp.float32)
        rW1 = jax.random.normal(ks[4], (E, d, h), jnp.float32) * s
        rb1 = jnp.zeros((E, h), jnp.float32)
        rW2 = jax.random.normal(ks[5], (E, h, d), jnp.float32) * s
        rb2 = jnp.zeros((E, d), jnp.float32)
        return dict(X=X, routing_W=routing_W, expert_bias=expert_bias, sW1=sW1, sb1=sb1, sW2=sW2, sb2=sb2, rW1=rW1, rb1=rb1, rW2=rW2, rb2=rb2)
    _L1_ffn_all = _L1_ffn_setup()
    _L1_ffn_in = {k: v for k, v in _L1_ffn_all.items() if k in ('routing_W', 'expert_bias', 'sW1', 'sb1', 'sW2', 'sb2', 'rW1', 'rb1', 'rW2', 'rb2')}
    del _L1_ffn_all
    return {'x': x, 'ctx_768': ctx_768, 'mask_BxS2_bf1': mask_BxS2_bf1, 'L0_xattn_Wq': _L0_xattn_in['Wq'], 'L0_xattn_Wk': _L0_xattn_in['Wk'], 'L0_xattn_Wv': _L0_xattn_in['Wv'], 'L0_xattn_Wo': _L0_xattn_in['Wo'], 'L0_attn_Wq': _L0_attn_in['Wq'], 'L0_attn_bq': _L0_attn_in['bq'], 'L0_attn_Wk': _L0_attn_in['Wk'], 'L0_attn_bk': _L0_attn_in['bk'], 'L0_attn_Wv': _L0_attn_in['Wv'], 'L0_attn_bv': _L0_attn_in['bv'], 'L0_attn_Wo': _L0_attn_in['Wo'], 'L0_attn_bo': _L0_attn_in['bo'], 'L0_ffn_Wg': _L0_ffn_in['Wg'], 'L0_ffn_W1': _L0_ffn_in['W1'], 'L0_ffn_b1': _L0_ffn_in['b1'], 'L0_ffn_W2': _L0_ffn_in['W2'], 'L0_ffn_b2': _L0_ffn_in['b2'], 'L1_xattn_Wq': _L1_xattn_in['Wq'], 'L1_xattn_Wk': _L1_xattn_in['Wk'], 'L1_xattn_Wv': _L1_xattn_in['Wv'], 'L1_xattn_Wo': _L1_xattn_in['Wo'], 'L1_attn_W_x': _L1_attn_in['W_x'], 'L1_attn_b_x': _L1_attn_in['b_x'], 'L1_attn_W_g': _L1_attn_in['W_g'], 'L1_attn_b_g': _L1_attn_in['b_g'], 'L1_attn_conv_w': _L1_attn_in['conv_w'], 'L1_attn_conv_b': _L1_attn_in['conv_b'], 'L1_attn_A_raw': _L1_attn_in['A_raw'], 'L1_attn_B_ssm': _L1_attn_in['B_ssm'], 'L1_attn_C_ssm': _L1_attn_in['C_ssm'], 'L1_attn_W_dt': _L1_attn_in['W_dt'], 'L1_attn_b_dt': _L1_attn_in['b_dt'], 'L1_attn_W_out': _L1_attn_in['W_out'], 'L1_attn_b_out': _L1_attn_in['b_out'], 'L1_attn_ln_g': _L1_attn_in['ln_g'], 'L1_attn_ln_b': _L1_attn_in['ln_b'], 'L1_ffn_routing_W': _L1_ffn_in['routing_W'], 'L1_ffn_expert_bias': _L1_ffn_in['expert_bias'], 'L1_ffn_sW1': _L1_ffn_in['sW1'], 'L1_ffn_sb1': _L1_ffn_in['sb1'], 'L1_ffn_sW2': _L1_ffn_in['sW2'], 'L1_ffn_sb2': _L1_ffn_in['sb2'], 'L1_ffn_rW1': _L1_ffn_in['rW1'], 'L1_ffn_rb1': _L1_ffn_in['rb1'], 'L1_ffn_rW2': _L1_ffn_in['rW2'], 'L1_ffn_rb2': _L1_ffn_in['rb2']}

def reference(x, ctx_768, mask_BxS2_bf1, L0_xattn_Wq, L0_xattn_Wk, L0_xattn_Wv, L0_xattn_Wo, L0_attn_Wq, L0_attn_bq, L0_attn_Wk, L0_attn_bk, L0_attn_Wv, L0_attn_bv, L0_attn_Wo, L0_attn_bo, L0_ffn_Wg, L0_ffn_W1, L0_ffn_b1, L0_ffn_W2, L0_ffn_b2, L1_xattn_Wq, L1_xattn_Wk, L1_xattn_Wv, L1_xattn_Wo, L1_attn_W_x, L1_attn_b_x, L1_attn_W_g, L1_attn_b_g, L1_attn_conv_w, L1_attn_conv_b, L1_attn_A_raw, L1_attn_B_ssm, L1_attn_C_ssm, L1_attn_W_dt, L1_attn_b_dt, L1_attn_W_out, L1_attn_b_out, L1_attn_ln_g, L1_attn_ln_b, L1_ffn_routing_W, L1_ffn_expert_bias, L1_ffn_sW1, L1_ffn_sb1, L1_ffn_sW2, L1_ffn_sb2, L1_ffn_rW1, L1_ffn_rb1, L1_ffn_rW2, L1_ffn_rb2):
    import jax
    import jax.numpy as jnp

    def _L0_xattn_ref(x, context, context_mask, Wq, Wk, Wv, Wo):
        import jax, jax.numpy as jnp
        import numpy as np
        DIM = 128
        CTX_DIM = 96
        HEADS = 16
        B, N, _ = x.shape
        M = context.shape[1]
        hd = DIM // HEADS
        scale = hd ** (-0.5)
        q = (x @ Wq).reshape(B, N, HEADS, hd).transpose(0, 2, 1, 3)
        k = (context @ Wk).reshape(B, M, HEADS, hd).transpose(0, 2, 1, 3)
        v = (context @ Wv).reshape(B, M, HEADS, hd).transpose(0, 2, 1, 3)
        scores = jnp.einsum('bhid,bhjd->bhij', q, k) * scale
        max_neg = -jnp.finfo(scores.dtype).max
        scores = jnp.where(context_mask[:, None, None, :], scores, max_neg)
        attn = jax.nn.softmax(scores, axis=-1)
        out = jnp.einsum('bhij,bhjd->bhid', attn, v)
        out = out.transpose(0, 2, 1, 3).reshape(B, N, DIM)
        return out @ Wo

    def _L0_attn_ref(x, Wq, bq, Wk, bk, Wv, bv, Wo, bo):
        import jax, jax.numpy as jnp
        import numpy as np
        EMBED_DIM = 128
        NUM_HEADS = 16
        HEAD_DIM = EMBED_DIM // NUM_HEADS
        ROPE_BASE = 10000.0

        def _rotary_emb(seq_len, dtype=jnp.float32):
            half = HEAD_DIM // 2
            inv_freq = 1.0 / ROPE_BASE ** (jnp.arange(half, dtype=dtype) / half)
            pos = jnp.arange(seq_len, dtype=dtype)
            sinusoid = pos[:, None] * inv_freq[None, :]
            sin = jnp.sin(sinusoid)
            cos = jnp.cos(sinusoid)
            sin = jnp.stack((sin, sin), axis=-1).reshape(seq_len, HEAD_DIM)
            cos = jnp.stack((cos, cos), axis=-1).reshape(seq_len, HEAD_DIM)
            return (sin, cos)

        def _rotate_half(x):
            x1 = x[..., ::2]
            x2 = x[..., 1::2]
            return jnp.stack((-x2, x1), axis=-1).reshape(x.shape)

        def _apply_rope(x, sin, cos):
            return x * cos[None, None] + _rotate_half(x) * sin[None, None]
        B, S, E = x.shape
        H, D = (NUM_HEADS, HEAD_DIM)

        def proj(W, b):
            t = x @ W.T + b
            return t.reshape(B, S, H, D).transpose(0, 2, 1, 3)
        q = proj(Wq, bq)
        k = proj(Wk, bk)
        v = proj(Wv, bv)
        sin, cos = _rotary_emb(S, x.dtype)
        q = _apply_rope(q, sin, cos)
        k = _apply_rope(k, sin, cos)
        scores = jnp.einsum('bhqd,bhkd->bhqk', q, k) / jnp.sqrt(jnp.asarray(D, x.dtype))
        causal = jnp.tril(jnp.ones((S, S), dtype=bool))
        scores = jnp.where(causal[None, None], scores, -jnp.inf)
        weights = jax.nn.softmax(scores, axis=-1)
        out = jnp.einsum('bhqk,bhkd->bhqd', weights, v)
        out = out.transpose(0, 2, 1, 3).reshape(B, S, E)
        return out @ Wo.T + bo

    def _L0_ffn_ref(x, Wg, W1, b1, W2, b2):
        import jax, jax.numpy as jnp
        import numpy as np
        HIDDEN = 128
        INTER = 512
        N_EXPERTS = 8
        TOP_K = 2
        INIT_STD = 0.02
        orig_shape = x.shape
        xt = x.reshape(-1, HIDDEN)
        T = xt.shape[0]
        logits = xt @ Wg.T
        topk_logits, topk_idx = jax.lax.top_k(logits, TOP_K)
        w = jax.nn.softmax(topk_logits, axis=-1)
        rows = jnp.arange(T)[:, None]
        gates = jnp.zeros((T, N_EXPERTS), xt.dtype).at[rows, topk_idx].add(w)
        h = jnp.einsum('th,ehi->tei', xt, W1) + b1
        h = jax.nn.gelu(h, approximate=False)
        o = jnp.einsum('tei,eih->teh', h, W2) + b2
        y = jnp.einsum('te,teh->th', gates, o)
        return y.reshape(orig_shape)

    def _L1_xattn_ref(q, k, Wq, Wk, Wv, Wo):
        import jax, jax.numpy as jnp
        import numpy as np
        EPS = 1e-05
        query = q @ Wq.T
        key_p = k @ Wk.T
        value = k @ Wv.T
        sim = jnp.einsum('bqd,bkd->bqk', query, key_p)
        mean = jnp.mean(sim, axis=(1, 2), keepdims=True)
        var = jnp.var(sim, axis=(1, 2), keepdims=True)
        sim = (sim - mean) * jax.lax.rsqrt(var + EPS)
        attn = jax.nn.softmax(sim, axis=-1)
        out = jnp.einsum('bqk,bkd->bqd', attn, value)
        return out @ Wo.T

    def _L1_attn_ref(x, W_x, b_x, W_g, b_g, conv_w, conv_b, A_raw, B_ssm, C_ssm, W_dt, b_dt, W_out, b_out, ln_g, ln_b):
        import jax, jax.numpy as jnp
        import numpy as np
        D_MODEL = 128
        HIDDEN = 256
        D_STATE = 16
        KERN = 3
        BATCH = 2
        SEQ = 256

        def _layernorm(x, g, b, eps=1e-05):
            m = jnp.mean(x, axis=-1, keepdims=True)
            v = jnp.var(x, axis=-1, keepdims=True)
            return (x - m) * jax.lax.rsqrt(v + eps) * g + b
        u = jnp.einsum('bld,hd->blh', x, W_x) + b_x
        g = jax.nn.sigmoid(jnp.einsum('bld,hd->blh', x, W_g) + b_g)
        pad = conv_w.shape[-1] // 2
        h = jax.lax.conv_general_dilated(jnp.transpose(u, (0, 2, 1)), conv_w, window_strides=(1,), padding=[(pad, pad)], feature_group_count=conv_w.shape[0], dimension_numbers=('NCH', 'OIH', 'NCH')) + conv_b[None, :, None]
        h = jnp.transpose(h, (0, 2, 1))
        u = u * g + h * (1.0 - g)
        dt = jax.nn.softplus(jnp.einsum('bld,hd->blh', x, W_dt) + b_dt).mean(axis=(0, 1))
        dt = jnp.clip(dt, 0.001, 2.0)
        A = -jax.nn.softplus(A_raw)
        A_d = jnp.exp(A * dt[:, None])
        B_d = (A_d - 1.0) / (A + 1e-06) * B_ssm
        Bsz, L, H = u.shape
        S = A_d.shape[1]

        def step(carry, u_t):
            new = A_d[None] * carry + B_d[None] * u_t[:, :, None]
            y_t = jnp.einsum('bhs,hs->bh', new, C_ssm)
            return (new, y_t)
        init = jnp.zeros((Bsz, H, S), dtype=u.dtype)
        _, ys = jax.lax.scan(step, init, jnp.transpose(u, (1, 0, 2)))
        y = jnp.transpose(ys, (1, 0, 2))
        out = jnp.einsum('blh,dh->bld', y, W_out) + b_out
        return _layernorm(x + out, ln_g, ln_b)

    def _L1_ffn_ref(X, routing_W, expert_bias, sW1, sb1, sW2, sb2, rW1, rb1, rW2, rb2):
        import jax, jax.numpy as jnp
        import numpy as np
        E = 8
        K = 2
        B, T, d = X.shape
        shared = jax.nn.silu(X @ sW1 + sb1) @ sW2 + sb2
        logits = jnp.einsum('btd,ed->bte', X, routing_W) + expert_bias
        activation = jnp.sqrt(jax.nn.softplus(logits))
        top_vals, top_idx = jax.lax.top_k(activation, K)
        combine = jnp.sum(jax.nn.one_hot(top_idx, E, dtype=X.dtype) * top_vals[..., None], axis=-2)
        Xf = X.reshape(-1, d)
        cf = combine.reshape(-1, E)
        hdn = jax.nn.silu(jnp.einsum('nd,edh->enh', Xf, rW1) + rb1[:, None, :])
        y = jnp.einsum('enh,ehd->end', hdn, rW2) + rb2[:, None, :]
        routed = jnp.einsum('ne,end->nd', cf, y).reshape(B, T, d)
        return shared + routed
    x = x + _L0_xattn_ref(_layernorm(x, axis=-1), ctx_768, mask_BxS2_bf1, L0_xattn_Wq, L0_xattn_Wk, L0_xattn_Wv, L0_xattn_Wo)
    x = x + _L0_attn_ref(_layernorm(x, axis=-1), L0_attn_Wq, L0_attn_bq, L0_attn_Wk, L0_attn_bk, L0_attn_Wv, L0_attn_bv, L0_attn_Wo, L0_attn_bo)
    x = x + _L0_ffn_ref(_layernorm(x, axis=-1), L0_ffn_Wg, L0_ffn_W1, L0_ffn_b1, L0_ffn_W2, L0_ffn_b2)
    x = x + _L1_xattn_ref(_layernorm(x, axis=-1), ctx_768, L1_xattn_Wq, L1_xattn_Wk, L1_xattn_Wv, L1_xattn_Wo)
    x = x + _L1_attn_ref(_layernorm(x, axis=-1), L1_attn_W_x, L1_attn_b_x, L1_attn_W_g, L1_attn_b_g, L1_attn_conv_w, L1_attn_conv_b, L1_attn_A_raw, L1_attn_B_ssm, L1_attn_C_ssm, L1_attn_W_dt, L1_attn_b_dt, L1_attn_W_out, L1_attn_b_out, L1_attn_ln_g, L1_attn_ln_b)
    x = x + _L1_ffn_ref(_layernorm(x, axis=-1), L1_ffn_routing_W, L1_ffn_expert_bias, L1_ffn_sW1, L1_ffn_sb1, L1_ffn_sW2, L1_ffn_sb2, L1_ffn_rW1, L1_ffn_rb1, L1_ffn_rW2, L1_ffn_rb2)
    return x

_drawn_inputs = setup_inputs


def setup_inputs(seed=0):
    import zlib

    import numpy as np

    out = dict(_drawn_inputs(seed))
    spreads = {'L0_attn_bq': (0.0, 0.436),
     'L0_attn_bk': (0.0, 0.569),
     'L0_attn_bv': (0.0, 0.1),
     'L0_attn_bo': (0.0, 0.1),
     'L0_ffn_b1': (0.0, 0.594),
     'L0_ffn_b2': (0.0, 0.1),
     'L1_attn_b_x': (0.0, 0.1),
     'L1_attn_b_g': (0.0, 0.8),
     'L1_attn_conv_b': (0.0, 0.1),
     'L1_attn_b_dt': (0.0, 0.8),
     'L1_attn_b_out': (0.0, 0.1),
     'L1_attn_ln_g': (1.0, 0.2),
     'L1_attn_ln_b': (0.0, 0.1),
     'L1_ffn_expert_bias': (0.0, 0.1),
     'L1_ffn_sb1': (0.0, 0.8),
     'L1_ffn_sb2': (0.0, 0.1),
     'L1_ffn_rb1': (0.0, 0.8),
     'L1_ffn_rb2': (0.0, 0.1)}
    factors = {'L1_attn_W_g': 4.058,
     'L1_attn_W_dt': 8.0,
     'L1_ffn_sW1': 7.536,
     'L1_ffn_sW2': 6.65,
     'L1_ffn_rW1': 5.619,
     'L1_ffn_rW2': 5.027}
    for name, (base, spread) in spreads.items():
        noise = np.random.default_rng([zlib.crc32(name.encode()), seed]).standard_normal(out[name].shape)
        drawn = base * np.exp(spread * noise) if base else spread * noise
        out[name] = jnp.asarray(drawn.astype(out[name].dtype))
    for name, factor in factors.items():
        out[name] = (out[name] * factor).astype(out[name].dtype)
    return out
```

```python
from contextlib import ExitStack

import concourse.bass as bass
from concourse import mybir
import numpy as np

F32 = mybir.dt.float32
BF16 = mybir.dt.bfloat16
U8 = mybir.dt.uint8
ACT = mybir.ActivationFunctionType
ALU = mybir.AluOpType
AX = mybir.AxisListType

P = 128
B, S, D = 32, 64, 128
M, C = 1601, 96
H, HD = 16, 8
PAIRS = B // 2
T = B * S
TCH = T // 512
KT = (M + P - 1) // P
KROWS = [min(P, M - P * j) for j in range(KT)]
MC = (M + 511) // 512
CCOLS = [min(512, M - 512 * c) for c in range(MC)]
G = H // 2
MASKED = -3.0e38
EPS = 1e-5
K_PARTS = (0, 0, 0, 1, 1, 2)
Q_PARTS = (0, 1, 2, 0, 1, 0)
TERMS = len(K_PARTS)
GH = TERMS * 2 * HD
MROW = GH
SROWS = GH + 4


class Names(dict):
    def __getattr__(self, name):
        return self[name]

    def __setattr__(self, name, thing):
        self[name] = thing


WEIGHTS = (
    "x0_wq",
    "x0_wk",
    "x0_wv",
    "x0_wo",
    "a0_wqT",
    "a0_wqT_sw",
    "a0_wkT",
    "a0_wkT_sw",
    "a0_wvT",
    "a0_woT",
    "a0_bq",
    "a0_bq_sw",
    "a0_bk",
    "a0_bk_sw",
    "a0_bv",
    "a0_bo",
    "a0_cos",
    "a0_sin",
    "a0_causal",
    "a0_heads",
    "lower",
    "f0_wgT",
    "f0_b1",
    "f0_b2",
    "halves",
    "x1_wq",
    "x1_wk",
    "x1_wv",
    "x1_woT",
    "s1_wxT",
    "s1_wgT",
    "s1_wdtT",
    "s1_bx",
    "s1_bg",
    "s1_bdt",
    "s1_cw",
    "s1_cb",
    "s1_araw",
    "s1_b",
    "s1_c",
    "s1_k",
    "s1_woT",
    "s1_bout",
    "s1_g",
    "s1_lb",
    "f1_wrT",
    "f1_eb",
    "f1_rw1",
    "f1_sw1",
    "f1_b1",
    "f1_rw2",
    "f1_sw2",
    "f1_sb2",
    "f1_rb2",
)


def opened(nc, ctx):
    return Names(
        sb=lambda name, shape, dt=F32: ctx.enter_context(nc.sbuf_tensor(name, shape, dt)),
        ps=lambda name, shape, dt=F32: ctx.enter_context(nc.psum_tensor(name, shape, dt)),
        sem=lambda name: ctx.enter_context(nc.semaphore(name)),
        block=lambda: ctx.enter_context(nc.Block()),
    )


def hold(eng, sem):
    eng.sem_inc(sem)


def load_all(nc, w, s):
    with ExitStack() as ctx:
        o = opened(nc, ctx)
        loads = [
            (s.x[:, :, :], w["x"].rearrange("(t p) d -> p t d", p=P)),
        ] + [(s.w[name][tuple(slice(None) for _ in s.w[name].shape)], w[name]) for name in s.w]
        mask_u8 = o.sb("mask_u8", [B, M], U8)
        mask_bias = o.sb("mask_bias", [B, M], BF16)
        zero_f = o.sb("zero_f", [P, P])
        loaded, mask_loaded, mask_ready, mask_stored = o.sem("loaded"), o.sem("mask_loaded"), o.sem("mask_ready"), o.sem("mask_stored")
        zeroed, made = o.sem("zeroed"), o.sem("made")
        block = o.block()

        @block.sync
        def _(sp):
            sp.dma_start(mask_u8[:, :], w["mask"]).then_inc(mask_loaded, 16)
            for dst, src in loads:
                sp.dma_start(dst, src).then_inc(loaded, 16)
            sp.wait_ge(mask_ready, 1)
            sp.dma_start(w["mask_bias"], mask_bias[:, :]).then_inc(mask_stored, 16)
            sp.wait_ge(mask_stored, 16)
            sp.wait_ge(loaded, 16 * len(loads))

        @block.vector
        def _(dve):
            dve.memset(zero_f[:, :], 0.0).then_inc(zeroed, 1)
            dve.memset(s.ones[:, :], 1.0).then_inc(zeroed, 1)
            dve.memset(s.eps[:, :], EPS).then_inc(zeroed, 1)
            dve.wait_ge(mask_loaded, 16)
            dve.tensor_scalar(mask_bias[:, :], mask_u8[:, :], -MASKED, MASKED, ALU.mult, ALU.add).then_inc(mask_ready, 1)
            dve.wait_ge(made, 1)
            dve.tensor_copy(s.ident_b[:, :], s.ident[:, :]).then_inc(made, 1)

        @block.gpsimd
        def _(pool):
            pool.wait_ge(zeroed, 1)
            pool.affine_select(out=s.ident[:, :], in_=zero_f[:, :], compare_op=ALU.not_equal, fill=1.0,
                               base=0, pattern=[[-1, P]], channel_multiplier=1).then_inc(made, 1)


def layer_norm(nc, s, tag):
    with ExitStack() as ctx:
        o = opened(nc, ctx)
        stats = o.sb(tag + "_stats", [P, PAIRS, 6])
        moments = o.sb(tag + "_moments", [P, PAIRS, 2])
        std = o.sb(tag + "_std", [P, PAIRS])
        rstd = o.sb(tag + "_rstd", [P, PAIRS])
        ps = o.ps(tag + "_ps", [P, TCH, 512])
        stats_ready, moments_ready, std_ready, rstd_ready, xn_ready, turned, taken = (
            o.sem(f"{tag}_{n}") for n in ("stats_ready", "moments_ready", "std_ready", "rstd_ready", "xn_ready", "turned", "taken"))
        block = o.block()

        @block.vector
        def _(dve):
            for t in range(PAIRS):
                dve.bn_stats(stats[:, t, :], s.x[:, t, :]).then_inc(stats_ready, 1)
            for t in range(PAIRS):
                dve.wait_ge(stats_ready, t + 1)
                dve.bn_aggr(moments[:, t, :], stats[:, t, :]).then_inc(moments_ready, 1)
            dve.wait_ge(std_ready, 1)
            dve.reciprocal(rstd[:, :], std[:, :]).then_inc(rstd_ready, 1)
            dve.wait_ge(rstd_ready, 1)
            for t in range(PAIRS):
                dve.tensor_scalar(s.xn[:, t, :], s.x[:, t, :], moments[:, t, 0:1], rstd[:, t:t + 1],
                                  ALU.subtract, ALU.mult).then_inc(xn_ready, 1)
            for c in range(0, TCH, 2):
                dve.wait_ge(turned, 4 * (c + 1))
                dve.tensor_copy(s.xT[:, 512 * c:512 * c + 512], ps[:, c, :]).then_inc(taken, 1)

        @block.scalar
        def _(act):
            act.wait_ge(moments_ready, PAIRS)
            act.activation(std[:, :], moments[:, :, 1], ACT.Sqrt, bias=s.eps[:, 0:1]).then_inc(std_ready, 1)
            for c in range(1, TCH, 2):
                act.wait_ge(turned, 4 * (c + 1))
                act.copy(s.xT[:, 512 * c:512 * c + 512], ps[:, c, :]).then_inc(taken, 1)

        @block.tensor
        def _(pe):
            for t in range(PAIRS):
                pe.wait_ge(xn_ready, t + 1)
                pe.transpose(ps[:, t // 4, P * (t % 4):P * (t % 4) + P], s.xn[:, t, :], s.ident[:, :]).then_inc(turned, 1)


def add_projection(nc, s, att, weight, bias, tag):
    with ExitStack() as ctx:
        o = opened(nc, ctx)
        ps_t = o.ps(tag + "_ps_t", [P, 2, 512])
        ps_y = o.ps(tag + "_ps_y", [P, 2, 512])
        attT = o.sb(tag + "_attT", [P, 2, 512])
        turned, taken, projected, added = (o.sem(f"{tag}_{n}") for n in ("turned", "taken", "projected", "added"))
        block = o.block()

        @block.tensor
        def _(pe):
            def turn(c):
                if c >= 2:
                    pe.wait_ge(taken, c - 1)
                for k in range(4):
                    ins = pe.transpose(ps_t[:, c % 2, P * k:P * k + P], att[:, 4 * c + k, :], s.ident[:, :])
                ins.then_inc(turned, 1)

            turn(0)
            for c in range(TCH):
                if c + 1 < TCH:
                    turn(c + 1)
                pe.wait_ge(taken, c + 1)
                if c >= 2:
                    pe.wait_ge(added, c - 1)
                for k in range(4):
                    ins = pe.matmul(ps_y[:, c % 2, P * k:P * k + P], attT[:, c % 2, P * k:P * k + P], weight[:, :],
                                    start=True, stop=True)
                ins.then_inc(projected, 1)

        @block.scalar
        def _(act):
            for c in range(TCH):
                act.wait_ge(turned, c + 1)
                if c >= 2:
                    act.wait_ge(projected, c - 1)
                act.copy(attT[:, c % 2, :], ps_t[:, c % 2, :]).then_inc(taken, 1)

        @block.vector
        def _(dve):
            if bias is not None:
                for t in range(PAIRS):
                    dve.tensor_tensor(s.x[:, t, :], s.x[:, t, :], bias[:, :], ALU.add).then_inc(s.x_biased, 1)
                s.x_biased_count += PAIRS
                dve.wait_ge(s.x_biased, s.x_biased_count)
            for c in range(TCH):
                dve.wait_ge(projected, c + 1)
                dve.tensor_tensor(s.x[:, 4 * c:4 * c + 4, :], s.x[:, 4 * c:4 * c + 4, :],
                                  ps_y[:, c % 2, :].rearrange("p (t d) -> p t d", t=4), ALU.add).then_inc(added, 1)


def cross_attention_0(nc, w, s):
    with ExitStack() as ctx:
        o = opened(nc, ctx)
        q_parts = o.sb("q_parts", [P, 3, T], BF16)
        num = o.sb("num", [P, PAIRS, D])
        den = o.sb("den", [P, PAIRS, H])
        project_queries_0(nc, s, q_parts)
        attend_context_0(nc, w, s, q_parts, num, den)
        rden = o.sb("rden", [P, PAIRS, H])
        inverted, scaled = o.sem("x0_inverted"), o.sem("x0_scaled")
        with nc.Block() as block:
            @block.vector
            def _(dve):
                dve.reciprocal(rden[:, :, :], den[:, :, :]).then_inc(inverted, 1)
                dve.wait_ge(inverted, 1)
                v = num[:, :, :].rearrange("p t (h d) -> p (t h) d", d=HD)
                r = rden[:, :, :].rearrange("p t h -> p (t h)").unsqueeze(2).broadcast_to([P, PAIRS * H, HD])
                dve.tensor_tensor(v, v, r, ALU.mult).then_inc(scaled, 1)
        add_projection(nc, s, num, s.w["x0_wo"], None, "x0o")


def project_queries_0(nc, s, q_parts):
    with ExitStack() as ctx:
        o = opened(nc, ctx)
        ps = o.ps("q0_ps", [P, TCH, 512])
        rest = o.sb("q0_rest", [P, TCH, 512])
        projected, high, rest1, mid, low = (o.sem("q0_" + n) for n in ("projected", "high", "rest1", "mid", "low"))
        block = o.block()

        @block.tensor
        def _(pe):
            for c in range(TCH):
                pe.matmul(ps[:, c, :], s.w["x0_wq"][:, :], s.xT[:, 512 * c:512 * c + 512],
                          start=True, stop=True).then_inc(projected, 1)

        @block.vector
        def _(dve):
            for c in range(TCH):
                at = slice(512 * c, 512 * c + 512)
                dve.wait_ge(projected, c + 1)
                dve.tensor_copy(q_parts[:, 0, at], ps[:, c, :]).then_inc(high, 1)
                dve.wait_ge(high, c + 1)
                dve.tensor_tensor(rest[:, c, :], ps[:, c, :], q_parts[:, 0, at], ALU.subtract).then_inc(rest1, 1)
                dve.wait_ge(rest1, c + 1)
                dve.tensor_copy(q_parts[:, 1, at], rest[:, c, :]).then_inc(mid, 1)
                dve.wait_ge(mid, c + 1)
                dve.tensor_tensor(q_parts[:, 2, at], rest[:, c, :], q_parts[:, 1, at], ALU.subtract).then_inc(low, 1)


def attend_context_0(nc, w, s, q_parts, num, den):
    with ExitStack() as ctx:
        o = opened(nc, ctx)
        ctxT = o.sb("ctxT", [C, 2, M])
        keys = o.sb("keys", [P, M])
        krest = o.sb("krest", [P, M])
        k_parts = o.sb("k_parts", [P, 3, M], BF16)
        kst = o.sb("kst", [SROWS, 2, G, M], BF16)
        qst = o.sb("qst", [SROWS, 2, G, 2, S], BF16)
        vals = o.sb("vals", [P, 2, KT, 6, 32])
        probs = o.sb("probs", [P, 2, H * S])
        max4 = o.sb("max4", [P, G, MC])
        negmax = o.sb("negmax", [P, G])
        maxrest = o.sb("maxrest", [P, G])
        m_parts = o.sb("m_parts", [P, 3, G], BF16)
        m_rows = o.sb("m_rows", [3 * G, P], BF16)
        acc_sb = o.sb("acc_sb", [P, 7, 2, S])
        turned_sb = o.sb("turned_sb", [P, 7, P])
        sum2 = o.sb("sum2", [P, 4, 2, 32])
        sum1 = o.sb("sum1", [P, 4, 32])
        ps_s = o.ps("ps_s", [P, 2, H * S])
        ps_m = o.ps("ps_m", [P, 2, 512])
        ps_x = o.ps("ps_x", [P, 512])
        ps_a = o.ps("ps_a", [P, 512])
        sem = {n: o.sem("x0_" + n) for n in (
            "set_up", "vals_set_up", "pool_held", "sp_held", "k_filled", "keys_ready", "v_filled", "vals_ready", "khigh", "krest1", "kmid", "k_split",
            "scored", "probs_ready", "pv_done", "max_filled", "max_taken", "max_chain", "m_parts_ready", "m_filled",
            "m_taken", "acc_taken", "turn_filled", "turn_taken", "sum2_ready", "sum1_ready", "gathered")}
        q = Names(**sem)
        q.ctx_loaded = [o.sem(f"x0_ctx_loaded{u}") for u in range(2)]
        q.k_stacked = [o.sem(f"x0_k_stacked{u}") for u in range(2)]
        q.q_stacked = [o.sem(f"x0_q_stacked{u}") for u in range(2)]
        q.m_stacked = [o.sem(f"x0_m_stacked{u}") for u in range(2)]
        NKD, NQD = 16 * (TERMS + 1), 16 * 2 * TERMS
        NMX = G * MC
        block = o.block()

        def pairs(eng, body):
            body(0, True, False)
            with eng.Fori(1, PAIRS - 1) as i:
                body(i, False, False)
            body(PAIRS - 1, False, True)

        @block.sync
        def _(sp):
            def load_ctx(b, u):
                sp.dma_start(ctxT[:, u, :], w["ctxT"][b]).then_inc(q.ctx_loaded[u], 16)

            def stack(b, u):
                sp.wait_ge(q.k_split, b + 1)
                for t in range(TERMS):
                    sp.dma_start(kst[2 * HD * t:2 * HD * (t + 1), u, :, :], k_parts[:, K_PARTS[t], :]).then_inc(q.k_stacked[u], 16)
                sp.dma_start(kst[MROW:MROW + 1, u, :, :],
                             w["mask_bias"][b].unsqueeze(0).unsqueeze(0).broadcast_to([1, G, M])).then_inc(q.k_stacked[u], 16)
                for t in range(TERMS):
                    for a in range(2):
                        sp.dma_start(qst[(2 * t + a) * HD:(2 * t + a + 1) * HD, u, :, a, :],
                                     q_parts[64 * a:64 * a + 64, Q_PARTS[t], bass.ds(S * b, S)]).then_inc(q.q_stacked[u], 16)

            def stack_maxima(b, u):
                sp.wait_ge(q.m_taken, b + 1)
                sp.dma_start(qst[MROW + 1:MROW + 4, u, :, :, :], m_rows[:, :]).then_inc(q.m_stacked[u], 16)

            load_ctx(0, 0)
            load_ctx(1, 1)
            sp.wait_ge(q.set_up, 3)
            stack(0, 0)
            stack(1, 1)
            sp.wait_ge(q.v_filled, 4)
            load_ctx(2, 0)
            stack_maxima(0, 0)

            def step(b, i, u, last, late):
                if not last:
                    sp.wait_ge(q.v_filled, 4 * (b + 2))
                    hold(sp, q.sp_held)
                    sp.wait_ge(q.scored, KT * (b + 1))
                    hold(sp, q.sp_held)
                    stack(b + 2, u)
                    if not (late and u == 1):
                        load_ctx(b + 3, 1 - u)
                if not (last and u == 1):
                    stack_maxima(b + 1, 1 - u)

            def body(i, first, last):
                for u in range(2):
                    step(2 * i + u, i, u, last, False)
            body(0, True, False)
            with sp.Fori(1, PAIRS - 2) as i:
                body(i, False, False)
            for u in range(2):
                step(2 * (PAIRS - 2) + u, PAIRS - 2, u, False, True)
            body(PAIRS - 1, False, True)
            for u in range(2):
                sp.wait_ge(q.m_stacked[u], 16 * PAIRS)

        @block.tensor
        def _(pe):
            def job_keys(b, c, i, u):
                if c == 0:
                    pe.wait_ge(q.ctx_loaded[u], 16 * (i + 1))
                n = CCOLS[c]
                pe.matmul(ps_x[:, 0:n], s.w["x0_wk"][:, :], ctxT[:, u, 512 * c:512 * c + n],
                          start=True, stop=True).then_inc(q.k_filled, 1)

            def job_values(b, v, i, u):
                if v == 0:
                    pe.wait_ge(q.ctx_loaded[u], 16 * (i + 1))
                for j in range(4 * v, min(4 * v + 4, KT)):
                    ins = pe.matmul(ps_x[0:KROWS[j], D * (j % 4):D * (j % 4) + D], ctxT[:, u, P * j:P * j + KROWS[j]],
                                    s.w["x0_wv"][:, :], start=True, stop=True)
                ins.then_inc(q.v_filled, 1)

            def job_maxima(b):
                pe.wait_ge(q.m_parts_ready, b + 1)
                pe.transpose(ps_x[:, :].bitcast(BF16)[0:3 * G, 0:P], m_parts[:, :, :].rearrange("p t g -> p (t g)"),
                             s.ident_b[:, :]).then_inc(q.m_filled, 1)

            def max_chunk(b, k, i, u, first):
                g, c = k // MC, k % MC
                if k == 0:
                    pe.wait_ge(q.k_stacked[u], NKD * (i + 1))
                    pe.wait_ge(q.q_stacked[u], NQD * (i + 1))
                if not (first and k < 2):
                    pe.wait_ge(q.max_taken, NMX * b + k - 1)
                n = CCOLS[c]
                pe.matmul(ps_m[:, k % 2, 0:n], qst[0:MROW + 1, u, g, :, :].rearrange("p a q -> p (a q)"),
                          kst[0:MROW + 1, u, g, 512 * c:512 * c + n], start=True, stop=True).then_inc(q.max_filled, 1)

            def scores(b, j, i, u, first):
                n = KT * b + j
                slot, k = (u + j) % 2, KROWS[j]
                if j == 0:
                    pe.wait_ge(q.m_stacked[u], 16 * (i + 1))
                if not (first and u == 0 and j < 2):
                    pe.wait_ge(q.probs_ready, n - 1)
                for g in range(G):
                    ins = pe.matmul(ps_s[0:k, slot, P * g:P * g + P], kst[:, u, g, P * j:P * j + k],
                                    qst[:, u, g, :, :].rearrange("p a q -> p (a q)"), start=True, stop=True)
                ins.then_inc(q.scored, 1)

            def value_sums(b, j, i, u, first):
                n = KT * b + j
                slot, k = (u + j) % 2, KROWS[j]
                pe.wait_ge(q.probs_ready, n + 1)
                if j == 0:
                    pe.wait_ge(q.vals_ready, 4 * (b + 1))
                    if not (first and u == 0):
                        pe.wait_ge(q.acc_taken, b)
                place = [(g, g, 0) for g in range(4)] + [(4, j % 4, 192), (5, (j + 2) % 4, 384)]
                for g, tile, col in place:
                    cols = 192 if g < 5 else 64
                    ins = pe.matmul(ps_a[32 * tile:32 * tile + 32, col:col + cols], vals[0:k, u, j, g, :],
                                    probs[0:k, slot, 192 * g:192 * g + cols],
                                    start=(j == 0 and g < 4), stop=(j == KT - 1), skip_group_check=True)
                ins.then_inc(q.pv_done, 1)

            def turn_sums(n, i):
                for r in range(4 * n, min(4 * n + 4, 7)):
                    ins = pe.transpose(ps_x[:, P * (r % 4):P * (r % 4) + P],
                                       acc_sb[:, r, :, :].rearrange("p b q -> p (b q)"), s.ident[:, :])
                ins.then_inc(q.turn_filled, 1)

            pe.wait_ge(q.set_up, 3)
            for b in range(2):
                for c in range(MC):
                    if b or c:
                        pe.wait_ge(q.keys_ready, MC * b + c)
                    job_keys(b, c, 0, b)
            for v in range(4):
                if v == 0:
                    pe.wait_ge(q.keys_ready, 2 * MC)
                else:
                    pe.wait_ge(q.vals_ready, v)
                job_values(0, v, 0, 0)
            for k in range(NMX):
                max_chunk(0, k, 0, 0, True)
            pe.wait_ge(q.vals_ready, 4)
            job_maxima(0)

            def step(b, i, u, first, last):
                for j in range(KT):
                    scores(b, j, i, u, first)
                    if j:
                        value_sums(b, j - 1, i, u, first)
                    if not (last and u == 1):
                        for k in range(3 * j, min(3 * j + 3, NMX)):
                            max_chunk(b + 1, k, i + u, 1 - u, False)
                        if j < 4:
                            if j == 0:
                                pe.wait_ge(q.m_taken, b + 1)
                            else:
                                pe.wait_ge(q.vals_ready, 4 * (b + 1) + j)
                            job_values(b + 1, j, i + u, 1 - u)
                    if 4 <= j < 8 and not last:
                        if j == 4:
                            pe.wait_ge(q.vals_ready, 4 * (b + 2))
                        else:
                            pe.wait_ge(q.keys_ready, MC * (b + 2) + j - 4)
                        job_keys(b + 2, j - 4, i + 1, u)
                    if j in (8, 9) and u == 0 and not first:
                        if j == 8:
                            pe.wait_ge(q.acc_taken, b)
                            if last:
                                pe.wait_ge(q.vals_ready, 4 * (b + 2))
                            else:
                                pe.wait_ge(q.keys_ready, MC * (b + 3))
                        else:
                            pe.wait_ge(q.turn_taken, 2 * i - 1)
                        turn_sums(j - 8, i - 1)
                value_sums(b, KT - 1, i, u, first)
                if not (last and u == 1):
                    if u == 0 and not first:
                        pe.wait_ge(q.turn_taken, 2 * i)
                    elif last:
                        pe.wait_ge(q.vals_ready, 4 * (b + 2))
                    else:
                        pe.wait_ge(q.keys_ready, MC * (b + 3))
                    job_maxima(b + 1)

            def body(i, first, last):
                for u in range(2):
                    step(2 * i + u, i, u, first, last)
            pairs(pe, body)
            pe.wait_ge(q.acc_taken, B)
            pe.wait_ge(q.m_taken, B)
            turn_sums(0, PAIRS - 1)
            pe.wait_ge(q.turn_taken, 2 * PAIRS - 1)
            turn_sums(1, PAIRS - 1)

        @block.scalar
        def _(act):
            def take_keys(b, c):
                act.wait_ge(q.k_filled, MC * b + c + 1)
                n = CCOLS[c]
                act.copy(keys[:, 512 * c:512 * c + n], ps_x[:, 0:n]).then_inc(q.keys_ready, 1)

            def take_values(b, v, u):
                act.wait_ge(q.v_filled, 4 * b + v + 1)
                k, n = (P, 4) if v < 3 else (KROWS[-1], 1)
                src = ps_x[0:k, 0:D * n].rearrange("p (j c) -> p j c", j=n)
                act.copy(vals[0:k, u, 4 * v:4 * v + n, 0:5, 0:24], src[:, :, 0:120].rearrange("p j (g c) -> p j g c", g=5))
                act.copy(vals[0:k, u, 4 * v:4 * v + n, 5, 0:8], src[:, :, 120:128]).then_inc(q.vals_ready, 1)

            act.wait_ge(q.vals_set_up, 2)
            for b in range(2):
                for c in range(MC):
                    if b and c == 0:
                        act.wait_ge(q.k_split, b)
                    take_keys(b, c)
            for v in range(4):
                take_values(0, v, 0)

            def step(b, i, u, first, last):
                for j in range(KT):
                    n = KT * b + j
                    slot, k = (u + j) % 2, KROWS[j]
                    act.wait_ge(q.scored, n + 1)
                    if not (first and u == 0 and j < 2):
                        act.wait_ge(q.pv_done, n - 1)
                    act.activation(probs[0:k, slot, :], ps_s[0:k, slot, :], ACT.Exp, scale=float(HD) ** -0.5).then_inc(q.probs_ready, 1)
                    if j < 4 and not (last and u == 1):
                        if j == 0 and not (first and u == 0):
                            act.wait_ge(q.pv_done, KT * b)
                        take_values(b + 1, j, 1 - u)
                    if 4 <= j < 8 and not last:
                        if j == 4:
                            act.wait_ge(q.k_split, b + 2)
                        take_keys(b + 2, j - 4)

            def body(i, first, last):
                for u in range(2):
                    step(2 * i + u, i, u, first, last)
            pairs(act, body)

        @block.vector
        def _(dve):
            dve.memset(qst[:, :, :, :, :], 0.0).then_inc(q.set_up, 1)
            dve.memset(kst[96:SROWS, :, :, :], 1.0).then_inc(q.set_up, 1)
            dve.wait_ge(q.set_up, 2)
            dve.memset(qst[96:97, :, :, :, :], 1.0).then_inc(q.set_up, 1)

            def take_max(b, k):
                g, c = k // MC, k % MC
                dve.wait_ge(q.max_filled, NMX * b + k + 1)
                dve.tensor_reduce(max4[:, g, c:c + 1], ps_m[:, k % 2, 0:CCOLS[c]], AX.X, ALU.max).then_inc(q.max_taken, 1)

            def split_max(b, u, i, first):
                dve.wait_ge(q.max_taken, NMX * (b + 1))
                dve.tensor_reduce(negmax[:, :], max4[:, :, :], AX.X, ALU.max, negate=True).then_inc(q.max_chain, 1)
                dve.wait_ge(q.max_chain, 4 * b + 1)
                dve.tensor_copy(m_parts[:, 0, :], negmax[:, :]).then_inc(q.max_chain, 1)
                dve.wait_ge(q.max_chain, 4 * b + 2)
                dve.tensor_tensor(maxrest[:, :], negmax[:, :], m_parts[:, 0, :], ALU.subtract).then_inc(q.max_chain, 1)
                dve.wait_ge(q.max_chain, 4 * b + 3)
                dve.tensor_copy(m_parts[:, 1, :], maxrest[:, :]).then_inc(q.max_chain, 1)
                dve.wait_ge(q.max_chain, 4 * b + 4)
                dve.tensor_tensor(m_parts[:, 2, :], maxrest[:, :], m_parts[:, 1, :], ALU.subtract).then_inc(q.m_parts_ready, 1)
                dve.wait_ge(q.m_filled, b + 1)
                if not first:
                    dve.wait_ge(q.m_stacked[1 - u], 16 * (i + u))
                dve.tensor_copy(m_rows[:, :], ps_x[:, :].bitcast(BF16)[0:3 * G, 0:P]).then_inc(q.m_taken, 1)

            for k in range(NMX):
                take_max(0, k)
            split_max(0, 0, 0, True)

            def take_turned(n, i, first):
                dve.wait_ge(q.turn_filled, 2 * i + n + 1)
                if n == 0 and not first:
                    dve.wait_ge(q.gathered, i)
                r = 4 if n == 0 else 3
                dve.tensor_copy(turned_sb[:, 4 * n:4 * n + r, :].rearrange("p r c -> p (r c)"),
                                ps_x[:, 0:P * r]).then_inc(q.turn_taken, 1)

            def step(b, i, u, first, last):
                if not (last and u == 1):
                    for k in range(NMX):
                        take_max(b + 1, k)
                        if u == 0 and not first and k in (26, 29):
                            take_turned((26, 29).index(k), i - 1, False)
                    split_max(b + 1, 1 - u, i + u, False)
                dve.wait_ge(q.pv_done, KT * (b + 1))
                if not first:
                    dve.wait_ge(q.turn_filled, 2 * i)
                dve.tensor_copy(acc_sb[:, :, u, :], ps_a[:, 0:448].rearrange("p (r q) -> p r q", q=S)).then_inc(q.acc_taken, 1)

            def body(i, first, last):
                for u in range(2):
                    step(2 * i + u, i, u, first, last)
            pairs(dve, body)
            for n in range(2):
                take_turned(n, PAIRS - 1, False)

        @block.gpsimd
        def _(pool):
            pool.memset(vals[:, :, :, :, :], 0.0).then_inc(q.vals_set_up, 1)

            def split_keys(b, i, u, first):
                pool.wait_ge(q.keys_ready, MC * (b + 1))
                if not first:
                    pool.wait_ge(q.k_stacked[1 - u], NKD * (i + u))
                hold(pool, q.pool_held)
                pool.tensor_copy(k_parts[:, 0, :], keys[:, :]).then_inc(q.khigh, 1)
                pool.wait_ge(q.khigh, b + 1)
                pool.tensor_tensor(krest[:, :], keys[:, :], k_parts[:, 0, :], ALU.subtract).then_inc(q.krest1, 1)
                pool.wait_ge(q.krest1, b + 1)
                hold(pool, q.pool_held)
                pool.tensor_copy(k_parts[:, 1, :], krest[:, :]).then_inc(q.kmid, 1)
                pool.wait_ge(q.kmid, b + 1)
                pool.tensor_tensor(k_parts[:, 2, :], krest[:, :], k_parts[:, 1, :], ALU.subtract).then_inc(q.k_split, 1)

            def gather(i):
                pool.wait_ge(q.turn_taken, 2 * i + 2)
                hold(pool, q.pool_held)
                for a in range(3):
                    tl = turned_sb[:, a, :].rearrange("p (s r) -> p s r", r=32)
                    pool.tensor_copy(num[:, bass.ds(i, 1), 0:96].rearrange("p o (s a d) -> p (o s) a d", s=4, a=3)[:, :, a, :],
                                     tl[:, :, HD * a:HD * a + HD])
                    pool.tensor_copy(den[:, bass.ds(i, 1), 0:12].rearrange("p o (s a) -> p (o s) a", a=3)[:, :, a:a + 1],
                                     tl[:, :, 24:25])
                tl = turned_sb[:, 3:7, :].rearrange("p r (s c) -> p r s c", c=32)
                pool.tensor_tensor(sum2[:, :, :, :], tl[:, :, 0:2, :], tl[:, :, 2:4, :], ALU.add).then_inc(q.sum2_ready, 1)
                pool.wait_ge(q.sum2_ready, i + 1)
                pool.tensor_tensor(sum1[:, :, :], sum2[:, :, 0, :], sum2[:, :, 1, :], ALU.add).then_inc(q.sum1_ready, 1)
                pool.wait_ge(q.sum1_ready, i + 1)
                hold(pool, q.pool_held)
                for r in range(4):
                    a = r if r < 3 else 0
                    pool.tensor_copy(num[:, bass.ds(i, 1), 96 + 8 * r:104 + 8 * r], sum1[:, r, HD * a:HD * a + HD].unsqueeze(1))
                pool.tensor_copy(den[:, bass.ds(i, 1), 12:16], sum1[:, :, 24].unsqueeze(1)).then_inc(q.gathered, 1)

            pool.wait_ge(q.vals_set_up, 1)
            pool.memset(vals[:, :, :, :, 24:25], 1.0).then_inc(q.vals_set_up, 1)
            for b in range(2):
                split_keys(b, 0, b, b == 0)

            def body(i, first, last):
                for u in range(2):
                    if not last:
                        split_keys(2 * i + u + 2, i + 1, u, False)
                    if u == 0 and not first:
                        gather(i - 1)
            pairs(pool, body)
            gather(PAIRS - 1)


PEEL = 4


def pipeline(eng, count, step):
    for n in range(PEEL):
        step(n, n % 2, n // 2)
    with eng.Fori(PEEL // 2, count // 2) as i:
        for u in range(2):
            step(2 * i + u, u, i)
    for n in range(count, count + PEEL):
        step(n, n % 2, n // 2)


def exists(n, back, count):
    return not isinstance(n, int) or 0 <= n - back < count


def since(n, first):
    return not isinstance(n, int) or n >= first


class Chain:

    def __init__(self, eng, sem):
        self.eng, self.sem, self.n = eng, sem, 0

    def __call__(self, ins):
        ins.then_inc(self.sem, 1)
        self.n += 1

    def wait(self):
        self.eng.wait_ge(self.sem, self.n)


def self_attention_0(nc, w, s):
    with ExitStack() as ctx:
        o = opened(nc, ctx)
        qT = o.sb("a0_qT", [P, T])
        kT = o.sb("a0_kT", [P, T])
        v_all = o.sb("a0_v", [S, B, D])
        att = o.sb("a0_att", [P, PAIRS, D])
        project_rotate_0(nc, s, qT, kT, v_all)
        attend_self_0(nc, s, qT, kT, v_all, att)
        add_projection(nc, s, att, s.w["a0_woT"], s.w["a0_bo"], "a0o")


def project_rotate_0(nc, s, qT, kT, v_all):
    with ExitStack() as ctx:
        o = opened(nc, ctx)
        ps = o.ps("r0_ps", [P, 4, 512])
        ps_v = o.ps("r0_ps_v", [S, 2, 512])
        turned = o.sb("r0_turned", [P, 2, 512])
        projected, straight, crossed, rotated, v_filled, v_ready = (
            o.sem("r0_" + n) for n in ("projected", "straight", "crossed", "rotated", "v_filled", "v_ready"))
        jobs = [(c, which) for c in range(TCH) for which in range(2)]
        block = o.block()

        @block.tensor
        def _(pe):
            for n, (c, which) in enumerate(jobs):
                names = (("a0_wqT", "a0_wqT_sw"), ("a0_wkT", "a0_wkT_sw"))[which]
                for r in range(2):
                    if n >= 2:
                        pe.wait_ge((straight, crossed)[r], n - 1)
                    pe.matmul(ps[:, 2 * (n % 2) + r, :], s.w[names[r]][:, :], s.xT[:, 512 * c:512 * c + 512],
                              start=True, stop=True).then_inc(projected, 1)
                if n >= 2:
                    pe.wait_ge(v_ready, n - 1)
                for k in range(4):
                    b = 4 * n + k
                    ins = pe.matmul(ps_v[:, n % 2, D * k:D * k + D], s.xT[:, S * b:S * b + S], s.w["a0_wvT"][:, :],
                                    start=True, stop=True)
                ins.then_inc(v_filled, 1)

        @block.vector
        def _(dve):
            for n, (c, which) in enumerate(jobs):
                dst, b0, b1 = ((qT, "a0_bq", "a0_bq_sw"), (kT, "a0_bk", "a0_bk_sw"))[which]
                at = dst[:, 512 * c:512 * c + 512].rearrange("p (b s) -> p b s", s=S)
                cos = s.w["a0_cos"][:, :].unsqueeze(1).broadcast_to([P, 8, S])
                sin = s.w["a0_sin"][:, :].unsqueeze(1).broadcast_to([P, 8, S])
                tmp = turned[:, n % 2, :].rearrange("p (b s) -> p b s", s=S)
                dve.wait_ge(projected, 2 * n + 2)
                dve.scalar_tensor_tensor(out=at, in0=ps[:, 2 * (n % 2), :].rearrange("p (b s) -> p b s", s=S),
                                         scalar=s.w[b0][:, 0:1], in1=cos, op0=ALU.add, op1=ALU.mult).then_inc(straight, 1)
                dve.scalar_tensor_tensor(out=tmp, in0=ps[:, 2 * (n % 2) + 1, :].rearrange("p (b s) -> p b s", s=S),
                                         scalar=s.w[b1][:, 0:1], in1=sin, op0=ALU.add, op1=ALU.mult).then_inc(crossed, 1)
                dve.wait_ge(straight, n + 1)
                dve.wait_ge(crossed, n + 1)
                dve.tensor_tensor(at, at, tmp, ALU.add).then_inc(rotated, 1)
                dve.wait_ge(v_filled, n + 1)
                dve.tensor_tensor(v_all[:, 4 * n:4 * n + 4, :], ps_v[:, n % 2, :].rearrange("p (b d) -> p b d", d=D),
                                  s.w["a0_bv"][0:S, :].unsqueeze(1).broadcast_to([S, 4, D]), ALU.add).then_inc(v_ready, 1)


def attend_self_0(nc, s, qT, kT, v_all, att):
    with ExitStack() as ctx:
        o = opened(nc, ctx)
        qbd = o.sb("a0_qbd", [P, 2, H, S])
        sc = o.sb("a0_sc", [P, 2, G, S])
        pr = o.sb("a0_pr", [P, 2, G, S])
        prT = o.sb("a0_prT", [S, 2, H, S])
        vst = o.sb("a0_vst", [S, 2, D])
        mx = o.sb("a0_mx", [P, 2, G])
        sm = o.sb("a0_sm", [P, 2, G])
        ps_s = o.ps("a0_ps_s", [P, 2, 512])
        ps_t = o.ps("a0_ps_t", [S, H * S])
        ps_o = o.ps("a0_ps_o", [P, 2, 512])
        q = Names(**{n: o.sem("a0_" + n) for n in (
            "held", "qbd_ready", "v_staged", "scored", "masked", "maxed", "shifted", "probs_ready", "summed", "inverted",
            "normed", "turned", "turned_ready", "pv_done", "att_ready")})
        block = o.block()

        @block.tensor
        def _(pe):
            def step(n, u, i):
                if exists(n, 0, B):
                    pe.wait_ge(q.qbd_ready, n + 1)
                    if since(n, 2):
                        pe.wait_ge(q.masked, n - 1)
                    for g in range(G):
                        ins = pe.matmul(ps_s[:, u, S * g:S * g + S], qbd[:, u, 2 * g:2 * g + 2, :].rearrange("p h q -> p (h q)"),
                                        kT[:, bass.ds(S * n, S)], start=True, stop=True)
                    ins.then_inc(q.scored, 1)
                if exists(n, 2, B):
                    pe.wait_ge(q.normed, n - 1)
                    if since(n, 3):
                        pe.wait_ge(q.turned_ready, n - 2)
                    pe.sem_inc(q.held)
                    for g in range(G):
                        ins = pe.transpose(ps_t[:, P * g:P * g + P], pr[:, u, g, :], s.ident[:, :])
                    ins.then_inc(q.turned, 1)
                if exists(n, 3, B):
                    r = 1 - u
                    pe.wait_ge(q.turned_ready, n - 2)
                    pe.wait_ge(q.v_staged, n - 2)
                    if since(n, 5):
                        pe.wait_ge(q.att_ready, n - 4)
                    pe.sem_inc(q.held)
                    for h in range(H):
                        ins = pe.matmul(ps_o[S * r:S * r + S, r, HD * h:HD * h + HD], prT[:, r, h, :],
                                        vst[:, r, HD * h:HD * h + HD], start=True, stop=True)
                    ins.then_inc(q.pv_done, 1)
            pipeline(pe, B, step)

        @block.vector
        def _(dve):
            def step(n, u, i):
                if exists(n, 0, B):
                    dve.wait_ge(q.scored, n + 1)
                    if since(n, 2):
                        dve.wait_ge(q.probs_ready, n - 1)
                    dve.scalar_tensor_tensor(out=sc[:, u, :, :], in0=ps_s[:, u, :].rearrange("p (g k) -> p g k", k=S),
                                             scalar=float(HD) ** -0.5,
                                             in1=s.w["a0_causal"][:, :].unsqueeze(1).broadcast_to([P, G, S]),
                                             op0=ALU.mult, op1=ALU.add).then_inc(q.masked, 1)
                    dve.wait_ge(q.masked, n + 1)
                    dve.tensor_reduce(mx[:, u, :], sc[:, u, :, :], AX.X, ALU.max).then_inc(q.maxed, 1)
                    dve.wait_ge(q.maxed, n + 1)
                    dve.tensor_tensor(sc[:, u, :, :], sc[:, u, :, :], mx[:, u, :].unsqueeze(2).broadcast_to([P, G, S]),
                                      ALU.subtract).then_inc(q.shifted, 1)
                if exists(n, 1, B):
                    r = 1 - u
                    dve.wait_ge(q.probs_ready, n)
                    if since(n, 3):
                        dve.wait_ge(q.normed, n - 2)
                    dve.tensor_reduce(sm[:, r, :], pr[:, r, :, :], AX.X, ALU.add).then_inc(q.summed, 1)
                    dve.wait_ge(q.summed, n)
                    dve.reciprocal(sm[:, r, :], sm[:, r, :]).then_inc(q.inverted, 1)
            pipeline(dve, B, step)

        @block.scalar
        def _(act):
            def step(n, u, i):
                if exists(n, 0, B):
                    act.wait_ge(q.shifted, n + 1)
                    if since(n, 2):
                        act.wait_ge(q.turned, n - 1)
                    act.activation(pr[:, u, :, :], sc[:, u, :, :], ACT.Exp).then_inc(q.probs_ready, 1)
                if exists(n, 2, B):
                    act.wait_ge(q.turned, n - 1)
                    if since(n, 4):
                        act.wait_ge(q.pv_done, n - 3)
                    act.copy(prT[:, u, :, :].rearrange("p h q -> p (h q)"), ps_t[:, :]).then_inc(q.turned_ready, 1)
                if exists(n, 3, B):
                    r = 1 - u
                    act.wait_ge(q.pv_done, n - 2)
                    act.sem_inc(q.held)
                    dst = att[S * r:S * r + S, bass.ds(i - 2 + u, 1), :].rearrange("p t d -> p (t d)")
                    act.copy(dst, ps_o[S * r:S * r + S, r, 0:D]).then_inc(q.att_ready, 1)
            pipeline(act, B, step)

        @block.gpsimd
        def _(pool):
            def step(n, u, i):
                if exists(n, 0, B):
                    if since(n, 2):
                        pool.wait_ge(q.scored, n - 1)
                        pool.sem_inc(q.held)
                    pool.tensor_tensor(qbd[:, u, :, :], qT[:, bass.ds(S * n, S)].unsqueeze(1).broadcast_to([P, H, S]),
                                       s.w["a0_heads"][:, :].unsqueeze(2).broadcast_to([P, H, S]), ALU.mult).then_inc(q.qbd_ready, 1)
                if exists(n, 1, B):
                    r = 1 - u
                    pool.wait_ge(q.inverted, n)
                    pool.tensor_tensor(pr[:, r, :, :], pr[:, r, :, :], sm[:, r, :].unsqueeze(2).broadcast_to([P, G, S]),
                                       ALU.mult).then_inc(q.normed, 1)
                if exists(n, 2, B):
                    if since(n, 4):
                        pool.wait_ge(q.pv_done, n - 3)
                        pool.sem_inc(q.held)
                    pool.tensor_copy(vst[:, u, :], v_all[:, bass.ds(n - 2, 1), :].rearrange("p b d -> p (b d)")).then_inc(q.v_staged, 1)
            pipeline(pool, B, step)


NE = 8


def route(nc, s, router, bias, gates, softmax, tag):
    with ExitStack() as ctx:
        o = opened(nc, ctx)
        ps = o.ps(tag + "_ps", [P, PAIRS * NE])
        lg = o.sb(tag + "_logits", [P, PAIRS, NE])
        above = o.sb(tag + "_above", [P, PAIRS, NE, NE])
        level = o.sb(tag + "_level", [P, PAIRS, NE, NE])
        chosen = o.sb(tag + "_chosen", [P, PAIRS, NE])
        top = o.sb(tag + "_top", [P, PAIRS])
        val = o.sb(tag + "_val", [P, PAIRS, NE])
        ex = o.sb(tag + "_ex", [P, PAIRS, NE])
        filled, chain_sem, act_in, act_out = (o.sem(f"{tag}_{n}") for n in ("filled", "chain", "act_in", "act_out"))
        block = o.block()
        full = [P, PAIRS, NE, NE]
        wide = [P, PAIRS, NE]

        @block.tensor
        def _(pe):
            for t in range(PAIRS):
                ins = pe.matmul(ps[:, NE * t:NE * t + NE], s.xT[:, P * t:P * t + P], router[:, :], start=True, stop=True)
            ins.then_inc(filled, 1)

        @block.scalar
        def _(act):
            act.wait_ge(act_in, 1)
            act.activation(ex[:, :, :], val[:, :, :], ACT.Exp).then_inc(act_out, 1)
            if not softmax:
                act.wait_ge(act_in, 2)
                act.activation(ex[:, :, :], ex[:, :, :], ACT.Ln).then_inc(act_out, 1)
                act.wait_ge(act_in, 3)
                act.activation(val[:, :, :], val[:, :, :], ACT.Sqrt).then_inc(act_out, 1)

        @block.vector
        def _(dve):
            c = Chain(dve, chain_sem)
            dve.wait_ge(filled, 1)
            logits = ps[:, :].rearrange("p (t e) -> p t e", e=NE)
            if bias is None:
                c(dve.tensor_copy(lg[:, :, :], logits))
            else:
                c(dve.tensor_tensor(lg[:, :, :], logits, bias[:, :].unsqueeze(1).broadcast_to(wide), ALU.add))
            c.wait()
            if softmax:
                c(dve.tensor_reduce(top[:, :], lg[:, :, :], AX.X, ALU.max))
                c.wait()
                dve.tensor_tensor(val[:, :, :], lg[:, :, :], top[:, :].unsqueeze(2).broadcast_to(wide), ALU.subtract).then_inc(act_in, 1)
            else:
                c(dve.tensor_scalar(val[:, :, :], lg[:, :, :], -1.0, None, ALU.mult))
                c.wait()
                dve.tensor_tensor(val[:, :, :], lg[:, :, :], val[:, :, :], ALU.min).then_inc(act_in, 1)
            f = lg[:, :, :].unsqueeze(2).broadcast_to(full)
            e = lg[:, :, :].unsqueeze(3).broadcast_to(full)
            c(dve.tensor_tensor(above[:, :, :, :], f, e, ALU.is_gt))
            c(dve.tensor_tensor(level[:, :, :, :], f, e, ALU.is_equal))
            c.wait()
            lower = s.w["lower"][:, :].unsqueeze(1).broadcast_to([P, PAIRS, NE * NE])
            flat = level[:, :, :, :].rearrange("p t e f -> p t (e f)")
            c(dve.tensor_tensor(flat, flat, lower, ALU.mult))
            c.wait()
            c(dve.tensor_tensor(above[:, :, :, :], above[:, :, :, :], level[:, :, :, :], ALU.add))
            c.wait()
            c(dve.tensor_reduce(chosen[:, :, :], above[:, :, :, :], AX.X, ALU.add))
            c.wait()
            c(dve.tensor_scalar(chosen[:, :, :], chosen[:, :, :], 1.5, None, ALU.is_lt))
            c.wait()
            if softmax:
                dve.wait_ge(act_out, 1)
                c(dve.tensor_tensor(ex[:, :, :], ex[:, :, :], chosen[:, :, :], ALU.mult))
                c.wait()
                c(dve.tensor_reduce(top[:, :], ex[:, :, :], AX.X, ALU.add))
                c.wait()
                c(dve.reciprocal(top[:, :], top[:, :]))
                c.wait()
                c(dve.tensor_tensor(gates[:, :, :], ex[:, :, :], top[:, :].unsqueeze(2).broadcast_to(wide), ALU.mult))
            else:
                dve.wait_ge(act_out, 1)
                dve.tensor_scalar(ex[:, :, :], ex[:, :, :], 1.0, None, ALU.add).then_inc(act_in, 1)
                dve.wait_ge(act_out, 2)
                c(dve.tensor_scalar(val[:, :, :], lg[:, :, :], 0.0, None, ALU.max))
                c.wait()
                dve.tensor_tensor(val[:, :, :], val[:, :, :], ex[:, :, :], ALU.add).then_inc(act_in, 1)
                dve.wait_ge(act_out, 3)
                c(dve.tensor_tensor(gates[:, :, :], val[:, :, :], chosen[:, :, :], ALU.mult))
            c.wait()


def add_gated_bias(nc, s, gates, bias, tag):
    with ExitStack() as ctx:
        o = opened(nc, ctx)
        ps_g = o.ps(tag + "_ps_g", [NE, T])
        ps_y = o.ps(tag + "_ps_y", [P, 4, 512])
        gatesT = o.sb(tag + "_gatesT", [NE, T])
        turned, taken, filled, added = (o.sem(f"{tag}_{n}") for n in ("turned", "taken", "filled", "added"))
        block = o.block()

        @block.tensor
        def _(pe):
            for t in range(PAIRS):
                ins = pe.transpose(ps_g[:, P * t:P * t + P], gates[:, t, :], s.ident[:, :])
            ins.then_inc(turned, 1)
            pe.wait_ge(taken, 1)
            for t in range(PAIRS):
                ins = pe.matmul(ps_y[:, t // 4, D * (t % 4):D * (t % 4) + D], gatesT[:, P * t:P * t + P], bias[:, :],
                                start=True, stop=True)
            ins.then_inc(filled, 1)

        @block.scalar
        def _(act):
            act.wait_ge(turned, 1)
            act.copy(gatesT[:, :], ps_g[:, :]).then_inc(taken, 1)

        @block.vector
        def _(dve):
            dve.wait_ge(filled, 1)
            x = s.x[:, :, :].rearrange("p t d -> p (t d)")
            dve.tensor_tensor(x, x, ps_y[:, :, :].rearrange("p c d -> p (c d)"), ALU.add).then_inc(added, 1)


IT = 4


def experts_0(nc, w, s):
    with ExitStack() as ctx:
        o = opened(nc, ctx)
        gates = o.sb("f0_gates", [P, PAIRS, NE])
        w1 = o.sb("f0_w1_sb", [P, NE, IT * P])
        w2 = o.sb("f0_w2_sb", [P, NE, IT, D])
        weights_loaded = o.sem("f0_weights_loaded")
        with nc.Block() as block:
            @block.sync
            def _(sp):
                sp.dma_start(w1[:, :, :], w["big_f0_w1"].rearrange("e d i -> d e i")).then_inc(weights_loaded, 16)
                sp.dma_start(w2[:, :, :, :], w["big_f0_w2"].rearrange("e (j p) d -> p e j d", p=P)).then_inc(weights_loaded, 16)
                sp.wait_ge(weights_loaded, 32)
        route(nc, s, s.w["f0_wgT"], None, gates, True, "f0r")
        add_gated_bias(nc, s, gates, s.w["f0_b2"], "f0b")
        hid = o.sb("f0_hid", [P, 2, IT, 512])
        ps_h = o.ps("f0_ps_h", [P, 4, 512])
        ps_y = o.ps("f0_ps_y", [P, 2, 512])
        filled, activated, summed, added = (o.sem("f0_" + n) for n in ("filled", "activated", "summed", "added"))
        block = o.block()

        @block.tensor
        def _(pe):
            def hidden(c, e, first):
                n = NE * c + e
                for i in range(IT):
                    if not (first and e == 0):
                        pe.wait_ge(activated, IT * (n - 1) + i + 1)
                    pe.matmul(ps_h[:, i, :], w1[:, e, P * i:P * i + P], s.xT[:, bass.ds(512 * c, 512)],
                              start=True, stop=True).then_inc(filled, 1)

            def output(c, e, first):
                n = NE * c + e
                pe.wait_ge(activated, IT * (n + 1))
                if not (first and e < 2):
                    pe.wait_ge(added, 4 * (n - 1))
                for k in range(4):
                    for i in range(IT):
                        ins = pe.matmul(ps_y[:, e % 2, D * k:D * k + D], hid[:, e % 2, i, P * k:P * k + P], w2[:, e, i, :],
                                        start=(i == 0), stop=(i == IT - 1))
                ins.then_inc(summed, 1)

            def chunk(c, first):
                hidden(c, 0, first)
                for e in range(NE):
                    if e + 1 < NE:
                        hidden(c, e + 1, first)
                    output(c, e, first)
            chunk(0, True)
            with pe.Fori(1, TCH) as c:
                chunk(c, False)

        @block.scalar
        def _(act):
            def chunk(c, first):
                for e in range(NE):
                    n = NE * c + e
                    for i in range(IT):
                        act.wait_ge(filled, IT * n + i + 1)
                        if i == 0 and not (first and e < 2):
                            act.wait_ge(summed, n - 1)
                        act.activation(hid[:, e % 2, i, :], ps_h[:, i, :], ACT.Gelu,
                                       bias=s.w["f0_b1"][:, IT * e + i:IT * e + i + 1]).then_inc(activated, 1)
            chunk(0, True)
            with act.Fori(1, TCH) as c:
                chunk(c, False)

        @block.vector
        def _(dve):
            def chunk(c, first):
                for e in range(NE):
                    n = NE * c + e
                    dve.wait_ge(summed, n + 1)
                    if not (first and e == 0):
                        dve.wait_ge(added, 4 * n)
                    for k in range(4):
                        x = s.x[:, bass.ds(4 * c + k, 1), :].rearrange("p t d -> p (t d)")
                        g = gates[:, bass.ds(4 * c + k, 1), e:e + 1].rearrange("p t e -> p (t e)")
                        dve.scalar_tensor_tensor(out=x, in0=ps_y[:, e % 2, D * k:D * k + D], scalar=g, in1=x,
                                                 op0=ALU.mult, op1=ALU.add).then_inc(added, 1)
            chunk(0, True)
            with dve.Fori(1, TCH) as c:
                chunk(c, False)


KJ = (M // P)
KREST = M - KJ * P


def cross_attention_1(nc, w, s):
    with ExitStack() as ctx:
        o = opened(nc, ctx)
        wqk = o.sb("x1_wqk", [P, C])
        wvo = o.sb("x1_wvo", [C, D])
        qk = o.sb("x1_qk", [C, T])
        with ExitStack() as inner:
            oi = opened(nc, inner)
            ps = oi.ps("x1p_ps", [P, 512])
            ps2 = oi.ps("x1p_ps2", [C, 512])
            ps_q = oi.ps("x1p_ps_q", [C, TCH, 512])
            filled, taken, q_filled, q_taken = (oi.sem("x1p_" + n) for n in ("filled", "taken", "q_filled", "q_taken"))
            block = oi.block()

            @block.tensor
            def _(pe):
                pe.matmul(ps[:, 0:C], s.w["x1_wq"][:, :], s.w["x1_wk"][:, :], start=True, stop=True).then_inc(filled, 1)
                pe.matmul(ps2[:, 0:D], s.w["x1_wv"][:, :], s.w["x1_woT"][:, :], start=True, stop=True).then_inc(filled, 1)
                pe.wait_ge(taken, 1)
                for c in range(TCH):
                    pe.matmul(ps_q[:, c, :], wqk[:, :], s.xT[:, 512 * c:512 * c + 512], start=True, stop=True).then_inc(q_filled, 1)

            @block.vector
            def _(dve):
                dve.wait_ge(filled, 1)
                dve.tensor_copy(wqk[:, :], ps[:, 0:C]).then_inc(taken, 1)
                dve.wait_ge(filled, 2)
                dve.tensor_copy(wvo[:, :], ps2[:, 0:D]).then_inc(taken, 1)
                for c in range(TCH):
                    dve.wait_ge(q_filled, c + 1)
                    dve.tensor_copy(qk[:, 512 * c:512 * c + 512], ps_q[:, c, :]).then_inc(q_taken, 1)

        ctxT = o.sb("x1_ctxT", [C, 2, 2, M])
        ctxN = o.sb("x1_ctx", [P, 2, 2, KJ * C])
        ctxR = o.sb("x1_ctx_rest", [KREST, 2, 2, C])
        qst = o.sb("x1_qst", [C, 2, P])
        pr = o.sb("x1_pr", [P, 2, M])
        prT = o.sb("x1_prT", [P, KJ + 1, P])
        stats = o.sb("x1_stats", [P, 2, MC, 6])
        mom = o.sb("x1_mom", [P, 2, 2])
        tot = o.sb("x1_tot", [P, 2, 2])
        var = o.sb("x1_var", [P, 2])
        power = o.sb("x1_power", [P, 1])
        rstd = o.sb("x1_rstd", [P, 2])
        mx = o.sb("x1_mx", [P, 2])
        nb = o.sb("x1_nb", [P, 2])
        den = o.sb("x1_den", [P, 2])
        o1 = o.sb("x1_o1", [P, C])
        o1T = o.sb("x1_o1T", [C, P])
        ps_s = o.ps("x1_ps_s", [P, MC * 512])
        ps_t = o.ps("x1_ps_t", [P, 2, 512])
        ps_x = o.ps("x1_ps_x", [P, 512])
        ps_o = o.ps("x1_ps_o", [P, 512])
        q = Names(**{n: o.sem("x1_" + n) for n in (
            "held", "set_up", "q_staged", "scored", "stats_ready", "aggregated", "mom_ready", "tot_filled", "tot_taken", "var_neg",
            "var_ready", "rstd_ready", "max_ready", "nb_ready", "probs_ready", "turned", "turned_ready", "pv_done",
            "den_inv", "scaled", "oT_filled", "oT_taken", "y_filled", "added")})
        q.loaded = [o.sem(f"x1_loaded{u}") for u in range(2)]
        block = o.block()
        GROUPS = [(4 * g, min(4 * g + 4, KJ + 1)) for g in range((KJ + 4) // 4)]
        NG = len(GROUPS)

        @block.sync
        def _(sp):
            def step(n, u, i):
                if exists(n, 0, PAIRS):
                    if since(n, 2):
                        sp.wait_ge(q.pv_done, n - 1)
                        sp.sem_inc(q.held)
                    for b in range(2):
                        sp.dma_start(ctxT[:, u, b, :], w["ctxT"][2 * n + b]).then_inc(q.loaded[u], 16)
                        sp.dma_start(ctxN[:, u, b, :], w["ctx"][2 * n + b, 0:KJ * P, :].rearrange("(p j) c -> p (j c)", p=P)).then_inc(q.loaded[u], 16)
                        sp.dma_start(ctxR[:, u, b, :], w["ctx"][2 * n + b, KJ * P:M, :]).then_inc(q.loaded[u], 16)
            pipeline(sp, PAIRS, step)

        @block.tensor
        def _(pe):
            def step(n, u, i):
                r = 1 - u
                if exists(n, 0, PAIRS):
                    pe.wait_ge(q.loaded[u], 96 * (i + 1))
                    pe.wait_ge(q.q_staged, n + 1)
                    if since(n, 1):
                        pe.wait_ge(q.probs_ready, n)
                    pe.sem_inc(q.held)
                    for c in range(MC):
                        for b in range(2):
                            ins = pe.matmul(ps_s[S * b:S * b + S, 512 * c:512 * c + CCOLS[c]], qst[:, u, S * b:S * b + S],
                                            ctxT[:, u, b, 512 * c:512 * c + CCOLS[c]], start=True, stop=True)
                        ins.then_inc(q.scored, 1)
                if exists(n, 1, PAIRS):
                    for g, (j0, j1) in enumerate(GROUPS):
                        if since(n, 2) or g >= 2:
                            pe.wait_ge(q.turned_ready, NG * (n - 1) + g - 1)
                        pe.sem_inc(q.held)
                        for j in range(j0, j1):
                            src = (pr[:, r, 0:KJ * P].rearrange("p (k j) -> p j k", j=KJ)[:, j, :] if j < KJ
                                   else pr[:, r, KJ * P:M])
                            k = P if j < KJ else KREST
                            ins = pe.transpose(ps_t[0:k, g % 2, P * (j - j0):P * (j - j0) + P], src, s.ident[:, :])
                        ins.then_inc(q.turned, 1)
                if exists(n, 0, PAIRS):
                    pe.wait_ge(q.mom_ready, n + 1)
                    if since(n, 2):
                        pe.wait_ge(q.added, n - 1)
                    pe.matmul(ps_x[:, 0:2], s.w["halves"][:, :], mom[:, u, :], start=True, stop=True).then_inc(q.tot_filled, 1)
                if exists(n, 1, PAIRS):
                    pe.wait_ge(q.turned_ready, NG * n)
                    if since(n, 2):
                        pe.wait_ge(q.scaled, n - 1)
                    pe.sem_inc(q.held)
                    for j in range(KJ + 1):
                        for b in range(2):
                            k = P if j < KJ else KREST
                            rhs = ctxN[:, r, b, C * j:C * j + C] if j < KJ else ctxR[:, r, b, :]
                            ins = pe.matmul(ps_o[S * b:S * b + S, 0:C], prT[0:k, j, S * b:S * b + S], rhs,
                                            start=(j == 0), stop=(j == KJ))
                    ins.then_inc(q.pv_done, 1)
                    pe.wait_ge(q.scaled, n)
                    if exists(n, 0, PAIRS):
                        pe.wait_ge(q.tot_taken, n + 1)
                    pe.sem_inc(q.held)
                    pe.transpose(ps_x[0:C, 0:P], o1[:, :], s.ident[:, :]).then_inc(q.oT_filled, 1)
                    pe.wait_ge(q.oT_taken, n)
                    pe.matmul(ps_x[:, 0:D], o1T[:, :], wvo[:, :], start=True, stop=True).then_inc(q.y_filled, 1)
            pipeline(pe, PAIRS, step)

        @block.vector
        def _(dve):
            dve.memset(power[:, :], -0.5).then_inc(q.set_up, 1)

            def step(n, u, i):
                r = 1 - u
                if exists(n, 0, PAIRS):
                    for c in range(MC):
                        dve.wait_ge(q.scored, MC * n + c + 1)
                        dve.bn_stats(stats[:, u, c, :], ps_s[:, 512 * c:512 * c + CCOLS[c]]).then_inc(q.stats_ready, 1)
                    dve.wait_ge(q.stats_ready, MC * (n + 1))
                    dve.sem_inc(q.held)
                    dve.bn_aggr(mom[:, u, :], stats[:, u, :, :]).then_inc(q.aggregated, 1)
                    dve.wait_ge(q.aggregated, n + 1)
                    dve.scalar_tensor_tensor(out=mom[:, u, 1:2], in0=mom[:, u, 0:1], scalar=mom[:, u, 0:1], in1=mom[:, u, 1:2],
                                             op0=ALU.mult, op1=ALU.add).then_inc(q.mom_ready, 1)
                    dve.tensor_reduce(mx[:, u:u + 1], ps_s[:, 0:M], AX.X, ALU.max).then_inc(q.max_ready, 1)
                    dve.wait_ge(q.tot_filled, n + 1)
                    dve.tensor_copy(tot[:, u, :], ps_x[:, 0:2]).then_inc(q.tot_taken, 1)
                    dve.wait_ge(q.tot_taken, n + 1)
                    dve.scalar_tensor_tensor(out=var[:, u:u + 1], in0=tot[:, u, 0:1], scalar=tot[:, u, 0:1], in1=tot[:, u, 1:2],
                                             op0=ALU.mult, op1=ALU.subtract).then_inc(q.var_neg, 1)
                    dve.wait_ge(q.var_neg, n + 1)
                    dve.tensor_scalar(var[:, u:u + 1], var[:, u:u + 1], -1.0, EPS, ALU.mult, ALU.add).then_inc(q.var_ready, 1)
                    dve.wait_ge(q.rstd_ready, n + 1)
                    dve.wait_ge(q.max_ready, n + 1)
                    dve.scalar_tensor_tensor(out=nb[:, u:u + 1], in0=mx[:, u:u + 1], scalar=-1.0, in1=rstd[:, u:u + 1],
                                             op0=ALU.mult, op1=ALU.mult).then_inc(q.nb_ready, 1)
                if exists(n, 1, PAIRS):
                    dve.wait_ge(q.probs_ready, n)
                    dve.reciprocal(den[:, r:r + 1], den[:, r:r + 1]).then_inc(q.den_inv, 1)
                    dve.wait_ge(q.den_inv, n)
                    dve.wait_ge(q.pv_done, n)
                    if since(n, 2):
                        dve.wait_ge(q.oT_filled, n - 1)
                    dve.tensor_scalar(o1[:, :], ps_o[:, 0:C], den[:, r:r + 1], None, ALU.mult).then_inc(q.scaled, 1)
                    dve.wait_ge(q.y_filled, n)
                    x = s.x[:, bass.ds(n - 1, 1), :].rearrange("p t d -> p (t d)")
                    dve.tensor_tensor(x, x, ps_x[:, 0:D], ALU.add).then_inc(q.added, 1)
            pipeline(dve, PAIRS, step)

        @block.scalar
        def _(act):
            def step(n, u, i):
                if exists(n, 1, PAIRS):
                    for g, (j0, j1) in enumerate(GROUPS):
                        k = P if g < NG - 1 else KREST
                        act.wait_ge(q.turned, NG * (n - 1) + g + 1)
                        if g == 0 and since(n, 2):
                            act.wait_ge(q.pv_done, n - 1)
                        act.copy(prT[0:k, j0:j1, :].rearrange("p j k -> p (j k)"), ps_t[0:k, g % 2, 0:P * (j1 - j0)]).then_inc(q.turned_ready, 1)
                if exists(n, 0, PAIRS):
                    act.wait_ge(q.nb_ready, n + 1)
                    if since(n, 2):
                        act.wait_ge(q.scaled, n - 1)
                    act.activation(pr[:, u, :], ps_s[:, 0:M], ACT.Exp, scale=rstd[:, u:u + 1], bias=nb[:, u:u + 1],
                                   accum_out=den[:, u:u + 1]).then_inc(q.probs_ready, 1)
                if exists(n, 1, PAIRS):
                    act.wait_ge(q.oT_filled, n)
                    act.copy(o1T[:, :], ps_x[0:C, 0:P]).then_inc(q.oT_taken, 1)
            pipeline(act, PAIRS, step)

        @block.gpsimd
        def _(pool):
            pool.wait_ge(q.set_up, 1)

            def step(n, u, i):
                if exists(n, 0, PAIRS):
                    if since(n, 2):
                        pool.wait_ge(q.scored, MC * (n - 1))
                        pool.sem_inc(q.held)
                    pool.tensor_copy(qst[:, u, :], qk[:, bass.ds(P * n, P)]).then_inc(q.q_staged, 1)
                    pool.wait_ge(q.var_ready, n + 1)
                    pool.tensor_tensor(rstd[:, u:u + 1], var[:, u:u + 1], power[:, :], ALU.pow).then_inc(q.rstd_ready, 1)
            pipeline(pool, PAIRS, step)


NS = 16
HF = 2


def state_space_1(nc, w, s):
    with ExitStack() as ctx:
        o = opened(nc, ctx)
        u = o.sb("s1_u", [P, HF, B, S])
        kern = o.sb("s1_kern", [P, HF, S])
        with ExitStack() as inner:
            oi = opened(nc, inner)
            g = oi.sb("s1_g", [P, HF, B, S])
            dt_sums = oi.sb("s1_dt_sums", [P, HF, 2 * TCH])
            project_states_1(nc, s, u, g, dt_sums)
            gate_states_1(nc, s, u, g)
            make_kernel_1(nc, s, dt_sums, kern)
        y = o.sb("s1_y", [P, HF, B, S])
        convolve_1(nc, s, u, kern, y)
        project_out_1(nc, s, y)


def project_states_1(nc, s, u, g, dt_sums):
    with ExitStack() as ctx:
        o = opened(nc, ctx)
        z = o.sb("s1_z", [P, HF, TCH, 512])
        ps = o.ps("s1_ps", [P, 6, 512])
        filled, u_taken, g_taken, z_taken, relu_taken, abs_ready, exp_ready, ln_ready = (
            o.sem("s1a_" + n) for n in ("filled", "u_taken", "g_taken", "z_taken", "relu_taken", "abs_ready", "exp_ready", "ln_ready"))
        jobs = [(h, c) for h in range(HF) for c in range(TCH)]
        block = o.block()

        @block.tensor
        def _(pe):
            for n, (h, c) in enumerate(jobs):
                for k, name in enumerate(("s1_wxT", "s1_wgT", "s1_wdtT")):
                    if n >= 2:
                        for done in ((u_taken,), (g_taken,), (z_taken, relu_taken))[k]:
                            pe.wait_ge(done, n - 1)
                    pe.matmul(ps[:, 3 * (n % 2) + k, :], s.w[name][:, P * h:P * h + P], s.xT[:, 512 * c:512 * c + 512],
                              start=True, stop=True).then_inc(filled, 1)

        @block.vector
        def _(dve):
            for n, (h, c) in enumerate(jobs):
                dve.wait_ge(filled, 3 * n + 1)
                dve.tensor_scalar(u[:, h, 8 * c:8 * c + 8, :].rearrange("p b s -> p (b s)"), ps[:, 3 * (n % 2), :],
                                  s.w["s1_bx"][:, h:h + 1], None, ALU.add).then_inc(u_taken, 1)
                dve.wait_ge(relu_taken, n + 1)
                dve.tensor_scalar(z[:, h, c, :], ps[:, 3 * (n % 2) + 2, :], s.w["s1_bdt"][:, h:h + 1], None, ALU.add).then_inc(z_taken, 1)
                dve.wait_ge(z_taken, n + 1)
                dve.scalar_tensor_tensor(out=z[:, h, c, :], in0=z[:, h, c, :], scalar=-1.0, in1=z[:, h, c, :], op0=ALU.mult, op1=ALU.min).then_inc(abs_ready, 1)

        @block.scalar
        def _(act):
            spare = o.sb("s1_spare", [P, 512])
            for n, (h, c) in enumerate(jobs):
                act.wait_ge(filled, 3 * n + 2)
                act.activation(g[:, h, 8 * c:8 * c + 8, :].rearrange("p b s -> p (b s)"), ps[:, 3 * (n % 2) + 1, :], ACT.Sigmoid,
                               bias=s.w["s1_bg"][:, h:h + 1]).then_inc(g_taken, 1)
                act.wait_ge(filled, 3 * n + 3)
                if n:
                    act.wait_ge(relu_taken, n)
                act.activation(spare[:, :], ps[:, 3 * (n % 2) + 2, :], ACT.Relu, bias=s.w["s1_bdt"][:, h:h + 1],
                               accum_out=dt_sums[:, h, c:c + 1]).then_inc(relu_taken, 1)
            for n, (h, c) in enumerate(jobs):
                act.wait_ge(abs_ready, n + 1)
                act.activation(z[:, h, c, :], z[:, h, c, :], ACT.Exp).then_inc(exp_ready, 1)
            for n, (h, c) in enumerate(jobs):
                act.wait_ge(exp_ready, n + 1)
                act.activation(z[:, h, c, :], z[:, h, c, :], ACT.Ln, bias=s.ones[:, 0:1],
                               accum_out=dt_sums[:, h, TCH + c:TCH + c + 1]).then_inc(ln_ready, 1)


def gate_states_1(nc, s, u, g):
    with ExitStack() as ctx:
        o = opened(nc, ctx)
        hc = o.sb("s1_hc", [P, HF, B, S])
        chain_sem = o.sem("s1b_chain")
        block = o.block()

        @block.vector
        def _(dve):
            chain = Chain(dve, chain_sem)
            both = range(HF)
            cw = s.w["s1_cw"]
            for h in both:
                chain(dve.tensor_scalar(hc[:, h, :, :], u[:, h, :, :], cw[:, 3 * h + 1:3 * h + 2], s.w["s1_cb"][:, h:h + 1],
                                        ALU.mult, ALU.add))
            for tap, dst, src in ((0, slice(1, S), slice(0, S - 1)), (2, slice(0, S - 1), slice(1, S))):
                chain.wait()
                for h in both:
                    chain(dve.scalar_tensor_tensor(out=hc[:, h, :, dst], in0=u[:, h, :, src], scalar=cw[:, 3 * h + tap:3 * h + tap + 1],
                                                   in1=hc[:, h, :, dst], op0=ALU.mult, op1=ALU.add))
            for h in both:
                chain.wait()
                chain(dve.tensor_tensor(u[:, h, :, :], u[:, h, :, :], hc[:, h, :, :], ALU.subtract))
                chain.wait()
                chain(dve.tensor_tensor(u[:, h, :, :], u[:, h, :, :], g[:, h, :, :], ALU.mult))
                chain.wait()
                chain(dve.tensor_tensor(u[:, h, :, :], u[:, h, :, :], hc[:, h, :, :], ALU.add))
            chain.wait()


def make_kernel_1(nc, s, dt_sums, kern):
    with ExitStack() as ctx:
        o = opened(nc, ctx)
        a = o.sb("s1_a", [P, HF, NS])
        e = o.sb("s1_e", [P, HF, NS])
        dt = o.sb("s1_dt", [P, HF])
        adt = o.sb("s1_adt", [P, HF, NS])
        cb = o.sb("s1_cbd", [P, HF, NS])
        powers = o.sb("s1_powers", [P, HF, S, NS])
        chain_sem, act_in, act_out = (o.sem("s1c_" + n) for n in ("chain", "act_in", "act_out"))
        block = o.block()
        wide = [P, HF, NS]
        raw = s.w["s1_araw"][:, :].rearrange("p (h n) -> p h n", h=HF)

        @block.scalar
        def _(act):
            act.wait_ge(act_in, 1)
            act.activation(e[:, :, :], e[:, :, :], ACT.Exp).then_inc(act_out, 1)
            act.wait_ge(act_out, 1)
            act.activation(e[:, :, :], e[:, :, :], ACT.Ln, bias=s.ones[:, 0:1]).then_inc(act_out, 1)
            act.wait_ge(act_in, 2)
            act.activation(e[:, :, :], adt[:, :, :], ACT.Exp).then_inc(act_out, 1)
            act.wait_ge(act_in, 3)
            act.activation(powers[:, :, :, :], powers[:, :, :, :], ACT.Exp).then_inc(act_out, 1)

        @block.vector
        def _(dve):
            c = Chain(dve, chain_sem)
            dve.scalar_tensor_tensor(out=e[:, :, :], in0=raw, scalar=-1.0, in1=raw, op0=ALU.mult, op1=ALU.min).then_inc(act_in, 1)
            c(dve.tensor_reduce(dt[:, :], dt_sums[:, :, :], AX.X, ALU.add))
            c.wait()
            c(dve.tensor_scalar(dt[:, :], dt[:, :], 1.0 / T, None, ALU.mult))
            c.wait()
            c(dve.tensor_scalar(dt[:, :], dt[:, :], 0.001, 2.0, ALU.max, ALU.min))
            c(dve.tensor_scalar(a[:, :, :], raw, 0.0, None, ALU.max))
            c.wait()
            dve.wait_ge(act_out, 2)
            c(dve.tensor_tensor(a[:, :, :], a[:, :, :], e[:, :, :], ALU.add))
            c.wait()
            c(dve.tensor_scalar(a[:, :, :], a[:, :, :], -1.0, None, ALU.mult))
            c.wait()
            dve.tensor_tensor(adt[:, :, :], a[:, :, :], dt[:, :].unsqueeze(2).broadcast_to(wide), ALU.mult).then_inc(act_in, 1)
            dve.wait_ge(act_in, 2)
            for h in range(HF):
                ins = dve.tensor_tensor(powers[:, h, :, :], adt[:, h, :].unsqueeze(1).broadcast_to([P, S, NS]),
                                        s.w["s1_k"][:, :].unsqueeze(2).broadcast_to([P, S, NS]), ALU.mult)
                if h == 0:
                    c(ins)
            ins.then_inc(act_in, 1)
            c(dve.tensor_scalar(a[:, :, :], a[:, :, :], 1e-6, None, ALU.add))
            c.wait()
            c(dve.reciprocal(a[:, :, :], a[:, :, :]))
            c.wait()
            dve.wait_ge(act_out, 3)
            c(dve.tensor_scalar(cb[:, :, :], e[:, :, :], -1.0, None, ALU.add))
            c.wait()
            for factor in (a[:, :, :], s.w["s1_b"][:, :].rearrange("p (h n) -> p h n", h=HF),
                           s.w["s1_c"][:, :].rearrange("p (h n) -> p h n", h=HF)):
                c(dve.tensor_tensor(cb[:, :, :], cb[:, :, :], factor, ALU.mult))
                c.wait()
            dve.wait_ge(act_out, 4)
            for h in range(HF):
                c(dve.tensor_tensor(powers[:, h, :, :], powers[:, h, :, :], cb[:, h, :].unsqueeze(1).broadcast_to([P, S, NS]), ALU.mult))
            c.wait()
            for h in range(HF):
                c(dve.tensor_reduce(kern[:, h, :], powers[:, h, :, :], AX.X, ALU.add))
            c.wait()


def convolve_1(nc, s, u, kern, y):
    with ExitStack() as ctx:
        o = opened(nc, ctx)
        done = [o.sem(f"s1d_done{h}") for h in range(HF)]
        block = o.block()

        @block.vector
        def _(dve):
            for k in range(S):
                for h in range(HF):
                    if k == 0:
                        dve.tensor_scalar(y[:, h, :, :], u[:, h, :, :], kern[:, h, 0:1], None, ALU.mult).then_inc(done[h], 1)
                    else:
                        dve.wait_ge(done[h], k)
                        dve.scalar_tensor_tensor(out=y[:, h, :, k:S], in0=u[:, h, :, 0:S - k], scalar=kern[:, h, k:k + 1],
                                                 in1=y[:, h, :, k:S], op0=ALU.mult, op1=ALU.add).then_inc(done[h], 1)


def project_out_1(nc, s, y):
    with ExitStack() as ctx:
        o = opened(nc, ctx)
        ps = o.ps("s1_ps_out", [P, PAIRS, D])
        r = o.sb("s1_r", [P, PAIRS, D])
        stats = o.sb("s1_stats", [P, PAIRS, 6])
        mom = o.sb("s1_mom", [P, PAIRS, 2])
        std = o.sb("s1_std", [P, PAIRS])
        filled, chain_sem, mom_ready, std_ready = (o.sem("s1e_" + n) for n in ("filled", "chain", "mom_ready", "std_ready"))
        block = o.block()
        wide = [P, PAIRS, D]

        @block.tensor
        def _(pe):
            for t in range(PAIRS):
                for h in range(HF):
                    ins = pe.matmul(ps[:, t, :], y[:, h, 2 * t:2 * t + 2, :].rearrange("p b s -> p (b s)"),
                                    s.w["s1_woT"][:, D * h:D * h + D], start=(h == 0), stop=(h == HF - 1))
            ins.then_inc(filled, 1)

        @block.scalar
        def _(act):
            act.wait_ge(mom_ready, PAIRS)
            act.activation(std[:, :], mom[:, :, 1], ACT.Sqrt, bias=s.eps[:, 0:1]).then_inc(std_ready, 1)

        @block.vector
        def _(dve):
            c = Chain(dve, chain_sem)
            dve.wait_ge(filled, 1)
            c(dve.tensor_tensor(r[:, :, :], s.xn[:, :, :], ps[:, :, :], ALU.add))
            c.wait()
            c(dve.tensor_tensor(r[:, :, :], r[:, :, :], s.w["s1_bout"][:, :].unsqueeze(1).broadcast_to(wide), ALU.add))
            c.wait()
            for t in range(PAIRS):
                c(dve.bn_stats(stats[:, t, :], r[:, t, :]))
            c.wait()
            for t in range(PAIRS):
                dve.bn_aggr(mom[:, t, :], stats[:, t, :]).then_inc(mom_ready, 1)
            dve.wait_ge(std_ready, 1)
            c(dve.reciprocal(std[:, :], std[:, :]))
            c.wait()
            for t in range(PAIRS):
                c(dve.tensor_scalar(r[:, t, :], r[:, t, :], mom[:, t, 0:1], std[:, t:t + 1], ALU.subtract, ALU.mult))
            c.wait()
            c(dve.tensor_tensor(r[:, :, :], r[:, :, :], s.w["s1_g"][:, :].unsqueeze(1).broadcast_to(wide), ALU.mult))
            c.wait()
            c(dve.tensor_tensor(r[:, :, :], r[:, :, :], s.w["s1_lb"][:, :].unsqueeze(1).broadcast_to(wide), ALU.add))
            c.wait()
            c(dve.tensor_tensor(s.x[:, :, :], s.x[:, :, :], r[:, :, :], ALU.add))
            c.wait()


HE = 64


def experts_1(nc, w, s):
    with ExitStack() as ctx:
        o = opened(nc, ctx)
        gates = o.sb("f1_gates", [P, PAIRS, NE])
        route(nc, s, s.w["f1_wrT"], s.w["f1_eb"], gates, False, "f1r")
        add_gated_bias(nc, s, gates, s.w["f1_rb2"], "f1b")
        hid = o.sb("f1_hid", [P, 2, 512])
        ps_h = o.ps("f1_ps_h", [P, 2, 512])
        ps_y = o.ps("f1_ps_y", [P, 2, 2, 512])
        q = Names(**{n: o.sem("f1_" + n) for n in ("held", "biased", "filled", "activated", "summed", "added")})
        UNITS = NE // 2 + 1
        block = o.block()

        def unit(n):
            return (s.w["f1_rw1"][:, P * n:P * n + P], n, P, 2) if n < UNITS - 1 else (s.w["f1_sw1"][:, :], n, HE, 1)

        @block.tensor
        def _(pe):
            def hidden(c, n):
                w1, _, rows, _ = unit(n % UNITS)
                if n >= 2:
                    pe.wait_ge(q.activated, n - 1)
                pe.matmul(ps_h[0:rows, n % 2, :], w1, s.xT[:, 512 * c:512 * c + 512], start=True, stop=True).then_inc(q.filled, 1)

            def output(c, n):
                _, m, _, experts = unit(n % UNITS)
                pe.wait_ge(q.activated, n + 1)
                if n >= 2:
                    pe.wait_ge(q.added, n - 1)
                for a in range(experts):
                    for k in range(4):
                        w2 = s.w["f1_rw2"][HE * a:HE * a + HE, D * m:D * m + D] if m < UNITS - 1 else s.w["f1_sw2"][:, :]
                        ins = pe.matmul(ps_y[:, n % 2, a, D * k:D * k + D], hid[HE * a:HE * a + HE, n % 2, P * k:P * k + P], w2,
                                        start=True, stop=True)
                ins.then_inc(q.summed, 1)

            total = TCH * UNITS
            hidden(0, 0)
            for n in range(total):
                if n + 1 < total:
                    hidden((n + 1) // UNITS, n + 1)
                output(n // UNITS, n)

        @block.scalar
        def _(act):
            for n in range(TCH * UNITS):
                _, m, rows, _ = unit(n % UNITS)
                act.wait_ge(q.filled, n + 1)
                if n >= 2:
                    act.wait_ge(q.summed, n - 1)
                act.activation(hid[0:rows, n % 2, :], ps_h[0:rows, n % 2, :], ACT.Silu, bias=s.w["f1_b1"][0:rows, m:m + 1]).then_inc(q.activated, 1)

        @block.vector
        def _(dve):
            x = s.x[:, :, :]
            dve.tensor_tensor(x, x, s.w["f1_sb2"][:, :].unsqueeze(1).broadcast_to([P, PAIRS, D]), ALU.add).then_inc(q.biased, 1)
            dve.wait_ge(q.biased, 1)
            for n in range(TCH * UNITS):
                c = n // UNITS
                _, m, _, experts = unit(n % UNITS)
                dve.wait_ge(q.summed, n + 1)
                if n:
                    dve.wait_ge(q.added, n)
                if experts == 1:
                    xs = s.x[:, 4 * c:4 * c + 4, :].rearrange("p t d -> p (t d)")
                    dve.tensor_tensor(xs, xs, ps_y[:, n % 2, 0, :], ALU.add).then_inc(q.added, 1)
                    continue
                for a in range(2):
                    for k in range(4):
                        xs = s.x[:, 4 * c + k, :]
                        ins = dve.scalar_tensor_tensor(out=xs, in0=ps_y[:, n % 2, a, D * k:D * k + D],
                                                       scalar=gates[:, 4 * c + k, 2 * m + a:2 * m + a + 1], in1=xs,
                                                       op0=ALU.mult, op1=ALU.add)
                        if a == 0:
                            ins.then_inc(q.held, 1)
                    if a == 0:
                        dve.wait_ge(q.held, 4 * (n - c + 1))
                ins.then_inc(q.added, 1)


def clear_semaphores(nc, first):
    with nc.semaphore("past_layer") as last, nc.Block() as block:
        @block.gpsimd
        def _(pool):
            pool.sem_clear(range(first.num, last.num + 1))


def program(nc, w):
    with ExitStack() as ctx:
        o = opened(nc, ctx)
        s = Names()
        s.x = o.sb("x", [P, PAIRS, D])
        s.xn = o.sb("xn", [P, PAIRS, D])
        s.xT = o.sb("xT", [P, T])
        s.ident = o.sb("ident", [P, P])
        s.ident_b = o.sb("ident_b", [P, P], BF16)
        s.ones = o.sb("ones", [P, P])
        s.eps = o.sb("eps", [P, 1])
        s.x_biased, s.x_biased_count = o.sem("x_biased"), 0
        s.w = {n: o.sb("w_" + n, list(w[n].shape)) for n in WEIGHTS if n in w}
        with nc.semaphore("of_layer") as first:
            pass
        load_all(nc, w, s)
        layer_norm(nc, s, "n0")
        cross_attention_0(nc, w, s)
        layer_norm(nc, s, "n1")
        self_attention_0(nc, w, s)
        layer_norm(nc, s, "n2")
        experts_0(nc, w, s)
        clear_semaphores(nc, first)
        layer_norm(nc, s, "n3")
        cross_attention_1(nc, w, s)
        layer_norm(nc, s, "n4")
        state_space_1(nc, w, s)
        layer_norm(nc, s, "n5")
        experts_1(nc, w, s)
        stored = o.sem("stored")
        with nc.Block() as block:
            @block.sync
            def _(sp):
                sp.dma_start(w["out"].rearrange("(t p) d -> p t d", p=P), s.x[:, :, :]).then_inc(stored, 16)
                sp.wait_ge(stored, 16)


def kernel(**inputs):
    import numpy as _np
    import concourse.bacc as _bacc
    from concourse import mybir as _mybir
    from concourse.bass_utils import run_bass_kernel_spmd as _run

    a = {n: _np.asarray(v) for n, v in inputs.items()}
    pair_order = _np.arange(D).reshape(G, 2 * HD).T.reshape(-1)
    swapped = _np.arange(D) ^ 1
    inv_freq = 1.0 / 10000.0 ** (_np.arange(HD // 2, dtype=_np.float32) / (HD // 2))
    angle = _np.arange(S, dtype=_np.float32)[None, :] * inv_freq.astype(_np.float32)[_np.arange(D) % HD // 2][:, None]
    cos = _np.cos(angle).astype(_np.float32)
    sin = (_np.sin(angle) * _np.where(_np.arange(D) % 2, 1.0, -1.0)[:, None]).astype(_np.float32)
    causal = _np.where(_np.arange(S)[None, :] <= (_np.arange(P) % S)[:, None], 0.0, MASKED).astype(_np.float32)
    heads = (_np.arange(D)[:, None] // HD == _np.arange(H)[None, :]).astype(_np.float32)
    lower = _np.tri(NE, k=-1, dtype=_np.float32).reshape(-1)

    def rows(v):
        return _np.broadcast_to(v, (P, *v.shape))

    def by_half(v):
        return v.reshape(HF, P, -1).transpose(1, 0, 2).reshape(P, -1)

    halves = (_np.arange(P)[:, None] // S == _np.arange(P)[None, :] // S).astype(_np.float32) / S
    b1 = _np.concatenate([a["L1_ffn_rb1"].reshape(NE // 2, 2 * HE).T, _np.tile(a["L1_ffn_sb1"], 2)[:, None]], axis=1)

    laid = {
        "x": a["x"].reshape(T, D),
        "ctxT": a["ctx_768"].transpose(0, 2, 1),
        "mask": a["mask_BxS2_bf1"].view(_np.uint8),
        "x0_wq": a["L0_xattn_Wq"][:, pair_order],
        "x0_wk": a["L0_xattn_Wk"][:, pair_order],
        "x0_wv": a["L0_xattn_Wv"],
        "x0_wo": a["L0_xattn_Wo"],
        "a0_wqT": a["L0_attn_Wq"].T,
        "a0_wqT_sw": a["L0_attn_Wq"][swapped].T,
        "a0_wkT": a["L0_attn_Wk"].T,
        "a0_wkT_sw": a["L0_attn_Wk"][swapped].T,
        "a0_wvT": a["L0_attn_Wv"].T,
        "a0_woT": a["L0_attn_Wo"].T,
        "a0_bq": a["L0_attn_bq"][:, None],
        "a0_bq_sw": a["L0_attn_bq"][swapped][:, None],
        "a0_bk": a["L0_attn_bk"][:, None],
        "a0_bk_sw": a["L0_attn_bk"][swapped][:, None],
        "a0_bv": rows(a["L0_attn_bv"]),
        "a0_bo": rows(a["L0_attn_bo"]),
        "a0_cos": cos,
        "a0_sin": sin,
        "a0_causal": causal,
        "a0_heads": heads,
        "lower": rows(lower),
        "f0_wgT": a["L0_ffn_Wg"].T,
        "f0_b1": a["L0_ffn_b1"].reshape(NE * IT, P).T,
        "f0_b2": a["L0_ffn_b2"],
        "big_f0_w1": a["L0_ffn_W1"],
        "big_f0_w2": a["L0_ffn_W2"],
        "ctx": a["ctx_768"],
        "halves": halves,
        "x1_wq": a["L1_xattn_Wq"],
        "x1_wk": a["L1_xattn_Wk"],
        "x1_wv": a["L1_xattn_Wv"],
        "x1_woT": a["L1_xattn_Wo"].T,
        "s1_wxT": a["L1_attn_W_x"].T,
        "s1_wgT": a["L1_attn_W_g"].T,
        "s1_wdtT": a["L1_attn_W_dt"].T,
        "s1_bx": by_half(a["L1_attn_b_x"][:, None]),
        "s1_bg": by_half(a["L1_attn_b_g"][:, None]),
        "s1_bdt": by_half(a["L1_attn_b_dt"][:, None]),
        "s1_cw": by_half(a["L1_attn_conv_w"][:, 0, :]),
        "s1_cb": by_half(a["L1_attn_conv_b"][:, None]),
        "s1_araw": by_half(a["L1_attn_A_raw"]),
        "s1_b": by_half(a["L1_attn_B_ssm"]),
        "s1_c": by_half(a["L1_attn_C_ssm"]),
        "s1_k": rows(_np.arange(S, dtype=_np.float32)),
        "s1_woT": by_half(a["L1_attn_W_out"].T),
        "s1_bout": rows(a["L1_attn_b_out"]),
        "s1_g": rows(a["L1_attn_ln_g"]),
        "s1_lb": rows(a["L1_attn_ln_b"]),
        "f1_wrT": a["L1_ffn_routing_W"].T,
        "f1_eb": rows(a["L1_ffn_expert_bias"]),
        "f1_rw1": a["L1_ffn_rW1"].transpose(1, 0, 2).reshape(D, NE * HE),
        "f1_sw1": a["L1_ffn_sW1"],
        "f1_b1": b1,
        "f1_rw2": a["L1_ffn_rW2"].reshape(NE // 2, 2 * HE, D).transpose(1, 0, 2).reshape(2 * HE, NE // 2 * D),
        "f1_sw2": a["L1_ffn_sW2"],
        "f1_sb2": rows(a["L1_ffn_sb2"]),
        "f1_rb2": a["L1_ffn_rb2"],
    }
    nc = _bacc.Bacc("TRN2", target_bir_lowering=False, num_devices=1)
    arrays, w = {}, {}
    for name, v in laid.items():
        v = _np.ascontiguousarray(v)
        arrays[f"in_{name}"] = v
        w[name] = nc.dram_tensor(f"in_{name}", v.shape, _mybir.dt.from_np(v.dtype), kind="ExternalInput").ap()
    w["mask_bias"] = nc.dram_tensor("mask_bias_rows", (B, M), _mybir.dt.bfloat16, kind="Internal").ap()
    w["out"] = nc.dram_tensor("out_x", (T, D), _mybir.dt.float32, kind="ExternalOutput").ap()
    program(nc, w)
    r = _run(nc, [arrays], core_ids=[0])
    return r.results[0]["out_x"].reshape(B, S, D)
```

```python
from contextlib import ExitStack

import concourse.bass as bass
from concourse import mybir
import numpy as np

F32 = mybir.dt.float32
BF16 = mybir.dt.bfloat16
U8 = mybir.dt.uint8
ACT = mybir.ActivationFunctionType
ALU = mybir.AluOpType
AX = mybir.AxisListType

P = 128
B, S, D = 32, 64, 128
M, C = 1601, 96
H, HD = 16, 8
PAIRS = B // 2
T = B * S
TCH = T // 512
KT = (M + P - 1) // P
KROWS = [min(P, M - P * j) for j in range(KT)]
MC = (M + 511) // 512
CCOLS = [min(512, M - 512 * c) for c in range(MC)]
G = H // 2
MASKED = -3.0e38
EPS = 1e-5
K_PARTS = (0, 0, 0, 1, 1, 2)
Q_PARTS = (0, 1, 2, 0, 1, 0)
TERMS = len(K_PARTS)
GH = TERMS * 2 * HD
MROW = GH
SROWS = GH + 4


class Names(dict):
    def __getattr__(self, name):
        return self[name]

    def __setattr__(self, name, thing):
        self[name] = thing


WEIGHTS = (
    "x0_wq",
    "x0_wk",
    "x0_wv",
    "x0_wo",
    "x0_own_head",
    "a0_wqT",
    "a0_wqT_sw",
    "a0_wkT",
    "a0_wkT_sw",
    "a0_wvT",
    "a0_woT",
    "a0_bq",
    "a0_bq_sw",
    "a0_bk",
    "a0_bk_sw",
    "a0_bv",
    "a0_bo",
    "a0_cos",
    "a0_sin",
    "a0_causal",
    "a0_heads",
    "lower",
    "f0_wgT",
    "f0_b1",
    "f0_b2",
    "halves",
    "x1_wq",
    "x1_wk",
    "x1_wv",
    "x1_woT",
    "s1_wxT",
    "s1_wgT",
    "s1_wdtT",
    "s1_bx",
    "s1_bg",
    "s1_bdt",
    "s1_cw",
    "s1_cb",
    "s1_araw",
    "s1_b",
    "s1_c",
    "s1_k",
    "s1_woT",
    "s1_bout",
    "s1_g",
    "s1_lb",
    "f1_wrT",
    "f1_eb",
    "f1_rw1",
    "f1_sw1",
    "f1_b1",
    "f1_rw2",
    "f1_sw2",
    "f1_sb2",
    "f1_rb2",
)


def opened(nc, ctx):
    return Names(
        sb=lambda name, shape, dt=F32: ctx.enter_context(nc.sbuf_tensor(name, shape, dt)),
        ps=lambda name, shape, dt=F32: ctx.enter_context(nc.psum_tensor(name, shape, dt)),
        sem=lambda name: ctx.enter_context(nc.semaphore(name)),
        block=lambda: ctx.enter_context(nc.Block()),
    )


def hold(eng, sem):
    eng.sem_inc(sem)


def load_first(nc, w, s):
    with ExitStack() as ctx:
        o = opened(nc, ctx)
        loads = [
            (s.x[:, :, :], w["x"].rearrange("(t p) d -> p t d", p=P)),
        ] + [(s.w[name][:, :], w[name]) for name in s.w if name.startswith("x0_")]
        mask_u8 = o.sb("mask_u8", [B, M], U8)
        mask_bias = o.sb("mask_bias", [B, M], BF16)
        zero_f = o.sb("zero_f", [P, P])
        loaded, mask_loaded, mask_ready, mask_stored = o.sem("loaded"), o.sem("mask_loaded"), o.sem("mask_ready"), o.sem("mask_stored")
        zeroed, made = o.sem("zeroed"), o.sem("made")
        block = o.block()

        @block.sync
        def _(sp):
            sp.dma_start(mask_u8[:, :], w["mask"]).then_inc(mask_loaded, 16)
            for dst, src in loads:
                sp.dma_start(dst, src).then_inc(loaded, 16)
            sp.wait_ge(mask_ready, 1)
            sp.dma_start(w["mask_bias"], mask_bias[:, :]).then_inc(mask_stored, 16)
            sp.wait_ge(mask_stored, 16)
            sp.wait_ge(loaded, 16 * len(loads))

        @block.vector
        def _(dve):
            dve.memset(zero_f[:, :], 0.0).then_inc(zeroed, 1)
            dve.memset(s.ones[:, :], 1.0).then_inc(zeroed, 1)
            dve.memset(s.eps[:, :], EPS).then_inc(zeroed, 1)
            dve.wait_ge(mask_loaded, 16)
            dve.tensor_scalar(mask_bias[:, :], mask_u8[:, :], -MASKED, MASKED, ALU.mult, ALU.add).then_inc(mask_ready, 1)
            dve.wait_ge(made, 1)
            dve.tensor_copy(s.ident_b[:, :], s.ident[:, :]).then_inc(made, 1)

        @block.gpsimd
        def _(pool):
            pool.wait_ge(zeroed, 1)
            pool.affine_select(out=s.ident[:, :], in_=zero_f[:, :], compare_op=ALU.not_equal, fill=1.0,
                               base=0, pattern=[[-1, P]], channel_multiplier=1).then_inc(made, 1)


def later_weights(s):
    return [name for name in s.w if not name.startswith("x0_")]


def load_weights(eng, w, s, half):
    for name in later_weights(s)[half::2]:
        eng.dma_start(s.w[name][:, :], w[name]).then_inc(s.weights_loaded, 16)


def layer_norm(nc, s, tag):
    with ExitStack() as ctx:
        o = opened(nc, ctx)
        stats = o.sb(tag + "_stats", [P, PAIRS, 6])
        moments = o.sb(tag + "_moments", [P, PAIRS, 2])
        std = o.sb(tag + "_std", [P, PAIRS])
        rstd = o.sb(tag + "_rstd", [P, PAIRS])
        ps = o.ps(tag + "_ps", [P, TCH, 512])
        stats_ready, moments_ready, std_ready, rstd_ready, xn_ready, turned, taken = (
            o.sem(f"{tag}_{n}") for n in ("stats_ready", "moments_ready", "std_ready", "rstd_ready", "xn_ready", "turned", "taken"))
        block = o.block()

        @block.vector
        def _(dve):
            for t in range(PAIRS):
                dve.bn_stats(stats[:, t, :], s.x[:, t, :]).then_inc(stats_ready, 1)
            for t in range(PAIRS):
                dve.wait_ge(stats_ready, t + 1)
                dve.bn_aggr(moments[:, t, :], stats[:, t, :]).then_inc(moments_ready, 1)
            dve.wait_ge(std_ready, 1)
            dve.reciprocal(rstd[:, :], std[:, :]).then_inc(rstd_ready, 1)
            dve.wait_ge(rstd_ready, 1)
            for t in range(PAIRS):
                dve.tensor_scalar(s.xn[:, t, :], s.x[:, t, :], moments[:, t, 0:1], rstd[:, t:t + 1],
                                  ALU.subtract, ALU.mult).then_inc(xn_ready, 1)
            for c in range(0, TCH, 2):
                dve.wait_ge(turned, 4 * (c + 1))
                dve.tensor_copy(s.xT[:, 512 * c:512 * c + 512], ps[:, c, :]).then_inc(taken, 1)

        @block.scalar
        def _(act):
            act.wait_ge(moments_ready, PAIRS)
            act.activation(std[:, :], moments[:, :, 1], ACT.Sqrt, bias=s.eps[:, 0:1]).then_inc(std_ready, 1)
            for c in range(1, TCH, 2):
                act.wait_ge(turned, 4 * (c + 1))
                act.copy(s.xT[:, 512 * c:512 * c + 512], ps[:, c, :]).then_inc(taken, 1)

        @block.tensor
        def _(pe):
            for t in range(PAIRS):
                pe.wait_ge(xn_ready, t + 1)
                pe.transpose(ps[:, t // 4, P * (t % 4):P * (t % 4) + P], s.xn[:, t, :], s.ident[:, :]).then_inc(turned, 1)


def add_projection(nc, s, att, weight, bias, tag):
    with ExitStack() as ctx:
        o = opened(nc, ctx)
        ps_t = o.ps(tag + "_ps_t", [P, 2, 512])
        ps_y = o.ps(tag + "_ps_y", [P, 2, 512])
        attT = o.sb(tag + "_attT", [P, 2, 512])
        turned, taken, projected, added = (o.sem(f"{tag}_{n}") for n in ("turned", "taken", "projected", "added"))
        block = o.block()

        @block.tensor
        def _(pe):
            def turn(c):
                if c >= 2:
                    pe.wait_ge(taken, c - 1)
                for k in range(4):
                    ins = pe.transpose(ps_t[:, c % 2, P * k:P * k + P], att[:, 4 * c + k, :], s.ident[:, :])
                ins.then_inc(turned, 1)

            turn(0)
            for c in range(TCH):
                if c + 1 < TCH:
                    turn(c + 1)
                pe.wait_ge(taken, c + 1)
                if c >= 2:
                    pe.wait_ge(added, c - 1)
                for k in range(4):
                    ins = pe.matmul(ps_y[:, c % 2, P * k:P * k + P], attT[:, c % 2, P * k:P * k + P], weight[:, :],
                                    start=True, stop=True)
                ins.then_inc(projected, 1)

        @block.scalar
        def _(act):
            for c in range(TCH):
                act.wait_ge(turned, c + 1)
                if c >= 2:
                    act.wait_ge(projected, c - 1)
                act.copy(attT[:, c % 2, :], ps_t[:, c % 2, :]).then_inc(taken, 1)

        @block.vector
        def _(dve):
            if bias is not None:
                for t in range(PAIRS):
                    dve.tensor_tensor(s.x[:, t, :], s.x[:, t, :], bias[:, :], ALU.add).then_inc(s.x_biased, 1)
                s.x_biased_count += PAIRS
                dve.wait_ge(s.x_biased, s.x_biased_count)
            for c in range(TCH):
                dve.wait_ge(projected, c + 1)
                dve.tensor_tensor(s.x[:, 4 * c:4 * c + 4, :], s.x[:, 4 * c:4 * c + 4, :],
                                  ps_y[:, c % 2, :].rearrange("p (t d) -> p t d", t=4), ALU.add).then_inc(added, 1)


def cross_attention_0(nc, w, s):
    with ExitStack() as ctx:
        o = opened(nc, ctx)
        q_parts = o.sb("q_parts", [P, 3, T], BF16)
        num = s.xn
        den = o.sb("den", [P, PAIRS, H])
        project_queries_0(nc, s, q_parts)
        attend_context_0(nc, w, s, q_parts, num, den)
        rden = o.sb("rden", [P, PAIRS, H])
        inverted, scaled = o.sem("x0_inverted"), o.sem("x0_scaled")
        with nc.Block() as block:
            @block.vector
            def _(dve):
                dve.reciprocal(rden[:, :, :], den[:, :, :]).then_inc(inverted, 1)
                dve.wait_ge(inverted, 1)
                v = num[:, :, :].rearrange("p t (h d) -> p (t h) d", d=HD)
                r = rden[:, :, :].rearrange("p t h -> p (t h)").unsqueeze(2).broadcast_to([P, PAIRS * H, HD])
                dve.tensor_tensor(v, v, r, ALU.mult).then_inc(scaled, 1)
        add_projection(nc, s, num, s.w["x0_wo"], None, "x0o")


def project_queries_0(nc, s, q_parts):
    with ExitStack() as ctx:
        o = opened(nc, ctx)
        ps = o.ps("q0_ps", [P, TCH, 512])
        rest = o.sb("q0_rest", [P, TCH, 512])
        projected, high, rest1, mid, low = (o.sem("q0_" + n) for n in ("projected", "high", "rest1", "mid", "low"))
        block = o.block()

        @block.tensor
        def _(pe):
            for c in range(TCH):
                pe.matmul(ps[:, c, :], s.w["x0_wq"][:, :], s.xT[:, 512 * c:512 * c + 512],
                          start=True, stop=True).then_inc(projected, 1)

        @block.vector
        def _(dve):
            for c in range(TCH):
                at = slice(512 * c, 512 * c + 512)
                dve.wait_ge(projected, c + 1)
                dve.tensor_copy(q_parts[:, 0, at], ps[:, c, :]).then_inc(high, 1)
                dve.wait_ge(high, c + 1)
                dve.tensor_tensor(rest[:, c, :], ps[:, c, :], q_parts[:, 0, at], ALU.subtract).then_inc(rest1, 1)
                dve.wait_ge(rest1, c + 1)
                dve.tensor_copy(q_parts[:, 1, at], rest[:, c, :]).then_inc(mid, 1)
                dve.wait_ge(mid, c + 1)
                dve.tensor_tensor(q_parts[:, 2, at], rest[:, c, :], q_parts[:, 1, at], ALU.subtract).then_inc(low, 1)


def attend_context_0(nc, w, s, q_parts, num, den):
    with ExitStack() as ctx:
        o = opened(nc, ctx)
        ctxT = o.sb("ctxT", [C, 2, M])
        keys = s.xT
        krest = o.sb("krest", [P, 2, 512])
        q_rows = o.sb("q_rows", [GH, G, 2 * S], BF16)
        k_parts = o.sb("k_parts", [P, 2, 3, M], BF16)
        kst = o.sb("kst", [SROWS, 2, G, M], BF16)
        qst = o.sb("qst", [SROWS, 2, G, 2, S], BF16)
        vals = o.sb("vals", [P, 2, KT, 6, 32])
        ones_row = o.sb("ones_row", [3, M], BF16)
        probs = o.sb("probs", [P, 2, H * S])
        max4 = o.sb("max4", [P, G, MC])
        negmax = o.sb("negmax", [P, G])
        maxrest = o.sb("maxrest", [P, G])
        m_parts = o.sb("m_parts", [P, 3, G], BF16)
        m_rows = o.sb("m_rows", [3 * G, P], BF16)
        acc_sb = o.sb("acc_sb", [P, 7, 2, S])
        turned_sb = o.sb("turned_sb", [P, 7, P])
        sum2 = o.sb("sum2", [P, 4, 2, 32])
        sum1 = o.sb("sum1", [P, 4, 32])
        ps_s = o.ps("ps_s", [P, 2, H * S])
        ps_m = o.ps("ps_m", [P, 2, 512])
        ps_x = o.ps("ps_x", [P, 512])
        ps_a = o.ps("ps_a", [P, 512])
        q = Names(**{n: o.sem("x0_" + n) for n in (
            "set_up", "ones_ready", "ones_stacked", "vals_set_up", "pool_held", "sp_held", "k_filled", "keys_ready", "v_filled", "vals_ready",
            "krest_ready", "kmid_ready", "klow_ready", "q_laid", "q_stacked", "scored", "probs_ready", "pv_done", "max_filled",
            "max_taken", "max_chain", "m_parts_ready", "m_filled", "m_taken", "acc_taken", "turn_filled", "turn_taken",
            "sum2_ready", "sum1_ready", "gathered")})
        q.ctx_loaded = [o.sem(f"x0_ctx_loaded{u}") for u in range(2)]
        q.k_stacked = [[o.sem(f"x0_k_stacked{u}_{part}") for part in range(2)] for u in range(2)]
        q.m_stacked = [o.sem(f"x0_m_stacked{u}") for u in range(2)]
        NKD = 16 * (TERMS + 1)
        NMX = G * MC
        PARTS = (slice(0, 1024), slice(1024, M))
        PART_TILES = (1024 // P, KT)
        MAX_SLOTS = 11
        block = o.block()

        def pairs(eng, body):
            body(0, True, False)
            with eng.Fori(0, (PAIRS - 2) // 2) as twice:
                body(2 * twice + 1, False, False)
                body(2 * twice + 2, False, False)
            body(PAIRS - 1, False, True)

        def first_bank(c):
            return ps_s[:, c // 2, 512 * (c % 2):512 * (c % 2) + 512]

        def chunk(c):
            return slice(512 * c, 512 * c + CCOLS[c])

        @block.sync
        def _(sp):
            def load_ctx(b, u):
                sp.dma_start(ctxT[:, u, :], w["ctxT"][b]).then_inc(q.ctx_loaded[u], 16)

            def stack(b, u, part):
                at = PARTS[part]
                sp.wait_ge(q.klow_ready, MC * b + 2 * part + 2)
                for t in range(TERMS):
                    sp.dma_start(kst[2 * HD * t:2 * HD * (t + 1), u, :, at],
                                 k_parts[:, u, K_PARTS[t], at]).then_inc(q.k_stacked[u][part], 16)
                sp.dma_start(kst[MROW:MROW + 1, u, :, at],
                             w["mask_bias"][b][at].unsqueeze(0).unsqueeze(0).broadcast_to([1, G, at.stop - at.start])
                             ).then_inc(q.k_stacked[u][part], 16)

            def stack_maxima(b, u):
                sp.wait_ge(q.m_taken, b + 1)
                sp.dma_start(qst[MROW + 1:MROW + 4, u, :, :, :], m_rows[:, :]).then_inc(q.m_stacked[u], 16)

            def lay_queries(i):
                for t in range(TERMS):
                    sp.dma_start(q_rows[2 * HD * t:2 * HD * (t + 1), :, :],
                                 q_parts[:, Q_PARTS[t], bass.ds(2 * S * i, 2 * S)]).then_inc(q.q_laid, 16)

            load_ctx(0, 0)
            load_ctx(1, 1)
            lay_queries(0)
            sp.wait_ge(q.ones_ready, 1)
            sp.dma_start(kst[MROW + 1:SROWS, :, :, :], ones_row[:, :].unsqueeze(1).broadcast_to([3, 2 * G, M])).then_inc(q.ones_stacked, 16)
            for u in range(2):
                for part in range(2):
                    stack(u, u, part)
            sp.wait_ge(q.v_filled, 4)
            load_ctx(2, 0)
            stack_maxima(0, 0)

            def step(b, i, u, last, late):
                if not last:
                    if u == 0:
                        sp.wait_ge(q.q_stacked, 2 * (b + 2))
                        lay_queries(i + 1)
                    if not (late and u == 1):
                        sp.wait_ge(q.v_filled, 4 * (b + 2))
                        load_ctx(b + 3, 1 - u)
                    sp.wait_ge(q.scored, KT * b + PART_TILES[0])
                    hold(sp, q.sp_held)
                    stack(b + 2, u, 0)
                if not (last and u == 1):
                    stack_maxima(b + 1, 1 - u)
                if not last:
                    sp.wait_ge(q.scored, KT * b + PART_TILES[1])
                    hold(sp, q.sp_held)
                    stack(b + 2, u, 1)

            def body(i, last, late):
                for u in range(2):
                    step(2 * i + u, i, u, last, late)
            body(0, False, False)
            with sp.Fori(1, PAIRS - 2) as i:
                body(i, False, False)
            body(PAIRS - 2, False, True)
            load_weights(sp, w, s, 0)
            body(PAIRS - 1, True, False)
            load_weights(sp, w, s, 1)
            for u in range(2):
                sp.wait_ge(q.m_stacked[u], 16 * PAIRS)
            sp.wait_ge(s.weights_loaded, 16 * len(later_weights(s)))

        @block.tensor
        def _(pe):
            def job_keys(b, c, i, u, bank=ps_x[:, :]):
                if c == 0:
                    pe.wait_ge(q.ctx_loaded[u], 16 * (i + 1))
                pe.matmul(bank[:, 0:CCOLS[c]], s.w["x0_wk"][:, :], ctxT[:, u, chunk(c)],
                          start=True, stop=True).then_inc(q.k_filled, 1)

            def job_values(b, v, i, u):
                if v == 0:
                    pe.wait_ge(q.ctx_loaded[u], 16 * (i + 1))
                for j in range(4 * v, min(4 * v + 4, KT)):
                    ins = pe.matmul(ps_x[0:KROWS[j], D * (j % 4):D * (j % 4) + D], ctxT[:, u, P * j:P * j + KROWS[j]],
                                    s.w["x0_wv"][:, :], start=True, stop=True)
                ins.then_inc(q.v_filled, 1)

            def job_maxima(b):
                pe.wait_ge(q.m_parts_ready, b + 1)
                pe.transpose(ps_x[:, :].bitcast(BF16)[0:3 * G, 0:P], m_parts[:, :, :].rearrange("p t g -> p (t g)"),
                             s.ident_b[:, :]).then_inc(q.m_filled, 1)

            def max_chunk(b, k, i, u, first):
                c, g = k // G, k % G
                if k == 0:
                    pe.wait_ge(q.q_stacked, 2 * (b + 1))
                if g == 0 and c % 2 == 0:
                    pe.wait_ge(q.k_stacked[u][c // 2], NKD * (i + 1))
                if not (first and k < 2):
                    pe.wait_ge(q.max_taken, NMX * b + k - 1)
                pe.matmul(ps_m[:, k % 2, 0:CCOLS[c]], qst[0:MROW + 1, u, g, :, :].rearrange("p a q -> p (a q)"),
                          kst[0:MROW + 1, u, g, chunk(c)], start=True, stop=True).then_inc(q.max_filled, 1)

            def scores(b, j, i, u, first):
                n = KT * b + j
                slot, k = (u + j) % 2, KROWS[j]
                if j == 0:
                    if first and u == 0:
                        pe.wait_ge(q.ones_stacked, 16)
                        pe.wait_ge(q.keys_ready, 2 * MC)
                    pe.wait_ge(q.m_stacked[u], 16 * (i + 1))
                if not (first and u == 0 and j < 2):
                    pe.wait_ge(q.probs_ready, n - 1)
                for g in range(G):
                    ins = pe.matmul(ps_s[0:k, slot, P * g:P * g + P], kst[:, u, g, P * j:P * j + k],
                                    qst[:, u, g, :, :].rearrange("p a q -> p (a q)"), start=True, stop=True)
                ins.then_inc(q.scored, 1)

            def value_sums(b, j, u, first):
                n = KT * b + j
                slot, k = (u + j) % 2, KROWS[j]
                pe.wait_ge(q.probs_ready, n + 1)
                if j == 0:
                    pe.wait_ge(q.vals_ready, 4 * (b + 1))
                    if not (first and u == 0):
                        pe.wait_ge(q.acc_taken, b)
                place = [(g, g, 0) for g in range(4)] + [(4, j % 4, 192), (5, (j + 2) % 4, 384)]
                for g, tile, col in place:
                    cols = 192 if g < 5 else 64
                    ins = pe.matmul(ps_a[32 * tile:32 * tile + 32, col:col + cols], vals[0:k, u, j, g, :],
                                    probs[0:k, slot, 192 * g:192 * g + cols],
                                    start=(j == 0 and g < 4), stop=(j == KT - 1), skip_group_check=True)
                ins.then_inc(q.pv_done, 1)

            def turn_sums(n, i):
                for r in range(4 * n, min(4 * n + 4, 7)):
                    ins = pe.transpose(ps_x[:, P * (r % 4):P * (r % 4) + P],
                                       acc_sb[:, r, :, :].rearrange("p b q -> p (b q)"), s.ident[:, :])
                ins.then_inc(q.turn_filled, 1)

            pe.wait_ge(q.set_up, 2)
            for b in range(2):
                for c in range(MC):
                    if b:
                        pe.wait_ge(q.keys_ready, c + 1)
                    job_keys(b, c, 0, b, first_bank(c))
            for v in range(4):
                if v:
                    pe.wait_ge(q.vals_ready, v)
                job_values(0, v, 0, 0)
            for k in range(NMX):
                max_chunk(0, k, 0, 0, True)
            pe.wait_ge(q.vals_ready, 4)
            job_maxima(0)

            def step(b, i, u, first, last):
                for j in range(KT):
                    chunks = []
                    if j < MAX_SLOTS and not (last and u == 1):
                        chunks = list(range(NMX * j // MAX_SLOTS, NMX * (j + 1) // MAX_SLOTS))

                    def maxima(n):
                        for k in chunks[:n]:
                            max_chunk(b + 1, k, i + u, 1 - u, False)
                        del chunks[:n]

                    if j:
                        scores(b, j, i, u, first)
                        maxima(1)
                        value_sums(b, j - 1, u, first)
                        maxima(1)
                    if j < 4 and not last:
                        if j == 0:
                            pe.wait_ge(q.m_taken, b + 1)
                        else:
                            pe.wait_ge(q.keys_ready, MC * (b + 2) + j)
                        job_keys(b + 2, j, i + 1, u)
                    if 4 <= j < 8 and not (last and u == 1):
                        if j > 4:
                            pe.wait_ge(q.vals_ready, 4 * (b + 1) + j - 4)
                        elif last:
                            pe.wait_ge(q.m_taken, b + 1)
                        else:
                            pe.wait_ge(q.keys_ready, MC * (b + 3))
                        job_values(b + 1, j - 4, i + u, 1 - u)
                    if j in (8, 9) and u == 0 and not first:
                        if j == 8:
                            pe.wait_ge(q.acc_taken, b)
                            pe.wait_ge(q.vals_ready, 4 * (b + 2))
                        else:
                            pe.wait_ge(q.turn_taken, 2 * i - 1)
                        turn_sums(j - 8, i - 1)
                    if j == 0 and not (first and u == 0):
                        value_sums(b - 1, KT - 1, 1 - u, first)
                    maxima(len(chunks))
                    if j == 0:
                        scores(b, j, i, u, first)
                    if j == 12 and not (last and u == 1):
                        if u == 0 and not first:
                            pe.wait_ge(q.turn_taken, 2 * i)
                        else:
                            pe.wait_ge(q.vals_ready, 4 * (b + 2))
                        job_maxima(b + 1)

            def body(i, first, last):
                for u in range(2):
                    step(2 * i + u, i, u, first, last)
            pairs(pe, body)
            value_sums(B - 1, KT - 1, 1, False)
            pe.wait_ge(q.acc_taken, B)
            pe.wait_ge(q.m_taken, B)
            turn_sums(0, PAIRS - 1)
            pe.wait_ge(q.turn_taken, 2 * PAIRS - 1)
            turn_sums(1, PAIRS - 1)

        @block.scalar
        def _(act):
            def take_keys(b, c, i, u, first, bank=ps_x[:, :]):
                if not (first and u == 0):
                    act.wait_ge(q.klow_ready, MC * (b - 1) + c + 1)
                if not first and c % 2 == 0:
                    act.wait_ge(q.k_stacked[u][c // 2], NKD * i)
                act.wait_ge(q.k_filled, MC * b + c + 1)
                act.copy(k_parts[:, u, 0, chunk(c)], bank[:, 0:CCOLS[c]])
                act.copy(keys[:, chunk(c)], bank[:, 0:CCOLS[c]]).then_inc(q.keys_ready, 1)

            def take_values(b, v, u):
                act.wait_ge(q.v_filled, 4 * b + v + 1)
                k, n = (P, 4) if v < 3 else (KROWS[-1], 1)
                src = ps_x[0:k, 0:D * n].rearrange("p (j c) -> p j c", j=n)
                act.copy(vals[0:k, u, 4 * v:4 * v + n, 0:5, 0:24], src[:, :, 0:120].rearrange("p j (g c) -> p j g c", g=5))
                act.copy(vals[0:k, u, 4 * v:4 * v + n, 5, 0:8], src[:, :, 120:128]).then_inc(q.vals_ready, 1)

            act.wait_ge(q.vals_set_up, 2)
            for b in range(2):
                for c in range(MC):
                    take_keys(b, c, 0, b, True, first_bank(c))
            for v in range(4):
                take_values(0, v, 0)

            def step(b, i, u, first, last):
                for j in range(KT):
                    n = KT * b + j
                    slot, k = (u + j) % 2, KROWS[j]
                    act.wait_ge(q.scored, n + 1)
                    if not (first and u == 0 and j < 2):
                        act.wait_ge(q.pv_done, n - 1)
                    act.activation(probs[0:k, slot, :], ps_s[0:k, slot, :], ACT.Exp, scale=float(HD) ** -0.5).then_inc(q.probs_ready, 1)
                    if j < 4 and not last:
                        take_keys(b + 2, j, i + 1, u, False)
                    if 4 <= j < 8 and not (last and u == 1):
                        take_values(b + 1, j - 4, 1 - u)

            def body(i, first, last):
                for u in range(2):
                    step(2 * i + u, i, u, first, last)
            pairs(act, body)

        @block.vector
        def _(dve):
            dve.memset(qst[:, :, :, :, :], 0.0).then_inc(q.set_up, 1)
            dve.memset(ones_row[:, :], 1.0).then_inc(q.ones_ready, 1)
            dve.wait_ge(q.set_up, 1)
            dve.memset(qst[96:97, :, :, :, :], 1.0).then_inc(q.set_up, 1)

            def stack_queries(b, i, u):
                if u == 0:
                    dve.wait_ge(q.q_laid, 16 * TERMS * (i + 1))
                for a in range(2):
                    dve.tensor_scalar(qst[0:GH, u, :, a, :], q_rows[:, :, S * u:S * u + S],
                                      s.w["x0_own_head"][0:GH, a:a + 1], None, ALU.mult).then_inc(q.q_stacked, 1)

            def split_mid(b, c, u):
                dve.wait_ge(q.krest_ready, MC * b + c + 1)
                dve.tensor_copy(k_parts[:, u, 1, chunk(c)], krest[:, c % 2, 0:CCOLS[c]]).then_inc(q.kmid_ready, 1)

            def take_max(b, k):
                c, g = k // G, k % G
                dve.wait_ge(q.max_filled, NMX * b + k + 1)
                dve.tensor_reduce(max4[:, g, c:c + 1], ps_m[:, k % 2, 0:CCOLS[c]], AX.X, ALU.max).then_inc(q.max_taken, 1)

            def split_max(b, u, i, first):
                dve.wait_ge(q.max_taken, NMX * (b + 1))
                dve.tensor_reduce(negmax[:, :], max4[:, :, :], AX.X, ALU.max, negate=True).then_inc(q.max_chain, 1)
                dve.wait_ge(q.max_chain, 4 * b + 1)
                dve.tensor_copy(m_parts[:, 0, :], negmax[:, :]).then_inc(q.max_chain, 1)
                dve.wait_ge(q.max_chain, 4 * b + 2)
                dve.tensor_tensor(maxrest[:, :], negmax[:, :], m_parts[:, 0, :], ALU.subtract).then_inc(q.max_chain, 1)
                dve.wait_ge(q.max_chain, 4 * b + 3)
                dve.tensor_copy(m_parts[:, 1, :], maxrest[:, :]).then_inc(q.max_chain, 1)
                dve.wait_ge(q.max_chain, 4 * b + 4)
                dve.tensor_tensor(m_parts[:, 2, :], maxrest[:, :], m_parts[:, 1, :], ALU.subtract).then_inc(q.m_parts_ready, 1)
                dve.wait_ge(q.m_filled, b + 1)
                if not first:
                    dve.wait_ge(q.m_stacked[1 - u], 16 * (i + u))
                dve.tensor_copy(m_rows[:, :], ps_x[:, :].bitcast(BF16)[0:3 * G, 0:P]).then_inc(q.m_taken, 1)

            def take_sums(b, u):
                dve.wait_ge(q.pv_done, KT * (b + 1))
                dve.tensor_copy(acc_sb[:, :, u, :], ps_a[:, 0:448].rearrange("p (r q) -> p r q", q=S)).then_inc(q.acc_taken, 1)

            dve.wait_ge(q.set_up, 2)
            stack_queries(0, 0, 0)
            for b in range(2):
                for c in range(MC):
                    split_mid(b, c, b)
            for k in range(NMX):
                take_max(0, k)
            split_max(0, 0, 0, True)

            def take_turned(n, i, first):
                dve.wait_ge(q.turn_filled, 2 * i + n + 1)
                if n == 0 and not first:
                    dve.wait_ge(q.gathered, i)
                r = 4 if n == 0 else 3
                dve.tensor_copy(turned_sb[:, 4 * n:4 * n + r, :].rearrange("p r c -> p (r c)"),
                                ps_x[:, 0:P * r]).then_inc(q.turn_taken, 1)

            def step(b, i, u, first, last):
                if not (last and u == 1):
                    if not (first and u == 0):
                        dve.wait_ge(q.scored, KT * b)
                    stack_queries(b + 1, i + u, 1 - u)
                if last and u == 1:
                    dve.wait_ge(q.turn_filled, 2 * i)
                    take_sums(b - 1, 1 - u)
                else:
                    for k in range(NMX):
                        take_max(b + 1, k)
                        if k == 1 and not (first and u == 0):
                            if u == 1 and not first:
                                dve.wait_ge(q.turn_filled, 2 * i)
                            take_sums(b - 1, 1 - u)
                        if k % 3 == 2 and 8 <= k < 8 + 3 * MC and not last:
                            split_mid(b + 2, (k - 8) // 3, u)
                        if u == 0 and not first and k in (25, 28):
                            take_turned((25, 28).index(k), i - 1, False)
                    split_max(b + 1, 1 - u, i + u, False)

            def body(i, first, last):
                for u in range(2):
                    step(2 * i + u, i, u, first, last)
            pairs(dve, body)
            dve.wait_ge(q.turn_filled, 2 * (PAIRS - 1))
            take_sums(B - 1, 1)
            for n in range(2):
                take_turned(n, PAIRS - 1, False)

        @block.gpsimd
        def _(pool):
            pool.memset(vals[:, :, :, :, :], 0.0).then_inc(q.vals_set_up, 1)

            def split_keys(b, u):
                for c in range(MC):
                    pool.wait_ge(q.keys_ready, MC * b + c + 1)
                    pool.tensor_tensor(krest[:, c % 2, 0:CCOLS[c]], keys[:, chunk(c)], k_parts[:, u, 0, chunk(c)],
                                       ALU.subtract).then_inc(q.krest_ready, 1)
                    pool.wait_ge(q.kmid_ready, MC * b + c + 1)
                    pool.tensor_tensor(k_parts[:, u, 2, chunk(c)], krest[:, c % 2, 0:CCOLS[c]], k_parts[:, u, 1, chunk(c)],
                                       ALU.subtract).then_inc(q.klow_ready, 1)

            def gather(i):
                pool.wait_ge(q.turn_taken, 2 * i + 2)
                hold(pool, q.pool_held)
                for a in range(3):
                    tl = turned_sb[:, a, :].rearrange("p (s r) -> p s r", r=32)
                    pool.tensor_copy(num[:, bass.ds(i, 1), 0:96].rearrange("p o (s a d) -> p (o s) a d", s=4, a=3)[:, :, a, :],
                                     tl[:, :, HD * a:HD * a + HD])
                    pool.tensor_copy(den[:, bass.ds(i, 1), 0:12].rearrange("p o (s a) -> p (o s) a", a=3)[:, :, a:a + 1],
                                     tl[:, :, 24:25])
                tl = turned_sb[:, 3:7, :].rearrange("p r (s c) -> p r s c", c=32)
                pool.tensor_tensor(sum2[:, :, :, :], tl[:, :, 0:2, :], tl[:, :, 2:4, :], ALU.add).then_inc(q.sum2_ready, 1)
                pool.wait_ge(q.sum2_ready, i + 1)
                pool.tensor_tensor(sum1[:, :, :], sum2[:, :, 0, :], sum2[:, :, 1, :], ALU.add).then_inc(q.sum1_ready, 1)
                pool.wait_ge(q.sum1_ready, i + 1)
                hold(pool, q.pool_held)
                for r in range(4):
                    a = r if r < 3 else 0
                    pool.tensor_copy(num[:, bass.ds(i, 1), 96 + 8 * r:104 + 8 * r], sum1[:, r, HD * a:HD * a + HD].unsqueeze(1))
                pool.tensor_copy(den[:, bass.ds(i, 1), 12:16], sum1[:, :, 24].unsqueeze(1)).then_inc(q.gathered, 1)

            pool.wait_ge(q.vals_set_up, 1)
            pool.memset(vals[:, :, :, :, 24:25], 1.0).then_inc(q.vals_set_up, 1)
            for b in range(2):
                split_keys(b, b)

            def body(i, first, last):
                for u in range(2):
                    if not last:
                        split_keys(2 * i + u + 2, u)
                    if u == 0 and not first:
                        gather(i - 1)
            pairs(pool, body)
            gather(PAIRS - 1)


PEEL = 4


def pipeline(eng, count, step, ahead=0):
    for n in range(PEEL):
        step(n, n % 2, n // 2)
    turn = 4 if ahead % 2 == 0 else 2
    with eng.Fori(PEEL // turn, (count - 2 * ahead) // turn) as i:
        for k in range(turn):
            step(turn * i + k, k % 2, turn // 2 * i + k // 2)
    for n in range(count - 2 * ahead, count + PEEL):
        step(n, n % 2, n // 2)


def exists(n, back, count):
    return not isinstance(n, int) or 0 <= n - back < count


def since(n, first):
    return not isinstance(n, int) or n >= first


class Chain:

    def __init__(self, eng, sem):
        self.eng, self.sem, self.n = eng, sem, 0

    def __call__(self, ins):
        ins.then_inc(self.sem, 1)
        self.n += 1

    def wait(self):
        self.eng.wait_ge(self.sem, self.n)


def reserve_experts_0(nc, ctx, s):
    o = opened(nc, ctx)
    s.f0_w1 = o.sb("f0_w1_sb", [P, NE, IT * P])
    s.f0_w2 = o.sb("f0_w2_sb", [P, NE, IT, D])
    s.f0_loaded = o.sem("f0_weights_loaded")


def self_attention_0(nc, w, s):
    with ExitStack() as ctx:
        o = opened(nc, ctx)
        qT = o.sb("a0_qT", [P, T])
        kT = o.sb("a0_kT", [P, T])
        v_all = o.sb("a0_v", [S, B, D])
        att = o.sb("a0_att", [P, PAIRS, D])
        project_rotate_0(nc, w, s, qT, kT, v_all)
        attend_self_0(nc, s, qT, kT, v_all, att)
        add_projection(nc, s, att, s.w["a0_woT"], s.w["a0_bo"], "a0o")


def project_rotate_0(nc, w, s, qT, kT, v_all):
    with ExitStack() as ctx:
        o = opened(nc, ctx)
        ps = o.ps("r0_ps", [P, 4, 512])
        ps_v = o.ps("r0_ps_v", [S, 2, 512])
        turned = o.sb("r0_turned", [P, 2, 512])
        projected, straight, crossed, rotated, v_filled, v_ready = (
            o.sem("r0_" + n) for n in ("projected", "straight", "crossed", "rotated", "v_filled", "v_ready"))
        jobs = [(c, which) for c in range(TCH) for which in range(2)]
        block = o.block()

        @block.sync
        def _(sp):
            sp.dma_start(s.f0_w1[:, :, :], w["big_f0_w1"].rearrange("e d i -> d e i")).then_inc(s.f0_loaded, 16)
            sp.dma_start(s.f0_w2[:, :, :, :], w["big_f0_w2"].rearrange("e (j p) d -> p e j d", p=P)).then_inc(s.f0_loaded, 16)

        @block.tensor
        def _(pe):
            for n, (c, which) in enumerate(jobs):
                names = (("a0_wqT", "a0_wqT_sw"), ("a0_wkT", "a0_wkT_sw"))[which]
                for r in range(2):
                    if n >= 2:
                        pe.wait_ge((straight, crossed)[r], n - 1)
                    pe.matmul(ps[:, 2 * (n % 2) + r, :], s.w[names[r]][:, :], s.xT[:, 512 * c:512 * c + 512],
                              start=True, stop=True).then_inc(projected, 1)
                if n >= 2:
                    pe.wait_ge(v_ready, n - 1)
                for k in range(4):
                    b = 4 * n + k
                    ins = pe.matmul(ps_v[:, n % 2, D * k:D * k + D], s.xT[:, S * b:S * b + S], s.w["a0_wvT"][:, :],
                                    start=True, stop=True)
                ins.then_inc(v_filled, 1)

        @block.vector
        def _(dve):
            for n, (c, which) in enumerate(jobs):
                dst, b0, b1 = ((qT, "a0_bq", "a0_bq_sw"), (kT, "a0_bk", "a0_bk_sw"))[which]
                at = dst[:, 512 * c:512 * c + 512].rearrange("p (b s) -> p b s", s=S)
                cos = s.w["a0_cos"][:, :].unsqueeze(1).broadcast_to([P, 8, S])
                sin = s.w["a0_sin"][:, :].unsqueeze(1).broadcast_to([P, 8, S])
                tmp = turned[:, n % 2, :].rearrange("p (b s) -> p b s", s=S)
                dve.wait_ge(projected, 2 * n + 2)
                dve.scalar_tensor_tensor(out=at, in0=ps[:, 2 * (n % 2), :].rearrange("p (b s) -> p b s", s=S),
                                         scalar=s.w[b0][:, 0:1], in1=cos, op0=ALU.add, op1=ALU.mult).then_inc(straight, 1)
                dve.scalar_tensor_tensor(out=tmp, in0=ps[:, 2 * (n % 2) + 1, :].rearrange("p (b s) -> p b s", s=S),
                                         scalar=s.w[b1][:, 0:1], in1=sin, op0=ALU.add, op1=ALU.mult).then_inc(crossed, 1)
                dve.wait_ge(straight, n + 1)
                dve.wait_ge(crossed, n + 1)
                dve.tensor_tensor(at, at, tmp, ALU.add).then_inc(rotated, 1)
                dve.wait_ge(v_filled, n + 1)
                dve.tensor_tensor(v_all[:, 4 * n:4 * n + 4, :], ps_v[:, n % 2, :].rearrange("p (b d) -> p b d", d=D),
                                  s.w["a0_bv"][0:S, :].unsqueeze(1).broadcast_to([S, 4, D]), ALU.add).then_inc(v_ready, 1)


def attend_self_0(nc, s, qT, kT, v_all, att):
    with ExitStack() as ctx:
        o = opened(nc, ctx)
        qbd = o.sb("a0_qbd", [P, 2, H, S])
        sc = o.sb("a0_sc", [P, 2, G, S])
        pr = o.sb("a0_pr", [P, 2, G, S])
        prT = o.sb("a0_prT", [S, 2, H, S])
        kst = o.sb("a0_kst", [P, 2, S])
        vst = o.sb("a0_vst", [S, 2, D])
        mx = o.sb("a0_mx", [P, 2, G])
        sm = o.sb("a0_sm", [P, 2, G])
        ps_s = o.ps("a0_ps_s", [P, 2, 512])
        ps_t = o.ps("a0_ps_t", [S, H * S])
        ps_o = o.ps("a0_ps_o", [P, 2, 512])
        q = Names(**{n: o.sem("a0_" + n) for n in (
            "held", "qbd_ready", "v_staged", "scored", "masked", "maxed", "shifted", "probs_ready", "summed", "inverted",
            "normed", "turned", "turned_ready", "pv_done", "att_ready")})
        block = o.block()

        @block.tensor
        def _(pe):
            def step(n, u, i):
                if exists(n, 0, B):
                    pe.wait_ge(q.qbd_ready, n + 1)
                    if since(n, 2):
                        pe.wait_ge(q.masked, n - 1)
                    for h in range(H):
                        at = S * (h % 2)
                        ins = pe.matmul(ps_s[at:at + S, u, S * (h // 2):S * (h // 2) + S], qbd[:, u, h, :],
                                        kst[:, u, :], start=True, stop=True)
                    ins.then_inc(q.scored, 1)
                if exists(n, 2, B):
                    pe.wait_ge(q.normed, n - 1)
                    if since(n, 3):
                        pe.wait_ge(q.turned_ready, n - 2)
                    pe.sem_inc(q.held)
                    for g in range(G):
                        ins = pe.transpose(ps_t[:, P * g:P * g + P], pr[:, u, g, :], s.ident[:, :])
                    ins.then_inc(q.turned, 1)
                if exists(n, 3, B):
                    r = 1 - u
                    pe.wait_ge(q.turned_ready, n - 2)
                    pe.wait_ge(q.v_staged, n - 2)
                    if since(n, 5):
                        pe.wait_ge(q.att_ready, n - 4)
                    pe.sem_inc(q.held)
                    for h in range(H):
                        ins = pe.matmul(ps_o[S * r:S * r + S, r, HD * h:HD * h + HD], prT[:, r, h, :],
                                        vst[:, r, HD * h:HD * h + HD], start=True, stop=True)
                    ins.then_inc(q.pv_done, 1)
            pipeline(pe, B, step)

        @block.vector
        def _(dve):
            def step(n, u, i):
                if exists(n, 0, B):
                    dve.wait_ge(q.scored, n + 1)
                    if since(n, 2):
                        dve.wait_ge(q.probs_ready, n - 1)
                    dve.scalar_tensor_tensor(out=sc[:, u, :, :], in0=ps_s[:, u, :].rearrange("p (g k) -> p g k", k=S),
                                             scalar=float(HD) ** -0.5,
                                             in1=s.w["a0_causal"][:, :].unsqueeze(1).broadcast_to([P, G, S]),
                                             op0=ALU.mult, op1=ALU.add).then_inc(q.masked, 1)
                    dve.wait_ge(q.masked, n + 1)
                    dve.tensor_reduce(mx[:, u, :], sc[:, u, :, :], AX.X, ALU.max).then_inc(q.maxed, 1)
                    dve.wait_ge(q.maxed, n + 1)
                    dve.tensor_tensor(sc[:, u, :, :], sc[:, u, :, :], mx[:, u, :].unsqueeze(2).broadcast_to([P, G, S]),
                                      ALU.subtract).then_inc(q.shifted, 1)
                if exists(n, 1, B):
                    r = 1 - u
                    dve.wait_ge(q.probs_ready, n)
                    if since(n, 3):
                        dve.wait_ge(q.normed, n - 2)
                    dve.tensor_reduce(sm[:, r, :], pr[:, r, :, :], AX.X, ALU.add).then_inc(q.summed, 1)
                    dve.wait_ge(q.summed, n)
                    dve.reciprocal(sm[:, r, :], sm[:, r, :]).then_inc(q.inverted, 1)
            pipeline(dve, B, step)

        @block.scalar
        def _(act):
            def step(n, u, i):
                if exists(n, 0, B):
                    act.wait_ge(q.shifted, n + 1)
                    if since(n, 2):
                        act.wait_ge(q.turned, n - 1)
                    act.activation(pr[:, u, :, :], sc[:, u, :, :], ACT.Exp).then_inc(q.probs_ready, 1)
                if exists(n, 2, B):
                    act.wait_ge(q.turned, n - 1)
                    if since(n, 4):
                        act.wait_ge(q.pv_done, n - 3)
                    act.copy(prT[:, u, :, :].rearrange("p h q -> p (h q)"), ps_t[:, :]).then_inc(q.turned_ready, 1)
                if exists(n, 3, B):
                    r = 1 - u
                    act.wait_ge(q.pv_done, n - 2)
                    act.sem_inc(q.held)
                    dst = att[S * r:S * r + S, bass.ds(i - 2 + u, 1), :].rearrange("p t d -> p (t d)")
                    act.copy(dst, ps_o[S * r:S * r + S, r, 0:D]).then_inc(q.att_ready, 1)
            pipeline(act, B, step)

        @block.gpsimd
        def _(pool):
            def spread(n, u):
                pool.tensor_copy(kst[:, u, :], kT[:, bass.ds(S * n, S)])
                pool.tensor_tensor(qbd[:, u, :, :], qT[:, bass.ds(S * n, S)].unsqueeze(1).broadcast_to([P, H, S]),
                                   s.w["a0_heads"][:, :].unsqueeze(2).broadcast_to([P, H, S]), ALU.mult).then_inc(q.qbd_ready, 1)

            spread(0, 0)

            def step(n, u, i):
                if exists(n, -1, B):
                    if since(n, 1):
                        pool.wait_ge(q.scored, n)
                        pool.sem_inc(q.held)
                    spread(n + 1, 1 - u)
                if exists(n, 1, B):
                    r = 1 - u
                    pool.wait_ge(q.inverted, n)
                    pool.tensor_tensor(pr[:, r, :, :], pr[:, r, :, :], sm[:, r, :].unsqueeze(2).broadcast_to([P, G, S]),
                                       ALU.mult).then_inc(q.normed, 1)
                if exists(n, 2, B):
                    if since(n, 4):
                        pool.wait_ge(q.pv_done, n - 3)
                        pool.sem_inc(q.held)
                    pool.tensor_copy(vst[:, u, :], v_all[:, bass.ds(n - 2, 1), :].rearrange("p b d -> p (b d)")).then_inc(q.v_staged, 1)
            pipeline(pool, B, step, ahead=1)


NE = 8


def routing(o, s, router, bias, gates, softmax, tag):
    ps = o.ps(tag + "_ps", [P, PAIRS * NE])
    lg = o.sb(tag + "_logits", [P, PAIRS, NE])
    above = o.sb(tag + "_above", [P, PAIRS, NE, NE])
    level = o.sb(tag + "_level", [P, PAIRS, NE, NE])
    chosen = o.sb(tag + "_chosen", [P, PAIRS, NE])
    top = o.sb(tag + "_top", [P, PAIRS])
    val = o.sb(tag + "_val", [P, PAIRS, NE])
    ex = o.sb(tag + "_ex", [P, PAIRS, NE])
    filled, chain_sem, act_in, act_out = (o.sem(f"{tag}_{n}") for n in ("filled", "chain", "act_in", "act_out"))
    full = [P, PAIRS, NE, NE]
    wide = [P, PAIRS, NE]

    def products(pe):
        for t in range(PAIRS):
            ins = pe.matmul(ps[:, NE * t:NE * t + NE], s.xT[:, P * t:P * t + P], router[:, :], start=True, stop=True)
        ins.then_inc(filled, 1)

    def functions(act):
        act.wait_ge(act_in, 1)
        act.activation(ex[:, :, :], val[:, :, :], ACT.Exp).then_inc(act_out, 1)
        if not softmax:
            act.wait_ge(act_in, 2)
            act.activation(ex[:, :, :], ex[:, :, :], ACT.Ln).then_inc(act_out, 1)
            act.wait_ge(act_in, 3)
            act.activation(val[:, :, :], val[:, :, :], ACT.Sqrt).then_inc(act_out, 1)

    def choice(dve):
        c = Chain(dve, chain_sem)
        dve.wait_ge(filled, 1)
        logits = ps[:, :].rearrange("p (t e) -> p t e", e=NE)
        if bias is None:
            c(dve.tensor_copy(lg[:, :, :], logits))
        else:
            c(dve.tensor_tensor(lg[:, :, :], logits, bias[:, :].unsqueeze(1).broadcast_to(wide), ALU.add))
        c.wait()
        if softmax:
            c(dve.tensor_reduce(top[:, :], lg[:, :, :], AX.X, ALU.max))
            c.wait()
            dve.tensor_tensor(val[:, :, :], lg[:, :, :], top[:, :].unsqueeze(2).broadcast_to(wide), ALU.subtract).then_inc(act_in, 1)
        else:
            c(dve.tensor_scalar(val[:, :, :], lg[:, :, :], -1.0, None, ALU.mult))
            c.wait()
            dve.tensor_tensor(val[:, :, :], lg[:, :, :], val[:, :, :], ALU.min).then_inc(act_in, 1)
        f = lg[:, :, :].unsqueeze(2).broadcast_to(full)
        e = lg[:, :, :].unsqueeze(3).broadcast_to(full)
        c(dve.tensor_tensor(above[:, :, :, :], f, e, ALU.is_gt))
        c(dve.tensor_tensor(level[:, :, :, :], f, e, ALU.is_equal))
        c.wait()
        lower = s.w["lower"][:, :].unsqueeze(1).broadcast_to([P, PAIRS, NE * NE])
        flat = level[:, :, :, :].rearrange("p t e f -> p t (e f)")
        c(dve.tensor_tensor(flat, flat, lower, ALU.mult))
        c.wait()
        c(dve.tensor_tensor(above[:, :, :, :], above[:, :, :, :], level[:, :, :, :], ALU.add))
        c.wait()
        c(dve.tensor_reduce(chosen[:, :, :], above[:, :, :, :], AX.X, ALU.add))
        c.wait()
        c(dve.tensor_scalar(chosen[:, :, :], chosen[:, :, :], 1.5, None, ALU.is_lt))
        c.wait()
        if softmax:
            dve.wait_ge(act_out, 1)
            c(dve.tensor_tensor(ex[:, :, :], ex[:, :, :], chosen[:, :, :], ALU.mult))
            c.wait()
            c(dve.tensor_reduce(top[:, :], ex[:, :, :], AX.X, ALU.add))
            c.wait()
            c(dve.reciprocal(top[:, :], top[:, :]))
            c.wait()
            c(dve.tensor_tensor(gates[:, :, :], ex[:, :, :], top[:, :].unsqueeze(2).broadcast_to(wide), ALU.mult))
        else:
            dve.wait_ge(act_out, 1)
            dve.tensor_scalar(ex[:, :, :], ex[:, :, :], 1.0, None, ALU.add).then_inc(act_in, 1)
            dve.wait_ge(act_out, 2)
            c(dve.tensor_scalar(val[:, :, :], lg[:, :, :], 0.0, None, ALU.max))
            c.wait()
            dve.tensor_tensor(val[:, :, :], val[:, :, :], ex[:, :, :], ALU.add).then_inc(act_in, 1)
            dve.wait_ge(act_out, 3)
            c(dve.tensor_tensor(gates[:, :, :], val[:, :, :], chosen[:, :, :], ALU.mult))
        c.wait()

    return products, functions, choice


def add_gated_bias(nc, s, gates, bias, tag):
    with ExitStack() as ctx:
        o = opened(nc, ctx)
        ps_g = o.ps(tag + "_ps_g", [NE, T])
        ps_y = o.ps(tag + "_ps_y", [P, 4, 512])
        gatesT = o.sb(tag + "_gatesT", [NE, T])
        turned, taken, filled, added = (o.sem(f"{tag}_{n}") for n in ("turned", "taken", "filled", "added"))
        block = o.block()

        @block.tensor
        def _(pe):
            for t in range(PAIRS):
                ins = pe.transpose(ps_g[:, P * t:P * t + P], gates[:, t, :], s.ident[:, :])
            ins.then_inc(turned, 1)
            pe.wait_ge(taken, 1)
            for t in range(PAIRS):
                ins = pe.matmul(ps_y[:, t // 4, D * (t % 4):D * (t % 4) + D], gatesT[:, P * t:P * t + P], bias[:, :],
                                start=True, stop=True)
            ins.then_inc(filled, 1)

        @block.scalar
        def _(act):
            act.wait_ge(turned, 1)
            act.copy(gatesT[:, :], ps_g[:, :]).then_inc(taken, 1)

        @block.vector
        def _(dve):
            dve.wait_ge(filled, 1)
            x = s.x[:, :, :].rearrange("p t d -> p (t d)")
            dve.tensor_tensor(x, x, ps_y[:, :, :].rearrange("p c d -> p (c d)"), ALU.add).then_inc(added, 1)


IT = 4


def experts_0(nc, w, s):
    with ExitStack() as ctx:
        gates = opened(nc, ctx).sb("f0_gates", [P, PAIRS, NE])
        gated_outputs_0(nc, s, gates)
        add_gated_bias(nc, s, gates, s.w["f0_b2"], "f0b")


def gated_outputs_0(nc, s, gates):
    with ExitStack() as ctx:
        o = opened(nc, ctx)
        w1, w2 = s.f0_w1, s.f0_w2
        route_products, route_functions, route_choice = routing(o, s, s.w["f0_wgT"], None, gates, True, "f0r")
        hid = o.sb("f0_hid", [P, 2, IT, 512])
        ps_h = o.ps("f0_ps_h", [P, 4, 512])
        ps_y = o.ps("f0_ps_y", [P, 2, 512])
        filled, activated, summed, added = (o.sem("f0_" + n) for n in ("filled", "activated", "summed", "added"))
        block = o.block()

        @block.tensor
        def _(pe):
            def hidden(c, e, first):
                n = NE * c + e
                for i in range(IT):
                    if not (first and e == 0):
                        pe.wait_ge(activated, IT * (n - 1) + i + 1)
                    pe.matmul(ps_h[:, i, :], w1[:, e, P * i:P * i + P], s.xT[:, bass.ds(512 * c, 512)],
                              start=True, stop=True).then_inc(filled, 1)

            def output(c, e, first):
                n = NE * c + e
                pe.wait_ge(activated, IT * (n + 1))
                if not (first and e < 2):
                    pe.wait_ge(added, 4 * (n - 1))
                for k in range(4):
                    for i in range(IT):
                        ins = pe.matmul(ps_y[:, e % 2, D * k:D * k + D], hid[:, e % 2, i, P * k:P * k + P], w2[:, e, i, :],
                                        start=(i == 0), stop=(i == IT - 1))
                ins.then_inc(summed, 1)

            def chunk(c, first):
                hidden(c, 0, first)
                for e in range(NE):
                    if e + 1 < NE:
                        hidden(c, e + 1, first)
                    output(c, e, first)
            route_products(pe)
            pe.wait_ge(s.f0_loaded, 32)
            chunk(0, True)
            with pe.Fori(1, TCH) as c:
                chunk(c, False)

        @block.scalar
        def _(act):
            def chunk(c, first):
                for e in range(NE):
                    n = NE * c + e
                    for i in range(IT):
                        act.wait_ge(filled, IT * n + i + 1)
                        if i == 0 and not (first and e < 2):
                            act.wait_ge(summed, n - 1)
                        act.activation(hid[:, e % 2, i, :], ps_h[:, i, :], ACT.Gelu,
                                       bias=s.w["f0_b1"][:, IT * e + i:IT * e + i + 1]).then_inc(activated, 1)
            route_functions(act)
            chunk(0, True)
            with act.Fori(1, TCH) as c:
                chunk(c, False)

        @block.vector
        def _(dve):
            def chunk(c, first):
                for e in range(NE):
                    n = NE * c + e
                    dve.wait_ge(summed, n + 1)
                    if not (first and e == 0):
                        dve.wait_ge(added, 4 * n)
                    for k in range(4):
                        x = s.x[:, bass.ds(4 * c + k, 1), :].rearrange("p t d -> p (t d)")
                        g = gates[:, bass.ds(4 * c + k, 1), e:e + 1].rearrange("p t e -> p (t e)")
                        dve.scalar_tensor_tensor(out=x, in0=ps_y[:, e % 2, D * k:D * k + D], scalar=g, in1=x,
                                                 op0=ALU.mult, op1=ALU.add).then_inc(added, 1)
            route_choice(dve)
            chunk(0, True)
            with dve.Fori(1, TCH) as c:
                chunk(c, False)


KJ = (M // P)
KREST = M - KJ * P


def cross_attention_1(nc, w, s):
    with ExitStack() as ctx:
        o = opened(nc, ctx)
        wqk = o.sb("x1_wqk", [P, C])
        wvo = o.sb("x1_wvo", [C, D])
        qk = o.sb("x1_qk", [C, T])
        with ExitStack() as inner:
            oi = opened(nc, inner)
            ps = oi.ps("x1p_ps", [P, 512])
            ps2 = oi.ps("x1p_ps2", [C, 512])
            ps_q = oi.ps("x1p_ps_q", [C, TCH, 512])
            filled, taken, q_filled, q_taken = (oi.sem("x1p_" + n) for n in ("filled", "taken", "q_filled", "q_taken"))
            block = oi.block()

            @block.tensor
            def _(pe):
                pe.matmul(ps[:, 0:C], s.w["x1_wq"][:, :], s.w["x1_wk"][:, :], start=True, stop=True).then_inc(filled, 1)
                pe.matmul(ps2[:, 0:D], s.w["x1_wv"][:, :], s.w["x1_woT"][:, :], start=True, stop=True).then_inc(filled, 1)
                pe.wait_ge(taken, 1)
                for c in range(TCH):
                    pe.matmul(ps_q[:, c, :], wqk[:, :], s.xT[:, 512 * c:512 * c + 512], start=True, stop=True).then_inc(q_filled, 1)

            @block.vector
            def _(dve):
                dve.wait_ge(filled, 1)
                dve.tensor_copy(wqk[:, :], ps[:, 0:C]).then_inc(taken, 1)
                dve.wait_ge(filled, 2)
                dve.tensor_copy(wvo[:, :], ps2[:, 0:D]).then_inc(taken, 1)
                for c in range(TCH):
                    dve.wait_ge(q_filled, c + 1)
                    dve.tensor_copy(qk[:, 512 * c:512 * c + 512], ps_q[:, c, :]).then_inc(q_taken, 1)

        ctxT = o.sb("x1_ctxT", [C, 2, 2, M])
        ctxN = o.sb("x1_ctx", [P, 2, 2, KJ * C])
        ctxR = o.sb("x1_ctx_rest", [KREST, 2, 2, C])
        qst = o.sb("x1_qst", [C, 2, P])
        pr = o.sb("x1_pr", [P, 2, M])
        prT = o.sb("x1_prT", [P, KJ + 1, P])
        stats = o.sb("x1_stats", [P, 2, MC, 6])
        mom = o.sb("x1_mom", [P, 2, 2])
        tot = o.sb("x1_tot", [P, 2, 2])
        var = o.sb("x1_var", [P, 2])
        power = o.sb("x1_power", [P, 1])
        rstd = o.sb("x1_rstd", [P, 2])
        mx = o.sb("x1_mx", [P, 2])
        nb = o.sb("x1_nb", [P, 2])
        den = o.sb("x1_den", [P, 2])
        o1 = o.sb("x1_o1", [P, C])
        o1T = o.sb("x1_o1T", [C, P])
        ps_s = o.ps("x1_ps_s", [P, MC * 512])
        ps_t = o.ps("x1_ps_t", [P, 2, 512])
        ps_x = o.ps("x1_ps_x", [P, 512])
        ps_o = o.ps("x1_ps_o", [P, 512])
        q = Names(**{n: o.sem("x1_" + n) for n in (
            "held", "set_up", "q_staged", "scored", "copied", "stats_ready", "aggregated", "mom_ready", "tot_filled", "tot_taken", "var_neg",
            "var_ready", "rstd_ready", "max_ready", "nb_ready", "probs_ready", "turned", "turned_ready", "pv_done",
            "den_inv", "scaled", "oT_filled", "oT_taken", "y_filled", "added")})
        q.turned_loaded = [o.sem(f"x1_turned_loaded{u}") for u in range(2)]
        q.loaded = [o.sem(f"x1_loaded{u}") for u in range(2)]
        block = o.block()
        GROUPS = [(4 * g, min(4 * g + 4, KJ + 1)) for g in range((KJ + 4) // 4)]
        NG = len(GROUPS)

        @block.sync
        def _(sp):
            def step(n, u, i):
                if exists(n, 0, PAIRS):
                    if since(n, 2):
                        sp.wait_ge(q.scored, MC * (n - 1))
                        sp.sem_inc(q.held)
                    for b in range(2):
                        sp.dma_start(ctxT[:, u, b, :], w["ctxT"][2 * n + b]).then_inc(q.turned_loaded[u], 16)
                    if since(n, 2):
                        sp.wait_ge(q.pv_done, n - 1)
                        sp.sem_inc(q.held)
                    for b in range(2):
                        sp.dma_start(ctxN[:, u, b, :], w["ctx"][2 * n + b, 0:KJ * P, :].rearrange("(p j) c -> p (j c)", p=P)).then_inc(q.loaded[u], 16)
                        sp.dma_start(ctxR[:, u, b, :], w["ctx"][2 * n + b, KJ * P:M, :]).then_inc(q.loaded[u], 16)
            pipeline(sp, PAIRS, step)

        @block.tensor
        def _(pe):
            def turn_out(n):
                pe.wait_ge(q.scaled, n - 1)
                pe.sem_inc(q.held)
                pe.transpose(ps_x[0:C, 0:P], o1[:, :], s.ident[:, :]).then_inc(q.oT_filled, 1)

            def step(n, u, i):
                r = 1 - u
                if exists(n, 0, PAIRS):
                    pe.wait_ge(q.turned_loaded[u], 32 * (i + 1))
                    pe.wait_ge(q.q_staged, n + 1)
                    if since(n, 1):
                        pe.wait_ge(q.copied, MC * n)
                    pe.sem_inc(q.held)
                    for c in range(MC):
                        if c == 2 and exists(n, 2, PAIRS):
                            turn_out(n)
                        for b in range(2):
                            ins = pe.matmul(ps_s[S * b:S * b + S, 512 * c:512 * c + CCOLS[c]], qst[:, u, S * b:S * b + S],
                                            ctxT[:, u, b, 512 * c:512 * c + CCOLS[c]], start=True, stop=True)
                        ins.then_inc(q.scored, 1)
                elif exists(n, 2, PAIRS):
                    turn_out(n)
                if exists(n, 2, PAIRS):
                    pe.wait_ge(q.oT_taken, n - 1)
                    pe.matmul(ps_x[:, 0:D], o1T[:, :], wvo[:, :], start=True, stop=True).then_inc(q.y_filled, 1)
                if exists(n, 1, PAIRS):
                    pe.wait_ge(q.probs_ready, n)
                    for g, (j0, j1) in enumerate(GROUPS):
                        if since(n, 2) or g >= 2:
                            pe.wait_ge(q.turned_ready, NG * (n - 1) + g - 1)
                        pe.sem_inc(q.held)
                        for j in range(j0, j1):
                            src = (pr[:, r, 0:KJ * P].rearrange("p (k j) -> p j k", j=KJ)[:, j, :] if j < KJ
                                   else pr[:, r, KJ * P:M])
                            k = P if j < KJ else KREST
                            ins = pe.transpose(ps_t[0:k, g % 2, P * (j - j0):P * (j - j0) + P], src, s.ident[:, :])
                        ins.then_inc(q.turned, 1)
                if exists(n, 0, PAIRS):
                    pe.wait_ge(q.mom_ready, n + 1)
                    if since(n, 2):
                        pe.wait_ge(q.added, n - 1)
                    pe.matmul(ps_x[:, 0:2], s.w["halves"][:, :], mom[:, u, :], start=True, stop=True).then_inc(q.tot_filled, 1)
                if exists(n, 1, PAIRS):
                    pe.wait_ge(q.turned_ready, NG * n)
                    pe.wait_ge(q.loaded[r], 64 * (i + u))
                    pe.sem_inc(q.held)
                    if since(n, 2):
                        pe.wait_ge(q.scaled, n - 1)
                    pe.sem_inc(q.held)
                    for j in range(KJ + 1):
                        for b in range(2):
                            k = P if j < KJ else KREST
                            rhs = ctxN[:, r, b, C * j:C * j + C] if j < KJ else ctxR[:, r, b, :]
                            ins = pe.matmul(ps_o[S * b:S * b + S, 0:C], prT[0:k, j, S * b:S * b + S], rhs,
                                            start=(j == 0), stop=(j == KJ))
                    ins.then_inc(q.pv_done, 1)
            pipeline(pe, PAIRS, step)

        @block.vector
        def _(dve):
            dve.memset(power[:, :], -0.5).then_inc(q.set_up, 1)

            def add_out(n):
                dve.wait_ge(q.y_filled, n - 1)
                x = s.x[:, bass.ds(n - 2, 1), :].rearrange("p t d -> p (t d)")
                dve.tensor_tensor(x, x, ps_x[:, 0:D], ALU.add).then_inc(q.added, 1)

            def step(n, u, i):
                r = 1 - u
                if exists(n, 0, PAIRS):
                    for c in range(MC):
                        dve.wait_ge(q.copied, MC * n + c + 1)
                        dve.bn_stats(stats[:, u, c, :], pr[:, u, 512 * c:512 * c + CCOLS[c]]).then_inc(q.stats_ready, 1)
                    if exists(n, 2, PAIRS):
                        add_out(n)
                    dve.wait_ge(q.stats_ready, MC * (n + 1))
                    dve.sem_inc(q.held)
                    dve.bn_aggr(mom[:, u, :], stats[:, u, :, :]).then_inc(q.aggregated, 1)
                    dve.wait_ge(q.aggregated, n + 1)
                    dve.scalar_tensor_tensor(out=mom[:, u, 1:2], in0=mom[:, u, 0:1], scalar=mom[:, u, 0:1], in1=mom[:, u, 1:2],
                                             op0=ALU.mult, op1=ALU.add).then_inc(q.mom_ready, 1)
                    dve.tensor_reduce(mx[:, u:u + 1], pr[:, u, :], AX.X, ALU.max).then_inc(q.max_ready, 1)
                    dve.wait_ge(q.tot_filled, n + 1)
                    dve.tensor_copy(tot[:, u, :], ps_x[:, 0:2]).then_inc(q.tot_taken, 1)
                    dve.wait_ge(q.tot_taken, n + 1)
                    dve.scalar_tensor_tensor(out=var[:, u:u + 1], in0=tot[:, u, 0:1], scalar=tot[:, u, 0:1], in1=tot[:, u, 1:2],
                                             op0=ALU.mult, op1=ALU.subtract).then_inc(q.var_neg, 1)
                    dve.wait_ge(q.var_neg, n + 1)
                    dve.tensor_scalar(var[:, u:u + 1], var[:, u:u + 1], -1.0, EPS, ALU.mult, ALU.add).then_inc(q.var_ready, 1)
                    dve.wait_ge(q.rstd_ready, n + 1)
                    dve.wait_ge(q.max_ready, n + 1)
                    dve.scalar_tensor_tensor(out=nb[:, u:u + 1], in0=mx[:, u:u + 1], scalar=-1.0, in1=rstd[:, u:u + 1],
                                             op0=ALU.mult, op1=ALU.mult).then_inc(q.nb_ready, 1)
                elif exists(n, 2, PAIRS):
                    add_out(n)
                if exists(n, 1, PAIRS):
                    dve.wait_ge(q.probs_ready, n)
                    dve.reciprocal(den[:, r:r + 1], den[:, r:r + 1]).then_inc(q.den_inv, 1)
                    dve.wait_ge(q.den_inv, n)
                    dve.wait_ge(q.pv_done, n)
                    if since(n, 2):
                        dve.wait_ge(q.oT_filled, n - 1)
                    dve.tensor_scalar(o1[:, :], ps_o[:, 0:C], den[:, r:r + 1], None, ALU.mult).then_inc(q.scaled, 1)
            pipeline(dve, PAIRS, step)

        @block.scalar
        def _(act):
            def take_out(n):
                act.wait_ge(q.oT_filled, n - 1)
                act.copy(o1T[:, :], ps_x[0:C, 0:P]).then_inc(q.oT_taken, 1)

            def step(n, u, i):
                if exists(n, 2, PAIRS) and not exists(n, 0, PAIRS):
                    take_out(n)
                if exists(n, 0, PAIRS):
                    for c in range(MC):
                        act.wait_ge(q.scored, MC * n + c + 1)
                        if c == 0 and since(n, 2):
                            act.wait_ge(q.turned, NG * (n - 1))
                        if c == 2 and exists(n, 2, PAIRS):
                            take_out(n)
                        act.copy(pr[:, u, 512 * c:512 * c + CCOLS[c]], ps_s[:, 512 * c:512 * c + CCOLS[c]]).then_inc(q.copied, 1)
                if exists(n, 1, PAIRS):
                    for g, (j0, j1) in enumerate(GROUPS):
                        k = P if g < NG - 1 else KREST
                        act.wait_ge(q.turned, NG * (n - 1) + g + 1)
                        if g == 0 and since(n, 2):
                            act.wait_ge(q.pv_done, n - 1)
                        act.copy(prT[0:k, j0:j1, :].rearrange("p j k -> p (j k)"), ps_t[0:k, g % 2, 0:P * (j1 - j0)]).then_inc(q.turned_ready, 1)
                if exists(n, 0, PAIRS):
                    act.wait_ge(q.nb_ready, n + 1)
                    if since(n, 2):
                        act.wait_ge(q.scaled, n - 1)
                    act.activation(pr[:, u, :], pr[:, u, :], ACT.Exp, scale=rstd[:, u:u + 1], bias=nb[:, u:u + 1],
                                   accum_out=den[:, u:u + 1]).then_inc(q.probs_ready, 1)
            pipeline(act, PAIRS, step)

        @block.gpsimd
        def _(pool):
            pool.wait_ge(q.set_up, 1)

            def step(n, u, i):
                if exists(n, 0, PAIRS):
                    if since(n, 2):
                        pool.wait_ge(q.scored, MC * (n - 1))
                        pool.sem_inc(q.held)
                    pool.tensor_copy(qst[:, u, :], qk[:, bass.ds(P * n, P)]).then_inc(q.q_staged, 1)
                    pool.wait_ge(q.var_ready, n + 1)
                    pool.tensor_tensor(rstd[:, u:u + 1], var[:, u:u + 1], power[:, :], ALU.pow).then_inc(q.rstd_ready, 1)
            pipeline(pool, PAIRS, step)


NS = 16
HF = 2


def state_space_1(nc, w, s):
    with ExitStack() as ctx:
        o = opened(nc, ctx)
        u = o.sb("s1_u", [P, HF, B, S])
        kern = o.sb("s1_kern", [P, HF, S])
        with ExitStack() as inner:
            oi = opened(nc, inner)
            g = oi.sb("s1_g", [P, HF, B, S])
            dt_sums = oi.sb("s1_dt_sums", [P, HF, 2 * TCH])
            project_states_1(nc, s, u, g, dt_sums)
            gate_states_1(nc, s, u, g)
            make_kernel_1(nc, s, dt_sums, kern)
        y = o.sb("s1_y", [P, HF, B, S])
        convolve_1(nc, s, u, kern, y)
        project_out_1(nc, s, y)


def project_states_1(nc, s, u, g, dt_sums):
    with ExitStack() as ctx:
        o = opened(nc, ctx)
        z = o.sb("s1_z", [P, HF, TCH, 512])
        ps = o.ps("s1_ps", [P, 6, 512])
        filled, u_taken, g_taken, z_taken, relu_taken, abs_ready, exp_ready, ln_ready = (
            o.sem("s1a_" + n) for n in ("filled", "u_taken", "g_taken", "z_taken", "relu_taken", "abs_ready", "exp_ready", "ln_ready"))
        jobs = [(h, c) for h in range(HF) for c in range(TCH)]
        block = o.block()

        @block.tensor
        def _(pe):
            for n, (h, c) in enumerate(jobs):
                for k, name in enumerate(("s1_wxT", "s1_wgT", "s1_wdtT")):
                    if n >= 2:
                        for done in ((u_taken,), (g_taken,), (z_taken, relu_taken))[k]:
                            pe.wait_ge(done, n - 1)
                    pe.matmul(ps[:, 3 * (n % 2) + k, :], s.w[name][:, P * h:P * h + P], s.xT[:, 512 * c:512 * c + 512],
                              start=True, stop=True).then_inc(filled, 1)

        @block.vector
        def _(dve):
            for n, (h, c) in enumerate(jobs):
                dve.wait_ge(filled, 3 * n + 1)
                dve.tensor_scalar(u[:, h, 8 * c:8 * c + 8, :].rearrange("p b s -> p (b s)"), ps[:, 3 * (n % 2), :],
                                  s.w["s1_bx"][:, h:h + 1], None, ALU.add).then_inc(u_taken, 1)
                dve.wait_ge(relu_taken, n + 1)
                dve.tensor_scalar(z[:, h, c, :], ps[:, 3 * (n % 2) + 2, :], s.w["s1_bdt"][:, h:h + 1], None, ALU.add).then_inc(z_taken, 1)
                dve.wait_ge(z_taken, n + 1)
                dve.scalar_tensor_tensor(out=z[:, h, c, :], in0=z[:, h, c, :], scalar=-1.0, in1=z[:, h, c, :], op0=ALU.mult, op1=ALU.min).then_inc(abs_ready, 1)

        @block.scalar
        def _(act):
            spare = o.sb("s1_spare", [P, 512])
            for n, (h, c) in enumerate(jobs):
                act.wait_ge(filled, 3 * n + 2)
                act.activation(g[:, h, 8 * c:8 * c + 8, :].rearrange("p b s -> p (b s)"), ps[:, 3 * (n % 2) + 1, :], ACT.Sigmoid,
                               bias=s.w["s1_bg"][:, h:h + 1]).then_inc(g_taken, 1)
                act.wait_ge(filled, 3 * n + 3)
                if n:
                    act.wait_ge(relu_taken, n)
                act.activation(spare[:, :], ps[:, 3 * (n % 2) + 2, :], ACT.Relu, bias=s.w["s1_bdt"][:, h:h + 1],
                               accum_out=dt_sums[:, h, c:c + 1]).then_inc(relu_taken, 1)
            for n, (h, c) in enumerate(jobs):
                act.wait_ge(abs_ready, n + 1)
                act.activation(z[:, h, c, :], z[:, h, c, :], ACT.Exp).then_inc(exp_ready, 1)
            for n, (h, c) in enumerate(jobs):
                act.wait_ge(exp_ready, n + 1)
                act.activation(z[:, h, c, :], z[:, h, c, :], ACT.Ln, bias=s.ones[:, 0:1],
                               accum_out=dt_sums[:, h, TCH + c:TCH + c + 1]).then_inc(ln_ready, 1)


def gate_states_1(nc, s, u, g):
    with ExitStack() as ctx:
        o = opened(nc, ctx)
        hc = o.sb("s1_hc", [P, HF, B, S])
        chain_sem = o.sem("s1b_chain")
        block = o.block()

        @block.vector
        def _(dve):
            chain = Chain(dve, chain_sem)
            both = range(HF)
            cw = s.w["s1_cw"]
            for h in both:
                chain(dve.tensor_scalar(hc[:, h, :, :], u[:, h, :, :], cw[:, 3 * h + 1:3 * h + 2], s.w["s1_cb"][:, h:h + 1],
                                        ALU.mult, ALU.add))
            for tap, dst, src in ((0, slice(1, S), slice(0, S - 1)), (2, slice(0, S - 1), slice(1, S))):
                chain.wait()
                for h in both:
                    chain(dve.scalar_tensor_tensor(out=hc[:, h, :, dst], in0=u[:, h, :, src], scalar=cw[:, 3 * h + tap:3 * h + tap + 1],
                                                   in1=hc[:, h, :, dst], op0=ALU.mult, op1=ALU.add))
            for h in both:
                chain.wait()
                chain(dve.tensor_tensor(u[:, h, :, :], u[:, h, :, :], hc[:, h, :, :], ALU.subtract))
                chain.wait()
                chain(dve.tensor_tensor(u[:, h, :, :], u[:, h, :, :], g[:, h, :, :], ALU.mult))
                chain.wait()
                chain(dve.tensor_tensor(u[:, h, :, :], u[:, h, :, :], hc[:, h, :, :], ALU.add))
            chain.wait()


def make_kernel_1(nc, s, dt_sums, kern):
    with ExitStack() as ctx:
        o = opened(nc, ctx)
        a = o.sb("s1_a", [P, HF, NS])
        e = o.sb("s1_e", [P, HF, NS])
        dt = o.sb("s1_dt", [P, HF])
        adt = o.sb("s1_adt", [P, HF, NS])
        cb = o.sb("s1_cbd", [P, HF, NS])
        powers = o.sb("s1_powers", [P, HF, S, NS])
        chain_sem, act_in, act_out = (o.sem("s1c_" + n) for n in ("chain", "act_in", "act_out"))
        block = o.block()
        wide = [P, HF, NS]
        raw = s.w["s1_araw"][:, :].rearrange("p (h n) -> p h n", h=HF)

        @block.scalar
        def _(act):
            act.wait_ge(act_in, 1)
            act.activation(e[:, :, :], e[:, :, :], ACT.Exp).then_inc(act_out, 1)
            act.wait_ge(act_out, 1)
            act.activation(e[:, :, :], e[:, :, :], ACT.Ln, bias=s.ones[:, 0:1]).then_inc(act_out, 1)
            act.wait_ge(act_in, 2)
            act.activation(e[:, :, :], adt[:, :, :], ACT.Exp).then_inc(act_out, 1)
            act.wait_ge(act_in, 3)
            act.activation(powers[:, :, :, :], powers[:, :, :, :], ACT.Exp).then_inc(act_out, 1)

        @block.vector
        def _(dve):
            c = Chain(dve, chain_sem)
            dve.scalar_tensor_tensor(out=e[:, :, :], in0=raw, scalar=-1.0, in1=raw, op0=ALU.mult, op1=ALU.min).then_inc(act_in, 1)
            c(dve.tensor_reduce(dt[:, :], dt_sums[:, :, :], AX.X, ALU.add))
            c.wait()
            c(dve.tensor_scalar(dt[:, :], dt[:, :], 1.0 / T, None, ALU.mult))
            c.wait()
            c(dve.tensor_scalar(dt[:, :], dt[:, :], 0.001, 2.0, ALU.max, ALU.min))
            c(dve.tensor_scalar(a[:, :, :], raw, 0.0, None, ALU.max))
            c.wait()
            dve.wait_ge(act_out, 2)
            c(dve.tensor_tensor(a[:, :, :], a[:, :, :], e[:, :, :], ALU.add))
            c.wait()
            c(dve.tensor_scalar(a[:, :, :], a[:, :, :], -1.0, None, ALU.mult))
            c.wait()
            dve.tensor_tensor(adt[:, :, :], a[:, :, :], dt[:, :].unsqueeze(2).broadcast_to(wide), ALU.mult).then_inc(act_in, 1)
            dve.wait_ge(act_in, 2)
            for h in range(HF):
                ins = dve.tensor_tensor(powers[:, h, :, :], adt[:, h, :].unsqueeze(1).broadcast_to([P, S, NS]),
                                        s.w["s1_k"][:, :].unsqueeze(2).broadcast_to([P, S, NS]), ALU.mult)
                if h == 0:
                    c(ins)
            ins.then_inc(act_in, 1)
            c(dve.tensor_scalar(a[:, :, :], a[:, :, :], 1e-6, None, ALU.add))
            c.wait()
            c(dve.reciprocal(a[:, :, :], a[:, :, :]))
            c.wait()
            dve.wait_ge(act_out, 3)
            c(dve.tensor_scalar(cb[:, :, :], e[:, :, :], -1.0, None, ALU.add))
            c.wait()
            for factor in (a[:, :, :], s.w["s1_b"][:, :].rearrange("p (h n) -> p h n", h=HF),
                           s.w["s1_c"][:, :].rearrange("p (h n) -> p h n", h=HF)):
                c(dve.tensor_tensor(cb[:, :, :], cb[:, :, :], factor, ALU.mult))
                c.wait()
            dve.wait_ge(act_out, 4)
            for h in range(HF):
                c(dve.tensor_tensor(powers[:, h, :, :], powers[:, h, :, :], cb[:, h, :].unsqueeze(1).broadcast_to([P, S, NS]), ALU.mult))
            c.wait()
            for h in range(HF):
                c(dve.tensor_reduce(kern[:, h, :], powers[:, h, :, :], AX.X, ALU.add))
            c.wait()


def convolve_1(nc, s, u, kern, y):
    with ExitStack() as ctx:
        o = opened(nc, ctx)
        diag = o.sb("s1_diag", [P, 8, P])
        y_pool = o.sb("s1_y_pool", [P, HF, B, S])
        term = o.sb("s1_term", [P, HF, B, S])
        ps = o.ps("s1_ps_conv", [P, HF, B, S])
        zeroed, diag_ready, scaled, summed, joined = (
            o.sem("s1d_" + n) for n in ("zeroed", "diag_ready", "scaled", "summed", "joined"))
        tapped = [o.sem(f"s1d_tapped{h}") for h in range(HF)]
        pool_tapped = [o.sem(f"s1d_pool_tapped{h}") for h in range(HF)]
        on_pe = [k for k in range(S) if k % 5 == 0 or k % 20 == 3]
        pe_taps = [(k, h) for k in on_pe for h in range(HF)]
        pool_taps = [k for k in range(S) if k % 5 == 1]
        dve_taps = [k for k in range(S) if k not in on_pe and k not in pool_taps]
        BC = 512 // S
        block = o.block()

        @block.scalar
        def _(act):
            for n, (k, h) in enumerate(pe_taps):
                if n >= 8:
                    act.wait_ge(summed, n - 7)
                act.activation(diag[:, n % 8, :], s.ident[:, :], ACT.Copy, scale=kern[:, h, k:k + 1]).then_inc(diag_ready, 1)
                if n < HF * len(pool_taps):
                    tap = pool_taps[n // HF]
                    if n >= HF:
                        act.wait_ge(pool_tapped[h], n // HF + 1)
                    act.activation(term[:, h, :, 0:S - tap], u[:, h, :, 0:S - tap], ACT.Copy, scale=kern[:, h, tap:tap + 1]).then_inc(scaled, 1)

        @block.tensor
        def _(pe):
            for n, (k, h) in enumerate(pe_taps):
                pe.wait_ge(diag_ready, n + 1)
                for c in range(B // BC):
                    ins = pe.matmul(ps[:, h, BC * c:BC * c + BC, k:S], diag[:, n % 8, :], u[:, h, BC * c:BC * c + BC, 0:S - k],
                                    start=(k == 0), stop=(n >= len(pe_taps) - HF), skip_group_check=True)
                ins.then_inc(summed, 1)

        @block.gpsimd
        def _(pool):
            for h in range(HF):
                pool.memset(y[:, h, :, :], 0.0).then_inc(zeroed, 1)
            for h in range(HF):
                pool.memset(y_pool[:, h, :, :], 0.0).then_inc(pool_tapped[h], 1)
            for n, k in enumerate(pool_taps):
                for h in range(HF):
                    pool.wait_ge(pool_tapped[h], n + 1)
                    pool.wait_ge(scaled, HF * n + h + 1)
                    pool.tensor_tensor(y_pool[:, h, :, k:S], y_pool[:, h, :, k:S], term[:, h, :, 0:S - k],
                                       ALU.add).then_inc(pool_tapped[h], 1)

        @block.vector
        def _(dve):
            for n, k in enumerate(dve_taps):
                for h in range(HF):
                    if n == 0:
                        dve.wait_ge(zeroed, h + 1)
                    else:
                        dve.wait_ge(tapped[h], n)
                    dve.scalar_tensor_tensor(out=y[:, h, :, k:S], in0=u[:, h, :, 0:S - k], scalar=kern[:, h, k:k + 1],
                                             in1=y[:, h, :, k:S], op0=ALU.mult, op1=ALU.add).then_inc(tapped[h], 1)
            for h in range(HF):
                dve.wait_ge(pool_tapped[h], len(pool_taps) + 1)
                dve.wait_ge(tapped[h], len(dve_taps))
                dve.tensor_tensor(y[:, h, :, :], y[:, h, :, :], y_pool[:, h, :, :], ALU.add).then_inc(tapped[h], 1)
            dve.wait_ge(summed, len(pe_taps))
            for h in range(HF):
                dve.wait_ge(tapped[h], len(dve_taps) + 1)
                dve.tensor_tensor(y[:, h, :, :], y[:, h, :, :], ps[:, h, :, :], ALU.add).then_inc(joined, 1)


def project_out_1(nc, s, y):
    with ExitStack() as ctx:
        o = opened(nc, ctx)
        ps = o.ps("s1_ps_out", [P, PAIRS, D])
        r = o.sb("s1_r", [P, PAIRS, D])
        stats = o.sb("s1_stats", [P, PAIRS, 6])
        mom = o.sb("s1_mom", [P, PAIRS, 2])
        std = o.sb("s1_std", [P, PAIRS])
        filled, chain_sem, mom_ready, std_ready = (o.sem("s1e_" + n) for n in ("filled", "chain", "mom_ready", "std_ready"))
        block = o.block()
        wide = [P, PAIRS, D]

        @block.tensor
        def _(pe):
            for t in range(PAIRS):
                for h in range(HF):
                    ins = pe.matmul(ps[:, t, :], y[:, h, 2 * t:2 * t + 2, :].rearrange("p b s -> p (b s)"),
                                    s.w["s1_woT"][:, D * h:D * h + D], start=(h == 0), stop=(h == HF - 1))
            ins.then_inc(filled, 1)

        @block.scalar
        def _(act):
            act.wait_ge(mom_ready, PAIRS)
            act.activation(std[:, :], mom[:, :, 1], ACT.Sqrt, bias=s.eps[:, 0:1]).then_inc(std_ready, 1)

        @block.vector
        def _(dve):
            c = Chain(dve, chain_sem)
            dve.wait_ge(filled, 1)
            c(dve.tensor_tensor(r[:, :, :], s.xn[:, :, :], ps[:, :, :], ALU.add))
            c.wait()
            c(dve.tensor_tensor(r[:, :, :], r[:, :, :], s.w["s1_bout"][:, :].unsqueeze(1).broadcast_to(wide), ALU.add))
            c.wait()
            for t in range(PAIRS):
                c(dve.bn_stats(stats[:, t, :], r[:, t, :]))
            c.wait()
            for t in range(PAIRS):
                dve.bn_aggr(mom[:, t, :], stats[:, t, :]).then_inc(mom_ready, 1)
            dve.wait_ge(std_ready, 1)
            c(dve.reciprocal(std[:, :], std[:, :]))
            c.wait()
            for t in range(PAIRS):
                c(dve.tensor_scalar(r[:, t, :], r[:, t, :], mom[:, t, 0:1], std[:, t:t + 1], ALU.subtract, ALU.mult))
            c.wait()
            c(dve.tensor_tensor(r[:, :, :], r[:, :, :], s.w["s1_g"][:, :].unsqueeze(1).broadcast_to(wide), ALU.mult))
            c.wait()
            c(dve.tensor_tensor(r[:, :, :], r[:, :, :], s.w["s1_lb"][:, :].unsqueeze(1).broadcast_to(wide), ALU.add))
            c.wait()
            c(dve.tensor_tensor(s.x[:, :, :], s.x[:, :, :], r[:, :, :], ALU.add))
            c.wait()


HE = 64


def experts_1(nc, w, s):
    with ExitStack() as ctx:
        gates = opened(nc, ctx).sb("f1_gates", [P, PAIRS, NE])
        gated_outputs_1(nc, s, gates)
        add_gated_bias(nc, s, gates, s.w["f1_rb2"], "f1b")


def gated_outputs_1(nc, s, gates):
    with ExitStack() as ctx:
        o = opened(nc, ctx)
        route_products, route_functions, route_choice = routing(o, s, s.w["f1_wrT"], s.w["f1_eb"], gates, False, "f1r")
        hid = o.sb("f1_hid", [P, 2, 512])
        ps_h = o.ps("f1_ps_h", [P, 2, 512])
        ps_y = o.ps("f1_ps_y", [P, 2, 2, 512])
        q = Names(**{n: o.sem("f1_" + n) for n in ("held", "biased", "filled", "activated", "summed", "added")})
        UNITS = NE // 2 + 1
        block = o.block()

        def unit(n):
            return (s.w["f1_rw1"][:, P * n:P * n + P], n, P, 2) if n < UNITS - 1 else (s.w["f1_sw1"][:, :], n, HE, 1)

        @block.tensor
        def _(pe):
            def hidden(c, n):
                w1, _, rows, _ = unit(n % UNITS)
                if n >= 2:
                    pe.wait_ge(q.activated, n - 1)
                pe.matmul(ps_h[0:rows, n % 2, :], w1, s.xT[:, 512 * c:512 * c + 512], start=True, stop=True).then_inc(q.filled, 1)

            def output(c, n):
                _, m, _, experts = unit(n % UNITS)
                pe.wait_ge(q.activated, n + 1)
                if n >= 2:
                    pe.wait_ge(q.added, n - 1)
                for a in range(experts):
                    for k in range(4):
                        w2 = s.w["f1_rw2"][HE * a:HE * a + HE, D * m:D * m + D] if m < UNITS - 1 else s.w["f1_sw2"][:, :]
                        ins = pe.matmul(ps_y[:, n % 2, a, D * k:D * k + D], hid[HE * a:HE * a + HE, n % 2, P * k:P * k + P], w2,
                                        start=True, stop=True)
                ins.then_inc(q.summed, 1)

            route_products(pe)
            total = TCH * UNITS
            hidden(0, 0)
            for n in range(total):
                if n + 1 < total:
                    hidden((n + 1) // UNITS, n + 1)
                output(n // UNITS, n)

        @block.scalar
        def _(act):
            route_functions(act)
            for n in range(TCH * UNITS):
                _, m, rows, _ = unit(n % UNITS)
                act.wait_ge(q.filled, n + 1)
                if n >= 2:
                    act.wait_ge(q.summed, n - 1)
                act.activation(hid[0:rows, n % 2, :], ps_h[0:rows, n % 2, :], ACT.Silu, bias=s.w["f1_b1"][0:rows, m:m + 1]).then_inc(q.activated, 1)

        @block.vector
        def _(dve):
            route_choice(dve)
            x = s.x[:, :, :]
            dve.tensor_tensor(x, x, s.w["f1_sb2"][:, :].unsqueeze(1).broadcast_to([P, PAIRS, D]), ALU.add).then_inc(q.biased, 1)
            dve.wait_ge(q.biased, 1)
            for n in range(TCH * UNITS):
                c = n // UNITS
                _, m, _, experts = unit(n % UNITS)
                dve.wait_ge(q.summed, n + 1)
                if n:
                    dve.wait_ge(q.added, n)
                if experts == 1:
                    xs = s.x[:, 4 * c:4 * c + 4, :].rearrange("p t d -> p (t d)")
                    dve.tensor_tensor(xs, xs, ps_y[:, n % 2, 0, :], ALU.add).then_inc(q.added, 1)
                    continue
                for a in range(2):
                    for k in range(4):
                        xs = s.x[:, 4 * c + k, :]
                        ins = dve.scalar_tensor_tensor(out=xs, in0=ps_y[:, n % 2, a, D * k:D * k + D],
                                                       scalar=gates[:, 4 * c + k, 2 * m + a:2 * m + a + 1], in1=xs,
                                                       op0=ALU.mult, op1=ALU.add)
                        if a == 0:
                            ins.then_inc(q.held, 1)
                    if a == 0:
                        dve.wait_ge(q.held, 4 * (n - c + 1))
                ins.then_inc(q.added, 1)


def clear_semaphores(nc, first):
    with nc.semaphore("past_layer") as last, nc.Block() as block:
        @block.gpsimd
        def _(pool):
            pool.sem_clear(range(first.num, last.num + 1))


def program(nc, w):
    with ExitStack() as ctx:
        o = opened(nc, ctx)
        s = Names()
        s.x = o.sb("x", [P, PAIRS, D])
        s.xn = o.sb("xn", [P, PAIRS, D])
        s.xT = o.sb("xT", [P, T])
        s.ident = o.sb("ident", [P, P])
        s.ident_b = o.sb("ident_b", [P, P], BF16)
        s.ones = o.sb("ones", [P, P])
        s.eps = o.sb("eps", [P, 1])
        s.x_biased, s.x_biased_count = o.sem("x_biased"), 0
        s.w = {n: o.sb("w_" + n, list(w[n].shape)) for n in WEIGHTS if n in w}
        s.weights_loaded = o.sem("weights_loaded")
        with nc.semaphore("of_layer") as first:
            pass
        load_first(nc, w, s)
        layer_norm(nc, s, "n0")
        cross_attention_0(nc, w, s)
        experts = ExitStack()
        reserve_experts_0(nc, experts, s)
        layer_norm(nc, s, "n1")
        self_attention_0(nc, w, s)
        layer_norm(nc, s, "n2")
        experts_0(nc, w, s)
        experts.close()
        clear_semaphores(nc, first)
        layer_norm(nc, s, "n3")
        cross_attention_1(nc, w, s)
        layer_norm(nc, s, "n4")
        state_space_1(nc, w, s)
        layer_norm(nc, s, "n5")
        experts_1(nc, w, s)
        stored = o.sem("stored")
        with nc.Block() as block:
            @block.sync
            def _(sp):
                sp.dma_start(w["out"].rearrange("(t p) d -> p t d", p=P), s.x[:, :, :]).then_inc(stored, 16)
                sp.wait_ge(stored, 16)


def kernel(**inputs):
    import numpy as _np
    import concourse.bacc as _bacc
    from concourse import mybir as _mybir
    from concourse.bass_utils import run_bass_kernel_spmd as _run

    a = {n: _np.asarray(v) for n, v in inputs.items()}
    pair_order = _np.arange(D).reshape(G, 2 * HD).T.reshape(-1)
    swapped = _np.arange(D) ^ 1
    inv_freq = 1.0 / 10000.0 ** (_np.arange(HD // 2, dtype=_np.float32) / (HD // 2))
    angle = _np.arange(S, dtype=_np.float32)[None, :] * inv_freq.astype(_np.float32)[_np.arange(D) % HD // 2][:, None]
    cos = _np.cos(angle).astype(_np.float32)
    sin = (_np.sin(angle) * _np.where(_np.arange(D) % 2, 1.0, -1.0)[:, None]).astype(_np.float32)
    causal = _np.where(_np.arange(S)[None, :] <= (_np.arange(P) % S)[:, None], 0.0, MASKED).astype(_np.float32)
    heads = (_np.arange(D)[:, None] // HD == _np.arange(H)[None, :]).astype(_np.float32)
    own_head = (_np.arange(P)[:, None] // HD % 2 == _np.arange(2)[None, :]).astype(_np.float32)
    lower = _np.tri(NE, k=-1, dtype=_np.float32).reshape(-1)

    def rows(v):
        return _np.broadcast_to(v, (P, *v.shape))

    def by_half(v):
        return v.reshape(HF, P, -1).transpose(1, 0, 2).reshape(P, -1)

    halves = (_np.arange(P)[:, None] // S == _np.arange(P)[None, :] // S).astype(_np.float32) / S
    b1 = _np.concatenate([a["L1_ffn_rb1"].reshape(NE // 2, 2 * HE).T, _np.tile(a["L1_ffn_sb1"], 2)[:, None]], axis=1)

    laid = {
        "x": a["x"].reshape(T, D),
        "ctxT": a["ctx_768"].transpose(0, 2, 1),
        "mask": a["mask_BxS2_bf1"].view(_np.uint8),
        "x0_wq": a["L0_xattn_Wq"][:, pair_order],
        "x0_wk": a["L0_xattn_Wk"][:, pair_order],
        "x0_wv": a["L0_xattn_Wv"],
        "x0_wo": a["L0_xattn_Wo"],
        "x0_own_head": own_head,
        "a0_wqT": a["L0_attn_Wq"].T,
        "a0_wqT_sw": a["L0_attn_Wq"][swapped].T,
        "a0_wkT": a["L0_attn_Wk"].T,
        "a0_wkT_sw": a["L0_attn_Wk"][swapped].T,
        "a0_wvT": a["L0_attn_Wv"].T,
        "a0_woT": a["L0_attn_Wo"].T,
        "a0_bq": a["L0_attn_bq"][:, None],
        "a0_bq_sw": a["L0_attn_bq"][swapped][:, None],
        "a0_bk": a["L0_attn_bk"][:, None],
        "a0_bk_sw": a["L0_attn_bk"][swapped][:, None],
        "a0_bv": rows(a["L0_attn_bv"]),
        "a0_bo": rows(a["L0_attn_bo"]),
        "a0_cos": cos,
        "a0_sin": sin,
        "a0_causal": causal,
        "a0_heads": heads,
        "lower": rows(lower),
        "f0_wgT": a["L0_ffn_Wg"].T,
        "f0_b1": a["L0_ffn_b1"].reshape(NE * IT, P).T,
        "f0_b2": a["L0_ffn_b2"],
        "big_f0_w1": a["L0_ffn_W1"],
        "big_f0_w2": a["L0_ffn_W2"],
        "ctx": a["ctx_768"],
        "halves": halves,
        "x1_wq": a["L1_xattn_Wq"],
        "x1_wk": a["L1_xattn_Wk"],
        "x1_wv": a["L1_xattn_Wv"],
        "x1_woT": a["L1_xattn_Wo"].T,
        "s1_wxT": a["L1_attn_W_x"].T,
        "s1_wgT": a["L1_attn_W_g"].T,
        "s1_wdtT": a["L1_attn_W_dt"].T,
        "s1_bx": by_half(a["L1_attn_b_x"][:, None]),
        "s1_bg": by_half(a["L1_attn_b_g"][:, None]),
        "s1_bdt": by_half(a["L1_attn_b_dt"][:, None]),
        "s1_cw": by_half(a["L1_attn_conv_w"][:, 0, :]),
        "s1_cb": by_half(a["L1_attn_conv_b"][:, None]),
        "s1_araw": by_half(a["L1_attn_A_raw"]),
        "s1_b": by_half(a["L1_attn_B_ssm"]),
        "s1_c": by_half(a["L1_attn_C_ssm"]),
        "s1_k": rows(_np.arange(S, dtype=_np.float32)),
        "s1_woT": by_half(a["L1_attn_W_out"].T),
        "s1_bout": rows(a["L1_attn_b_out"]),
        "s1_g": rows(a["L1_attn_ln_g"]),
        "s1_lb": rows(a["L1_attn_ln_b"]),
        "f1_wrT": a["L1_ffn_routing_W"].T,
        "f1_eb": rows(a["L1_ffn_expert_bias"]),
        "f1_rw1": a["L1_ffn_rW1"].transpose(1, 0, 2).reshape(D, NE * HE),
        "f1_sw1": a["L1_ffn_sW1"],
        "f1_b1": b1,
        "f1_rw2": a["L1_ffn_rW2"].reshape(NE // 2, 2 * HE, D).transpose(1, 0, 2).reshape(2 * HE, NE // 2 * D),
        "f1_sw2": a["L1_ffn_sW2"],
        "f1_sb2": rows(a["L1_ffn_sb2"]),
        "f1_rb2": a["L1_ffn_rb2"],
    }
    nc = _bacc.Bacc("TRN2", target_bir_lowering=False, num_devices=1)
    arrays, w = {}, {}
    for name, v in laid.items():
        v = _np.ascontiguousarray(v)
        arrays[f"in_{name}"] = v
        w[name] = nc.dram_tensor(f"in_{name}", v.shape, _mybir.dt.from_np(v.dtype), kind="ExternalInput").ap()
    w["mask_bias"] = nc.dram_tensor("mask_bias_rows", (B, M), _mybir.dt.bfloat16, kind="Internal").ap()
    w["out"] = nc.dram_tensor("out_x", (T, D), _mybir.dt.float32, kind="ExternalOutput").ap()
    program(nc, w)
    r = _run(nc, [arrays], core_ids=[0])
    return r.results[0]["out_x"].reshape(B, S, D)
```
